# Optimizing a Trainium2 kernel written in Bass

```python
import numpy as np
import jax
import jax.numpy as jnp

def _softmax(x, axis=-1):
    return jax.nn.softmax(x, axis=axis)

def _gelu(x):
    return jax.nn.gelu(x, approximate=True)

def _silu(x):
    return jax.nn.silu(x)

def _sigmoid(x):
    return jax.nn.sigmoid(x)

def _layernorm(x, axis=-1, eps=1e-05):
    m = jnp.mean(x, axis=axis, keepdims=True)
    v = jnp.var(x, axis=axis, keepdims=True)
    return (x - m) / jnp.sqrt(v + eps)

def _scatter_add(tgt, idx, src, axis=0):
    return tgt.at[idx].add(src)

def _segment_sum(src, seg, n):
    return jax.ops.segment_sum(src, seg, n)
kernel_name = 'mk_seq_preln_d1_jaxref_r4_1cfabf'

def setup_inputs(seed: int=0):
    np.random.seed(seed)
    _w = jnp.asarray

    def _L0_attn_setup():
        import jax, jax.numpy as jnp
        import numpy as np
        import math
        DIM_EMB = 256
        DIM_QK = 256
        DIM_V = 256
        NORM_FACT = 1.0 / math.sqrt(DIM_EMB)
        key = jax.random.key(seed)
        k0, k1, k2, k3 = jax.random.split(key, 4)
        x = jax.random.normal(k0, (4, 1024, DIM_EMB), dtype=jnp.float32)
        s = 1.0 / math.sqrt(DIM_EMB)
        Wq = jax.random.uniform(k1, (DIM_QK, DIM_EMB), jnp.float32, -s, s)
        Wk = jax.random.uniform(k2, (DIM_QK, DIM_EMB), jnp.float32, -s, s)
        Wv = jax.random.uniform(k3, (DIM_V, DIM_EMB), jnp.float32, -s, s)
        return {'x': x, 'Wq': Wq, 'Wk': Wk, 'Wv': Wv}
    _L0_attn_in = _L0_attn_setup()

    def _L0_ffn_setup():
        import jax, jax.numpy as jnp
        import numpy as np
        B, S, D = (2, 512, 256)
        E, K, F = (16, 2, 128)
        FS = 256
        key = jax.random.key(seed)
        ks = jax.random.split(key, 8)

        def w(k, shape, fan_in):
            return jax.random.normal(k, shape, jnp.float32) / np.sqrt(fan_in).astype(np.float32)
        return {'x': jax.random.normal(ks[0], (B, S, D), jnp.float32), 'Wr': w(ks[1], (D, E), D), 'Wg': w(ks[2], (E, D, F), D), 'Wu': w(ks[3], (E, D, F), D), 'Wd': w(ks[4], (E, F, D), F), 'Sg': w(ks[5], (D, FS), D), 'Su': w(ks[6], (D, FS), D), 'Sd': w(ks[7], (FS, D), FS)}
    _L0_ffn_in = _L0_ffn_setup()
    _d = {'L0_attn_x': _L0_attn_in['x'], 'L0_attn_Wq': _L0_attn_in['Wq'], 'L0_attn_Wk': _L0_attn_in['Wk'], 'L0_attn_Wv': _L0_attn_in['Wv'], 'L0_ffn_Wr': _L0_ffn_in['Wr'], 'L0_ffn_Wg': _L0_ffn_in['Wg'], 'L0_ffn_Wu': _L0_ffn_in['Wu'], 'L0_ffn_Wd': _L0_ffn_in['Wd'], 'L0_ffn_Sg': _L0_ffn_in['Sg'], 'L0_ffn_Su': _L0_ffn_in['Su'], 'L0_ffn_Sd': _L0_ffn_in['Sd']}
    _x0 = _d['L0_attn_x']
    _d['L0_attn_x'] = jax.random.normal(jax.random.fold_in(jax.random.key(seed), 1), (8, 512, 256), dtype=_x0.dtype)
    del _x0
    return _d

def reference(L0_attn_x, L0_attn_Wq, L0_attn_Wk, L0_attn_Wv, L0_ffn_Wr, L0_ffn_Wg, L0_ffn_Wu, L0_ffn_Wd, L0_ffn_Sg, L0_ffn_Su, L0_ffn_Sd):

    def _L0_attn_ref(x, Wq, Wk, Wv):
        import jax, jax.numpy as jnp
        import numpy as np
        import math
        DIM_EMB = 256
        DIM_QK = 256
        DIM_V = 256
        NORM_FACT = 1.0 / math.sqrt(DIM_EMB)
        q = jnp.einsum('bne,de->bnd', x, Wq)
        k = jnp.einsum('bne,de->bnd', x, Wk)
        v = jnp.einsum('bne,de->bnd', x, Wv)
        logits = jnp.einsum('bnd,bmd->bnm', q, k)
        score = jax.nn.softmax(logits, axis=-1) * NORM_FACT
        att = jnp.einsum('bnm,bmv->bnv', score, v)
        return att

    def _L0_ffn_ref(x, Wr, Wg, Wu, Wd, Sg, Su, Sd):
        import jax, jax.numpy as jnp
        import numpy as np
        B, S, D = (2, 512, 256)
        E, K, F = (16, 2, 128)
        FS = 256
        b, s, d = x.shape
        T = b * s
        xf = x.reshape(T, d)
        shared = jax.nn.silu(xf @ Sg) * (xf @ Su) @ Sd
        probs = jax.nn.softmax(xf @ Wr, axis=-1)
        topk_p, topk_i = jax.lax.top_k(probs, K)
        n_exp = Wr.shape[1]
        cw = jnp.zeros((T, n_exp), x.dtype).at[jnp.arange(T)[:, None], topk_i].add(topk_p)

        def step(acc, ew):
            wg, wu, wd, c = ew
            y = jax.nn.silu(xf @ wg) * (xf @ wu) @ wd
            return (acc + y * c[:, None], None)
        routed, _ = jax.lax.scan(step, jnp.zeros_like(xf), (Wg, Wu, Wd, cw.T))
        return (routed + shared).reshape(b, s, d)
    x = L0_attn_x
    x = x + _L0_attn_ref(_layernorm(x, axis=-1), L0_attn_Wq, L0_attn_Wk, L0_attn_Wv)
    x = x + _L0_ffn_ref(_layernorm(x, axis=-1), L0_ffn_Wr, L0_ffn_Wg, L0_ffn_Wu, L0_ffn_Wd, L0_ffn_Sg, L0_ffn_Su, L0_ffn_Sd)
    return x

_drawn_inputs = setup_inputs


def setup_inputs(seed=0):
    import zlib

    import numpy as np

    out = dict(_drawn_inputs(seed))
    spreads = {}
    factors = {}
    for name, (base, spread) in spreads.items():
        noise = np.random.default_rng([zlib.crc32(name.encode()), seed]).standard_normal(out[name].shape)
        drawn = base * np.exp(spread * noise) if base else spread * noise
        out[name] = jnp.asarray(drawn.astype(out[name].dtype))
    for name, factor in factors.items():
        out[name] = (out[name] * factor).astype(out[name].dtype)
    return out
```

```python
from contextlib import ExitStack

import concourse.bass as bass
from concourse import mybir
from concourse.alu_op_type import AluOpType as ALU

F32, F32R, BF16 = mybir.dt.float32, mybir.dt.float32r, mybir.dt.bfloat16
I32, U32 = mybir.dt.int32, mybir.dt.uint32
ACT = mybir.ActivationFunctionType
AX = mybir.AxisListType.X
P = 128
EPS = 1e-5


def block_kernel(nc, x_in, wq_in, wk_in, wv_in, wr_in, wg_in, wu_in, wd_in, sg_in, su_in, sd_in, out):
    B, N, D = x_in.shape
    E, _, F = wg_in.shape
    FS = sg_in.shape[1]
    NT = N // P
    DK = D // P
    FK = FS // P
    K = 2
    T = B * N
    REGION = T + P
    TILES = T * K // P + E
    QUADS = TILES // 4
    WROW = 3 * D
    assert (NT, DK, FK, F, E) == (4, 2, 2, P, 16) and TILES % 8 == 0 and B % 4 == 0 and TILES <= P

    x_v = x_in.rearrange("b (p j) d -> b p (j d)", p=P)
    out_v = out.rearrange("b (p j) d -> b p (j d)", p=P)
    x1_dram = nc.dram_tensor("x1_dram", [B, P, NT * D], F32, kind="Internal").ap()
    xn2_dram = nc.dram_tensor("xn2_dram", [B, P, NT * D], F32, kind="Internal").ap()
    rows_by_expert = nc.dram_tensor("rows_by_expert", [E * REGION, D], F32, kind="Internal").ap()
    outs_by_tile = nc.dram_tensor("outs_by_tile", [TILES * P, D], F32, kind="Internal").ap()

    with ExitStack() as ctx:
        def sb(name, shape, dt=F32):
            return ctx.enter_context(nc.sbuf_tensor(name, shape, dt))

        def sem(name):
            return ctx.enter_context(nc.semaphore(name))

        ATTN_BYTES = 100 * 1024
        LATE_BYTES = 48 * 1024
        attn_start = -(-nc.sbuf_base // 32) * 32
        attn_area = sb("attn_area", [P, ATTN_BYTES // 4])
        late_start = -(-nc.sbuf_base // 32) * 32
        late_area = sb("late_area", [P, LATE_BYTES // 4])
        places = {}

        def place(area, key, name, shape, dt=F32):
            size = 4
            for n in shape[1:]:
                size *= n
            at = places.get(key, 0)
            places[key] = at + size
            assert at + size <= (ATTN_BYTES if area is attn_area else LATE_BYTES), name
            return nc.alloc_sbuf_tensor_at(name, shape, dt, offset=(attn_start if area is attn_area else late_start) + at)

        x = place(attn_area, "A", "x", [P, B, NT, D])
        xn = place(attn_area, "A", "xn", [P, NT, D])
        xT_hi = place(attn_area, "A", "xT_hi", [P, DK, N], F32R)
        xT_lo = place(attn_area, "A", "xT_lo", [P, DK, N], F32R)
        q_hi = place(attn_area, "A", "q_hi", [P, DK, N], F32R)
        q_lo = place(attn_area, "A", "q_lo", [P, DK, N], F32R)
        v_hi = place(attn_area, "A", "v_hi", [P, NT, D], F32R)
        v_lo = place(attn_area, "A", "v_lo", [P, NT, D], F32R)
        wqk_hi = place(attn_area, "A", "wqk_hi", [P, DK, D], F32R)
        wqk_lo = place(attn_area, "A", "wqk_lo", [P, DK, D], F32R)
        wvT_hi = place(attn_area, "A", "wvT_hi", [P, DK, D], F32R)
        wvT_lo = place(attn_area, "A", "wvT_lo", [P, DK, D], F32R)
        x2T_hi = place(attn_area, "A", "x2T_hi", [P, DK, N], F32R)
        x2T_lo = place(attn_area, "A", "x2T_lo", [P, DK, N], F32R)
        places["setup"] = places["A"]
        prob = place(attn_area, "A", "prob", [P, NT, N])
        pT_hi = place(attn_area, "A", "pT_hi", [P, NT, N], F32R)
        pT_lo = place(attn_area, "A", "pT_lo", [P, NT, N], F32R)
        wq = place(attn_area, "setup", "wq", [P, DK, D])
        wk = place(attn_area, "setup", "wk", [P, DK, D])
        wv = place(attn_area, "setup", "wv", [P, DK, D])
        wq_hi = place(attn_area, "setup", "wq_hi", [P, DK, D], F32R)
        wq_lo = place(attn_area, "setup", "wq_lo", [P, DK, D], F32R)
        wk_hi = place(attn_area, "setup", "wk_hi", [P, DK, D], F32R)
        wk_lo = place(attn_area, "setup", "wk_lo", [P, DK, D], F32R)
        sgu = place(attn_area, "setup", "sgu", [P, DK, 2 * FS])
        sd = place(attn_area, "setup", "sd", [P, FK, D])
        we_hi = place(attn_area, "C", "we_hi", [P, E * WROW], F32R)
        we_raw = place(late_area, "raw", "we_raw", [P, E * WROW])
        we_lo = place(late_area, "lo", "we_lo", [P, E * WROW], F32R)
        cx = [place(attn_area, "C", f"cx{i}", [P, 4, D]) for i in range(2)]
        cxT_hi = place(attn_area, "C", "cxT_hi", [P, 4 * DK, P], F32R)
        cxT_lo = place(attn_area, "C", "cxT_lo", [P, 4 * DK, P], F32R)
        csilu = place(attn_area, "C", "csilu", [P, 4, F])
        ch = place(attn_area, "C", "ch", [P, 4, F])
        chT_hi = place(attn_area, "C", "chT_hi", [P, 4, P], F32R)
        chT_lo = place(attn_area, "C", "chT_lo", [P, 4, P], F32R)
        cy = [place(attn_area, "C", f"cy{i}", [P, 4, D]) for i in range(2)]
        got = place(attn_area, "D", "got", [P, 4, K * NT, D])
        res = place(late_area, "D late", "res", [P, B, NT, D])
        dxT_hi = place(attn_area, "C", "dxT_hi", [P, DK, N], F32R)
        dxT_lo = place(attn_area, "C", "dxT_lo", [P, DK, N], F32R)
        dh = place(attn_area, "C", "dh", [P, FK, N])
        dh_hi = place(attn_area, "C", "dh_hi", [P, FK, N], F32R)
        dh_lo = place(attn_area, "C", "dh_lo", [P, FK, N], F32R)

        xn2 = [sb(f"xn2_{i}", [P, NT, D]) for i in range(2)]
        sgu_hi, sgu_lo = sb("sgu_hi", [P, DK, 2 * FS], F32R), sb("sgu_lo", [P, DK, 2 * FS], F32R)
        sd_hi, sd_lo = sb("sd_hi", [P, FK, D], F32R), sb("sd_lo", [P, FK, D], F32R)
        wr = sb("wr", [P, DK, E])
        wr_hi, wr_lo = sb("wr_hi", [P, DK, E], F32R), sb("wr_lo", [P, DK, E], F32R)
        ident = sb("ident", [P, P])
        before = sb("before", [P, P], BF16)
        ones = sb("ones", [P, P], BF16)
        expert_no = sb("expert_no", [P, E])
        region_start = sb("region_start", [P, E])
        tile_no = sb("tile_no", [P, 1])
        ones_e = sb("ones_e", [P, E])
        minus_half = sb("minus_half", [P, NT])
        zeros = sb("zeros", [P, D])
        stat = [sb(f"stat{k}", [P, NT, 6]) for k in range(2)]
        mean_var = [sb(f"mean_var{k}", [P, NT, 2]) for k in range(2)]
        var_eps = [sb(f"var_eps{k}", [P, NT]) for k in range(2)]
        neg_mean = [sb(f"neg_mean{k}", [P, NT]) for k in range(2)]
        rstd = [sb(f"rstd{k}", [P, NT]) for k in range(2)]
        shift = [sb(f"shift{k}", [P, NT]) for k in range(2)]
        neg_max = sb("neg_max", [P, NT])
        prob_sum = sb("prob_sum", [P, NT])
        prob_sum16 = sb("prob_sum16", [P, NT])
        prob_scale = sb("prob_scale", [P, NT])
        logit = sb("logit", [P, NT, E])
        top = sb("top", [P, NT, 8])
        top_no = sb("top_no", [P, NT, 8], U32)
        choice = sb("choice", [P, K, NT])
        onehot = sb("onehot", [P, K, NT * E])
        chosen = sb("chosen", [P, NT * E], BF16)
        over = sb("over", [P, NT * E + NT])
        over_exp = sb("over_exp", [P, NT * E + NT])
        gate_sum = sb("gate_sum", [P, NT])
        gate0 = sb("gate0", [P, NT])
        gates = sb("gates", [P, B, K, NT])
        next_row = sb("next_row", [P, E])
        row_of = sb("row_of", [P, NT * E])
        row_pick = sb("row_pick", [P, K, NT * E])
        slot = [sb(f"slot{i}", [P, K * NT], U32) for i in range(2)]
        region_rows = sb("region_rows", [P, B * K * NT])
        slots = sb("slots", [P, B, K * NT], U32)
        slot_d = [sb(f"slot_d{i}", [P, K * NT], U32) for i in range(4)]
        count = sb("count", [P, E])
        count_i = sb("count_i", [P, E], I32)
        tiles_i = sb("tiles_i", [P, E], I32)
        tiles_of = sb("tiles_of", [P, E])
        tile_end = sb("tile_end", [P, E])
        passed = sb("passed", [P, E])
        passed_tiles = sb("passed_tiles", [P, E])
        tcol = sb("tcol", [P, 12])
        tile_vals = sb("tile_vals", [P, 2])
        tile_map = sb("tile_map", [1, 2, TILES], I32)
        shift_of = sb("shift_of", [P, E])
        shift_step = sb("shift_step", [P, E])
        at_least = sb("at_least", [P, B * K * NT, E])
        row_shift = sb("row_shift", [P, B * K * NT])
        row_end = sb("row_end", [1, E], I32)

        bank = [ctx.enter_context(nc.psum_tensor(f"bank{i}", [P, 512], F32)) for i in range(8)]

        names = """x0_in x1_in x_in w_in wv_in wr_in s_in raw_in
            consts pool_step
            wqk_raw_hi wqk_raw_lo wqk_done wvT_done wqk_h wqk_l wr_h wr_l s_h s_l
            bn0 bn1 mv0 mv1 pm0 pm1 ln0 ln1 xn_ready xn2_ready t1 t2 xh xl x2h x2l
            q_done qh ql v_done vh vl s_done mx e_done pt ptH ptL ps16 pscale o_done x1_done
            x1_out xn2_out0 xn2_out1
            logits_done logit_read rt_top rt_pick rt_no rt_hot rt_mask rt_over rt_exp rt_sum rt_gate0 rt_gates
            rank_done rank_read rt_row rt_rowpick rt_slot rt_next slot_store row_end
            scattered0 scattered1 zero_fill
            map_step map_vals map_done map_ready slots_ready
            we_h we_l
            cx_in0 cx_in1 ct cxh cxl cgu cs chm cth chh chl cdn cyr c_out0 c_out1 got_used
            dx_in0 dx_in1 dt dxh dxl dgu dsi dhm dhh dhl ddn slot_cp got_in0 got_in1
            dsum got_in2 got_in3 res_in out_done dstep""".split()
        S = {n: sem(n) for n in names}

        def copies(k):
            return S[f"bn{k}"], S[f"mv{k}"], S[f"pm{k}"], S[f"ln{k}"]

        block = ctx.enter_context(nc.Block())

        def batches(eng, step):
            step(0, 0, first=True)
            with eng.Fori(0, (B - 2) // 2) as u:
                step(2 * u + 1, 1)
                step(2 * u + 2, 0)
            step(B - 1, 1, last=True)

        def quads(eng, step):
            step(0, 0, first=True)
            with eng.Fori(0, (QUADS - 2) // 2) as u:
                step(2 * u + 1, 1)
                step(2 * u + 2, 0)
            step(QUADS - 1, 1, last=True)

        def of_tiles(engine, row, q):
            return nc.values_load_multi_w_load_instructions(
                tile_map[0:1, row, bass.ds(4 * q, 4)], engines=[engine], min_val=0,
                max_val=E * REGION - P if row == 0 else (E - 1) * WROW,
                skip_runtime_bounds_check_because="made from counts that are bounded")[1]

        def zero_tails(eng, engine, half):
            eng.wait_ge(S["row_end"], 1)
            with eng.Fori(0, E // 8) as u:
                ends = nc.values_load_multi_w_load_instructions(
                    row_end[0:1, bass.ds(u * 4 + half * (E // 2), 4)], engines=[engine], min_val=0,
                    max_val=E * REGION - P, skip_runtime_bounds_check_because="a count that is bounded")[1]
                for end in ends:
                    eng.dma_start(rows_by_expert[bass.ds(end, P), :], zeros[:, :]).then_inc(S["zero_fill"], 16)

        @block.sync
        def _(sp):
            sp.dma_start(x[:, 0, :, :].rearrange("p j d -> p (j d)"), x_v[0]).then_inc(S["x0_in"], 16)
            sp.dma_start(wq[:, :, :], wq_in.rearrange("(k p) e -> p k e", p=P)).then_inc(S["w_in"], 16)
            sp.dma_start(wk[:, :, :], wk_in.rearrange("(k p) e -> p k e", p=P)).then_inc(S["w_in"], 16)
            sp.dma_start(wv[:, :, :], wv_in.rearrange("(k p) e -> p k e", p=P)).then_inc(S["wv_in"], 16)
            sp.dma_start(wr[:, :, :], wr_in.rearrange("(k p) e -> p k e", p=P)).then_inc(S["wr_in"], 16)
            sp.dma_start(x[:, 1, :, :].rearrange("p j d -> p (j d)"), x_v[1]).then_inc(S["x1_in"], 16)
            sp.dma_start(sgu[:, :, 0:FS], sg_in.rearrange("(k p) f -> p k f", p=P)).then_inc(S["s_in"], 16)
            sp.dma_start(sgu[:, :, FS:2 * FS], su_in.rearrange("(k p) f -> p k f", p=P)).then_inc(S["s_in"], 16)
            sp.dma_start(sd[:, :, :], sd_in.rearrange("(k p) e -> p k e", p=P)).then_inc(S["s_in"], 16)
            for b in range(2, B):
                sp.dma_start(x[:, b, :, :].rearrange("p j d -> p (j d)"), x_v[b]).then_inc(S["x_in"], 16)
            for e in range(E):
                w = we_raw[:, e * WROW:e * WROW + 2 * D].rearrange("p (k c f) -> p k c f", k=DK, c=2)
                sp.dma_start(w[:, :, 0, :], wg_in[e].rearrange("(k p) f -> p k f", p=P)).then_inc(S["raw_in"], 16)
                sp.dma_start(w[:, :, 1, :], wu_in[e].rearrange("(k p) f -> p k f", p=P)).then_inc(S["raw_in"], 16)
                sp.dma_start(we_raw[:, e * WROW + 2 * D:(e + 1) * WROW], wd_in[e]).then_inc(S["raw_in"], 16)

            def store_batch(i, par):
                sp.wait_ge(S["x1_done"], i + 1)
                sp.dma_start(x1_dram[bass.ds(i, 1), :, :].rearrange("b p n -> (b p) n"),
                             x[:, bass.ds(i, 1), :, :].rearrange("p b j d -> p (b j d)")).then_inc(S["x1_out"], 16)
                sp.wait_ge(S["xn2_ready"], i + 1)
                sp.dma_start(xn2_dram[bass.ds(i, 1), :, :].rearrange("b p n -> (b p) n"),
                             xn2[par][:, :, :].rearrange("p j d -> p (j d)")).then_inc(S[f"xn2_out{par}"], 16)

            store_batch(0, 0)
            with sp.Fori(0, (B - 2) // 2) as u:
                store_batch(2 * u + 1, 1)
                store_batch(2 * u + 2, 0)
            store_batch(B - 1, 1)

            zero_tails(sp, mybir.EngineType.SP, 0)

            sp.wait_ge(S["scattered0"], 16 * K * NT * B // 2)
            sp.wait_ge(S["scattered1"], 16 * K * NT * B // 2)
            sp.wait_ge(S["zero_fill"], 16 * E)
            sp.wait_ge(S["map_ready"], 1)
            sp.wait_ge(S["we_h"], 1)

            def load_quad(q, par):
                if not isinstance(q, int) or q >= 2:
                    sp.wait_ge(S["ct"], 2 * q - 2)
                rows = of_tiles(mybir.EngineType.SP, 0, q)
                for s in range(4):
                    sp.dma_start(cx[par][:, s, :], rows_by_expert[bass.ds(rows[s], P), :]).then_inc(S[f"cx_in{par}"], 16)

            def store_quad(q, par):
                sp.wait_ge(S["cyr"], 2 * q + 2)
                sp.dma_start(outs_by_tile[bass.ds(q * (4 * P), 4 * P), :].rearrange("(s p) d -> p s d", p=P),
                             cy[par][:, :, :]).then_inc(S[f"c_out{par}"], 16)

            def load_rows(b, par):
                if not isinstance(b, int) or b >= 2:
                    sp.wait_ge(S["dt"], 2 * b - 2)
                sp.dma_start(xn2[par][:, :, :].rearrange("p j d -> p (j d)"),
                             xn2_dram[bass.ds(b, 1), :, :].rearrange("b p n -> (b p) n")).then_inc(S[f"dx_in{par}"], 16)

            def load_residual(b):
                sp.dma_start(res[:, bass.ds(b, 1), :, :].rearrange("p b j d -> p (b j d)"),
                             x1_dram[bass.ds(b, 1), :, :].rearrange("b p n -> (b p) n")).then_inc(S["res_in"], 16)

            def store_final(b):
                sp.wait_ge(S["got_used"], b + 1)
                sp.dma_start(out_v[bass.ds(b, 1), :, :].rearrange("b p n -> (b p) n"),
                             res[:, bass.ds(b, 1), :, :].rearrange("p b j d -> p (b j d)")).then_inc(S["out_done"], 16)

            sp.wait_ge(S["x1_out"], 16 * B)
            sp.wait_ge(S["xn2_out0"], 8 * B)
            sp.wait_ge(S["xn2_out1"], 8 * B)

            def step(q, par, first=False, last=False):
                if not (isinstance(q, int) and q + 2 >= QUADS):
                    load_quad(q + 2, par)
                if not first:
                    store_quad(q - 1, 1 - par)

            load_quad(0, 0)
            load_quad(1, 1)
            load_rows(0, 0)
            load_rows(1, 1)
            step(0, 0, first=True)
            with sp.Fori(0, (QUADS - 4) // 2) as u:
                step(2 * u + 1, 1)
                step(2 * u + 2, 0)
            for q in range(QUADS - 3, QUADS + 1):
                step(q, q % 2)

            sp.wait_ge(S["cdn"], 2 * QUADS)
            with sp.Fori(0, B) as b:
                load_residual(b)
            with sp.Fori(0, (B - 2) // 2) as u:
                for par in range(2):
                    load_rows(2 * u + (2 + par), par)
            with sp.Fori(0, B) as b:
                store_final(b)
            sp.wait_ge(S["out_done"], 16 * B)

        @block.gpsimd
        def _(pool):
            g = nc.gpsimd

            def hold(name, n):
                pool.wait_ge(S[name], n)
                pool.nop(nofuse=True)

            g.memset(ident[:, :], 0.0).then_inc(S["pool_step"], 1)
            g.memset(before[:, :], 1.0).then_inc(S["pool_step"], 1)
            g.memset(ones[:, :], 1.0).then_inc(S["pool_step"], 1)
            g.memset(ones_e[:, :], 1.0).then_inc(S["pool_step"], 1)
            g.memset(minus_half[:, :], -0.5).then_inc(S["pool_step"], 1)
            g.memset(zeros[:, :], 0.0).then_inc(S["pool_step"], 1)
            g.iota(expert_no[:, :], [[1, E]], base=0, channel_multiplier=0,
                   allow_small_or_imprecise_dtypes=True).then_inc(S["pool_step"], 1)
            g.iota(region_start[:, :], [[REGION, E]], base=0, channel_multiplier=0,
                   allow_small_or_imprecise_dtypes=True).then_inc(S["pool_step"], 1)
            g.iota(next_row[:, :], [[REGION, E]], base=0, channel_multiplier=0,
                   allow_small_or_imprecise_dtypes=True).then_inc(S["pool_step"], 1)
            g.iota(tile_no[:, :], [[0, 1]], base=0, channel_multiplier=1,
                   allow_small_or_imprecise_dtypes=True).then_inc(S["pool_step"], 1)
            pool.wait_ge(S["pool_step"], 10)
            g.affine_select(out=ident[:, :], in_=ident[:, :], compare_op=ALU.not_equal, fill=1.0, base=0,
                            pattern=[[-1, P]], channel_multiplier=1).then_inc(S["consts"], 1)
            g.affine_select(out=before[:, :], in_=before[:, :], compare_op=ALU.is_gt, fill=0.0, base=0,
                            pattern=[[1, P]], channel_multiplier=-1).then_inc(S["consts"], 1)

            def scale_shift(i, k):
                mv, pm, ln = S[f"mv{k}"], f"pm{k}", S[f"ln{k}"]
                hold(f"mv{k}", i + 1)
                g.tensor_scalar(var_eps[k][:, :], mean_var[k][:, :, 1], EPS, None, ALU.add).then_inc(S[pm], 1)
                g.tensor_scalar(neg_mean[k][:, :], mean_var[k][:, :, 0], -1.0, None, ALU.mult).then_inc(S[pm], 1)
                if not isinstance(i, int) or i >= 1:
                    pool.wait_ge(S["xn_ready" if k == 0 else "xn2_ready"], i)
                hold(pm, 3 * i + 2)
                g.tensor_tensor(rstd[k][:, :], var_eps[k][:, :], minus_half[:, :], ALU.pow).then_inc(S[pm], 1)
                hold(pm, 3 * i + 3)
                g.tensor_tensor(shift[k][:, :], neg_mean[k][:, :], rstd[k][:, :], ALU.mult).then_inc(ln, 1)

            def scatter(i, par):
                hold("rt_slot", i + 1)
                for c in range(K * NT):
                    g.indirect_dma_start(rows_by_expert, bass.IndirectOffsetOnAxis(ap=slot[par][:, c:c + 1], axis=0),
                                         xn2[par][:, c % NT, :], None).then_inc(S[f"scattered{par}"], 16)

            def step(i, par, first=False, last=False):
                if isinstance(i, int) and i + 2 >= B:
                    pass
                else:
                    scale_shift(i + 2, 0)
                scale_shift(i, 1)
                if not first:
                    scatter(i - 1, 1 - par)

            scale_shift(0, 0)
            scale_shift(1, 0)
            step(0, 0, first=True)
            with pool.Fori(0, (B - 4) // 2) as u:
                step(2 * u + 1, 1)
                step(2 * u + 2, 0)
            step(B - 3, 1)
            step(B - 2, 0)
            step(B - 1, 1, last=True)
            scatter(B - 1, 1)

            def gather(b, buf):
                if not isinstance(b, int) or b >= 4:
                    hold("got_used", b - 3)
                g.tensor_copy(slot_d[buf][:, :], slots[:, bass.ds(b, 1), :].rearrange("p b c -> p (b c)"))\
                    .then_inc(S["slot_cp"], 1)
                hold("slot_cp", b + 1)
                for c in range(K * NT):
                    g.indirect_dma_start(got[:, buf, c, :], None, outs_by_tile,
                                         bass.IndirectOffsetOnAxis(ap=slot_d[buf][:, c:c + 1], axis=0))\
                        .then_inc(S[f"got_in{buf}"], 16)

            pool.wait_ge(S["slots_ready"], 1)
            pool.wait_ge(S["c_out0"], 8 * QUADS)
            pool.wait_ge(S["c_out1"], 8 * QUADS)
            for b in range(4):
                gather(b, b)
            with pool.Fori(0, (B - 4) // 4) as u:
                for b in range(4):
                    gather(4 * u + (4 + b), b)

        @block.scalar
        def _(act):
            a = nc.scalar

            def hi(dst, src, done):
                return a.activation(dst, src, ACT.Copy).then_inc(S[done], 1)

            def normalise(i, k, par=0):
                act.wait_ge(S[f"ln{k}"], i + 1)
                if k == 0:
                    dst, done = xn, "xn_ready"
                    if not isinstance(i, int) or i >= 1:
                        act.wait_ge(S["t1"], DK * i)
                else:
                    dst, done = xn2[par], "xn2_ready"
                    if not isinstance(i, int) or i >= 2:
                        act.wait_ge(S[f"xn2_out{par}"], (i - par) * 8)
                        act.wait_ge(S[f"scattered{par}"], (i - par) * (8 * K * NT))
                for j in range(NT):
                    src = x[:, bass.ds(i, 1), j, :].rearrange("p b d -> p (b d)")
                    last = a.activation(dst[:, j, :], src, ACT.Identity, bias=shift[k][:, j:j + 1],
                                        scale=rstd[k][:, j:j + 1])
                last.then_inc(S[done], 1)

            def xT(i):
                for k in range(DK):
                    act.wait_ge(S["t1"], DK * i + k + 1)
                    hi(xT_hi[:, k, :], bank[k][:, :], "xh")

            def x2T(i):
                for k in range(DK):
                    act.wait_ge(S["t2"], DK * i + k + 1)
                    hi(x2T_hi[:, k, :], bank[4 + k][:, :], "x2h")

            def q(i):
                for m in range(DK):
                    act.wait_ge(S["q_done"], DK * i + m + 1)
                    hi(q_hi[:, m, :], bank[4 + m][:, :], "qh")

            def v(i):
                for m in range(2):
                    act.wait_ge(S["v_done"], 2 * i + m + 1)
                    hi(v_hi[:, 2 * m:2 * m + 2, :].rearrange("p j d -> p (j d)"), bank[2 + m][:, :], "vh")

            def exps(i, rows):
                for n in rows:
                    act.wait_ge(S["mx"], NT * i + n + 1)
                    a.activation(prob[:, n, :], bank[n][:, :], ACT.Exp, bias=neg_max[:, n:n + 1],
                                 accum_out=prob_sum[:, n:n + 1]).then_inc(S["e_done"], 1)

            def pT(i):
                for m in range(NT):
                    act.wait_ge(S["pt"], NT * i + m + 1)
                    hi(pT_hi[:, m, :], bank[(2 + m) % NT][:, :], "ptH")

            def gate_exp(i):
                act.wait_ge(S["rt_over"], 2 * i + 2)
                a.activation(over_exp[:, :], over[:, :], ACT.Exp).then_inc(S["rt_exp"], 1)

            act.wait_ge(S["w_in"], 32)
            hi(wq_hi[:, :, :], wq[:, :, :], "wqk_raw_hi")
            hi(wk_hi[:, :, :], wk[:, :, :], "wqk_raw_hi")
            act.wait_ge(S["wr_in"], 16)
            hi(wr_hi[:, :, :], wr[:, :, :], "wr_h")
            normalise(0, 0)
            act.wait_ge(S["wqk_done"], 1)
            hi(wqk_hi[:, :, :].rearrange("p k d -> p (k d)"), bank[4][:, :], "wqk_h")
            act.wait_ge(S["wvT_done"], 1)
            hi(wvT_hi[:, :, :].rearrange("p k d -> p (k d)"), bank[5][:, :], "wqk_h")
            xT(0)
            normalise(1, 0)
            act.wait_ge(S["s_in"], 48)
            hi(sgu_hi[:, :, :], sgu[:, :, :], "s_h")
            hi(sd_hi[:, :, :], sd[:, :, :], "s_h")
            q(0)
            v(0)

            def step(i, par, first=False, last=False):
                exps(i, range(0, 3))
                if not first:
                    x2T(i - 1)
                exps(i, range(3, 4))
                if not last:
                    xT(i + 1)
                pT(i)
                if not first:
                    gate_exp(i - 1)
                if not last:
                    q(i + 1)
                    v(i + 1)
                normalise(i, 1, par)
                if not (isinstance(i, int) and i + 2 >= B):
                    normalise(i + 2, 0)

            step(0, 0, first=True)
            with act.Fori(0, (B - 4) // 2) as u:
                step(2 * u + 1, 1)
                step(2 * u + 2, 0)
            step(B - 3, 1)
            step(B - 2, 0)
            step(B - 1, 1, last=True)
            x2T(B - 1)
            gate_exp(B - 1)

            act.wait_ge(S["raw_in"], 16 * 3 * E)
            act.wait_ge(S["logits_done"], B)
            act.wait_ge(S["x2l"], DK * B)
            act.wait_ge(S["x1_out"], 16 * B)
            def weights_hi(c):
                cols = slice(4 * c * WROW, 4 * (c + 1) * WROW)
                hi(we_hi[:, cols], we_raw[:, cols], "we_h")

            weights_hi(0)
            weights_hi(1)
            zero_tails(act, mybir.EngineType.Activation, 1)
            weights_hi(2)
            weights_hi(3)

            def c_x(q):
                for h in range(2):
                    act.wait_ge(S["ct"], 2 * q + h + 1)
                    hi(cxT_hi[:, 4 * h:4 * h + 4, :].rearrange("p k t -> p (k t)"), bank[h][:, :], "cxh")

            def c_silu(q):
                for h in range(2):
                    act.wait_ge(S["cgu"], 2 * q + h + 1)
                    a.activation(csilu[:, 2 * h:2 * h + 2, :],
                                 bank[2 + h][:, :].rearrange("p (s c f) -> p s c f", s=2, c=2)[:, :, 0, :],
                                 ACT.Silu).then_inc(S["cs"], 1)

            def c_h(q):
                act.wait_ge(S["cth"], q + 1)
                hi(chT_hi[:, :, :].rearrange("p s t -> p (s t)"), bank[4][:, :], "chh")

            def c_y(q, par):
                if not isinstance(q, int) or q >= 2:
                    act.wait_ge(S[f"c_out{par}"], 8 * (q - par))
                for h in range(2):
                    act.wait_ge(S["cdn"], 2 * q + h + 1)
                    a.activation(cy[par][:, 2 * h:2 * h + 2, :].rearrange("p s d -> p (s d)"), bank[6 + h][:, :],
                                 ACT.Copy).then_inc(S["cyr"], 1)

            def c_step(q, par, first=False, last=False):
                c_silu(q)
                if not last:
                    c_x(q + 1)
                if not first:
                    c_y(q - 1, 1 - par)
                c_h(q)

            c_x(0)
            quads(act, c_step)
            c_y(QUADS - 1, 1)

            def d_x(b):
                for k in range(DK):
                    act.wait_ge(S["dt"], DK * b + k + 1)
                    hi(dxT_hi[:, k, :], bank[k][:, :], "dxh")

            def d_silu(b):
                for f in range(FK):
                    act.wait_ge(S["dgu"], FK * b + f + 1)
                    if not isinstance(b, int) or b >= 1:
                        act.wait_ge(S["dhl"], FK * b)
                    a.activation(dh[:, f, :], bank[2 + 2 * f][:, :], ACT.Silu).then_inc(S["dsi"], 1)

            def d_h(b):
                if not isinstance(b, int) or b >= 1:
                    act.wait_ge(S["ddn"], 2 * b)
                for f in range(FK):
                    act.wait_ge(S["dhm"], FK * b + f + 1)
                    hi(dh_hi[:, f, :], dh[:, f, :], "dhh")

            def d_step(b, par, first=False, last=False):
                if not last:
                    d_silu(b)
                    if not (isinstance(b, int) and b + 1 >= B):
                        d_x(b + 1)
                    d_h(b)

            d_x(0)
            d_step(0, 0, first=True)
            with act.Fori(0, (B - 2) // 2) as u:
                d_step(2 * u + 1, 1)
                d_step(2 * u + 2, 0)
            d_step(B - 1, 1)

        @block.vector
        def _(dve):
            v_ = nc.vector

            def hold(name, n):
                dve.wait_ge(S[name], n)
                dve.nop(nofuse=True)

            def lo(dst, src, hi_half, done):
                return v_.tensor_tensor(dst, src, hi_half.bitcast(F32), ALU.subtract).then_inc(S[done], 1)

            def stats(i, k):
                if k == 0:
                    if isinstance(i, int) and i < 2:
                        dve.wait_ge(S[f"x{i}_in"], 16)
                    else:
                        dve.wait_ge(S["x_in"], 16 * (B - 2))
                else:
                    dve.wait_ge(S["x1_done"], i + 1)
                if not isinstance(i, int) or i >= 1:
                    dve.wait_ge(S[f"pm{k}"], 3 * i)
                    hold(f"ln{k}", i)
                for j in range(NT):
                    last = v_.bn_stats(stat[k][:, j, :], x[:, bass.ds(i, 1), j, :].rearrange("p b d -> p (b d)"))
                last.then_inc(S[f"bn{k}"], 1)
                hold(f"bn{k}", i + 1)
                for j in range(NT):
                    last = v_.bn_aggr(mean_var[k][:, j, :], stat[k][:, j, :])
                last.then_inc(S[f"mv{k}"], 1)

            def maxes(i, rows):
                for n in rows:
                    dve.wait_ge(S["s_done"], NT * i + n + 1)
                    v_.tensor_reduce(neg_max[:, n:n + 1], bank[n][:, :], AX, ALU.max, negate=True)\
                        .then_inc(S["mx"], 1)

            def xT(i):
                for k in range(DK):
                    dve.wait_ge(S["xh"], DK * i + k + 1)
                    lo(xT_lo[:, k, :], bank[k][:, :], xT_hi[:, k, :], "xl")

            def x2T(i):
                for k in range(DK):
                    dve.wait_ge(S["x2h"], DK * i + k + 1)
                    lo(x2T_lo[:, k, :], bank[4 + k][:, :], x2T_hi[:, k, :], "x2l")

            def q(i):
                for m in range(DK):
                    dve.wait_ge(S["qh"], DK * i + m + 1)
                    lo(q_lo[:, m, :], bank[4 + m][:, :], q_hi[:, m, :], "ql")

            def v(i):
                for m in range(2):
                    dve.wait_ge(S["vh"], 2 * i + m + 1)
                    lo(v_lo[:, 2 * m:2 * m + 2, :].rearrange("p j d -> p (j d)"), bank[2 + m][:, :],
                       v_hi[:, 2 * m:2 * m + 2, :].rearrange("p j d -> p (j d)"), "vl")

            def pT(i):
                for m in range(NT):
                    dve.wait_ge(S["ptH"], NT * i + m + 1)
                    lo(pT_lo[:, m, :], bank[(2 + m) % NT][:, :], pT_hi[:, m, :], "ptL")

            def residual(i):
                dve.wait_ge(S["e_done"], NT * (i + 1))
                v_.tensor_scalar(prob_sum16[:, :], prob_sum[:, :], float(D) ** 0.5, None, ALU.mult)\
                    .then_inc(S["ps16"], 1)
                dve.wait_ge(S["ps16"], i + 1)
                v_.reciprocal(prob_scale[:, :], prob_sum16[:, :]).then_inc(S["pscale"], 1)
                dve.wait_ge(S["pscale"], i + 1)
                for n in range(NT):
                    if n % 2 == 0:
                        dve.wait_ge(S["o_done"], 2 * i + n // 2 + 1)
                    row = x[:, bass.ds(i, 1), n, :].rearrange("p b d -> p (b d)")
                    last = v_.scalar_tensor_tensor(row, bank[6 + n // 2][:, n % 2 * D:(n % 2 + 1) * D],
                                                   prob_scale[:, n:n + 1], row, ALU.mult, ALU.add)
                last.then_inc(S["x1_done"], 1)

            per_e = lambda t: t.rearrange("p (j e) -> p j e", e=E)
            wide = lambda col: col.unsqueeze(2).to_broadcast([P, NT, E])

            def route_a(i):
                dve.wait_ge(S["logits_done"], i + 1)
                v_.tensor_copy(logit[:, :, :].rearrange("p j e -> p (j e)"), bank[4][:, 0:NT * E])\
                    .then_inc(S["logit_read"], 1)
                hold("logit_read", i + 1)
                for j in range(NT):
                    last = v_.max(top[:, j, :], logit[:, j, :])
                last.then_inc(S["rt_top"], 1)
                hold("rt_top", i + 1)
                for j in range(NT):
                    last = v_.max_index(top_no[:, j, :], top[:, j, :], logit[:, j, :])
                last.then_inc(S["rt_pick"], 1)
                v_.tensor_tensor(per_e(over[:, 0:NT * E]), logit[:, :, :], wide(top[:, :, 0]), ALU.subtract)\
                    .then_inc(S["rt_over"], 1)
                v_.tensor_tensor(over[:, NT * E:NT * E + NT], top[:, :, 1], top[:, :, 0], ALU.subtract)\
                    .then_inc(S["rt_over"], 1)
                dve.wait_ge(S["rt_pick"], i + 1)
                v_.tensor_copy(choice[:, :, :], top_no[:, :, 0:K].rearrange("p j k -> p k j")).then_inc(S["rt_no"], 1)
                dve.wait_ge(S["rt_no"], i + 1)
                for k in range(K):
                    v_.tensor_tensor(per_e(onehot[:, k, :]), expert_no[:, :].unsqueeze(1).to_broadcast([P, NT, E]),
                                     wide(choice[:, k, :]), ALU.is_equal).then_inc(S["rt_hot"], 1)
                dve.wait_ge(S["rt_hot"], 2 * i + 2)
                v_.tensor_tensor(chosen[:, :], onehot[:, 0, :], onehot[:, 1, :], ALU.add).then_inc(S["rt_mask"], 1)

            def route_b(i, par):
                dve.wait_ge(S["rt_exp"], i + 1)
                v_.tensor_reduce(gate_sum[:, :], per_e(over_exp[:, 0:NT * E]), AX, ALU.add).then_inc(S["rt_sum"], 1)
                dve.wait_ge(S["rank_done"], i + 1)
                v_.tensor_tensor(per_e(row_of[:, :]), per_e(bank[7][:, 0:NT * E]),
                                 next_row[:, :].unsqueeze(1).to_broadcast([P, NT, E]), ALU.add).then_inc(S["rt_row"], 1)
                dve.wait_ge(S["rt_sum"], i + 1)
                v_.reciprocal(gate0[:, :], gate_sum[:, :]).then_inc(S["rt_gate0"], 1)
                dve.wait_ge(S["rt_row"], i + 1)
                v_.tensor_tensor(next_row[:, :], next_row[:, :], bank[7][:, NT * E:(NT + 1) * E], ALU.add)\
                    .then_inc(S["rank_read"], 1)
                for k in range(K):
                    v_.tensor_tensor(row_pick[:, k, :], row_of[:, :], onehot[:, k, :], ALU.mult)\
                        .then_inc(S["rt_rowpick"], 1)
                if not isinstance(i, int) or i >= 2:
                    dve.wait_ge(S[f"scattered{par}"], (i - par) * (8 * K * NT))
                dve.wait_ge(S["rt_rowpick"], 2 * i + 2)
                with nc.allow_low_precision(reason="whole numbers below 2**24"):
                    v_.tensor_reduce(slot[par][:, :], row_pick[:, :, :].rearrange("p k (j e) -> p (k j) e", e=E), AX,
                                     ALU.add).then_inc(S["rt_slot"], 1)
                dve.wait_ge(S["rt_gate0"], i + 1)
                v_.tensor_copy(gates[:, bass.ds(i, 1), 0, :].rearrange("p b j -> p (b j)"), gate0[:, :])\
                    .then_inc(S["rt_gates"], 1)
                v_.tensor_tensor(gates[:, bass.ds(i, 1), 1, :].rearrange("p b j -> p (b j)"),
                                 over_exp[:, NT * E:NT * E + NT], gate0[:, :], ALU.mult).then_inc(S["rt_gates"], 1)
                dve.wait_ge(S["rt_slot"], i + 1)
                v_.tensor_copy(region_rows[:, bass.ds(i * (K * NT), K * NT)], slot[par][:, :])\
                    .then_inc(S["slot_store"], 1)

            stats(0, 0)
            dve.wait_ge(S["wqk_raw_hi"], 1)
            lo(wq_lo[:, :, :], wq[:, :, :], wq_hi[:, :, :], "wqk_raw_lo")
            dve.wait_ge(S["wqk_raw_hi"], 2)
            lo(wk_lo[:, :, :], wk[:, :, :], wk_hi[:, :, :], "wqk_raw_lo")
            dve.wait_ge(S["wr_h"], 1)
            lo(wr_lo[:, :, :], wr[:, :, :], wr_hi[:, :, :], "wr_l")
            stats(1, 0)
            dve.wait_ge(S["wqk_h"], 1)
            lo(wqk_lo[:, :, :].rearrange("p k d -> p (k d)"), bank[4][:, :],
               wqk_hi[:, :, :].rearrange("p k d -> p (k d)"), "wqk_l")
            dve.wait_ge(S["wqk_h"], 2)
            lo(wvT_lo[:, :, :].rearrange("p k d -> p (k d)"), bank[5][:, :],
               wvT_hi[:, :, :].rearrange("p k d -> p (k d)"), "wqk_l")
            xT(0)
            dve.wait_ge(S["s_h"], 1)
            lo(sgu_lo[:, :, :], sgu[:, :, :], sgu_hi[:, :, :], "s_l")
            dve.wait_ge(S["s_h"], 2)
            lo(sd_lo[:, :, :], sd[:, :, :], sd_hi[:, :, :], "s_l")
            q(0)
            v(0)

            def step(i, par, first=False, last=False):
                maxes(i, range(0, 3))
                if not first:
                    x2T(i - 1)
                maxes(i, range(3, 4))
                if not last:
                    xT(i + 1)
                if not first:
                    route_a(i - 1)
                pT(i)
                if not last:
                    q(i + 1)
                if not first:
                    route_b(i - 1, 1 - par)
                if not (isinstance(i, int) and i + 2 >= B):
                    stats(i + 2, 0)
                residual(i)
                stats(i, 1)
                if not last:
                    v(i + 1)

            step(0, 0, first=True)
            with dve.Fori(0, (B - 4) // 2) as u:
                step(2 * u + 1, 1)
                step(2 * u + 2, 0)
            step(B - 3, 1)
            step(B - 2, 0)
            step(B - 1, 1, last=True)
            x2T(B - 1)
            route_a(B - 1)
            route_b(B - 1, 1)

            made = [0]

            def chained(instruction):
                instruction.then_inc(S["map_step"], 1)
                made[0] += 1
                dve.wait_ge(S["map_step"], made[0])

            dve.wait_ge(S["rank_read"], B)
            v_.tensor_copy(row_end[0:1, :], next_row[0:1, :]).then_inc(S["row_end"], 1)
            chained(v_.tensor_tensor(count[:, :], next_row[:, :], region_start[:, :], ALU.subtract))
            chained(v_.tensor_scalar(count_i[:, :], count[:, :], float(P - 1), None, ALU.add))
            chained(v_.tensor_scalar(tiles_i[:, :], count_i[:, :], P.bit_length() - 1, None, ALU.logical_shift_right))
            chained(v_.tensor_copy(tiles_of[:, :], tiles_i[:, :]))
            chained(v_.tensor_tensor_scan(tile_end[:, :], ones_e[:, :], tiles_of[:, :], 0.0, ALU.mult, ALU.add))
            chained(v_.tensor_scalar(passed[:, :], tile_end[:, :], tile_no[:, 0:1], None, ALU.is_le))
            chained(v_.tensor_reduce(tcol[:, 0:1], passed[:, :], AX, ALU.add))
            chained(v_.tensor_tensor(passed_tiles[:, :], passed[:, :], tiles_of[:, :], ALU.mult))
            chained(v_.tensor_reduce(tcol[:, 1:2], passed_tiles[:, :], AX, ALU.add))
            chained(v_.tensor_tensor(tcol[:, 2:3], tile_no[:, :], tcol[:, 1:2], ALU.subtract))
            chained(v_.tensor_scalar(tcol[:, 3:4], tcol[:, 0:1], float(REGION), None, ALU.mult))
            chained(v_.scalar_tensor_tensor(tcol[:, 6:7], tcol[:, 2:3], float(P), tcol[:, 3:4], ALU.mult, ALU.add))
            chained(v_.tensor_tensor(tcol[:, 4:5], tile_no[:, :], tile_end[:, E - 1:E], ALU.is_lt))
            chained(v_.tensor_tensor(tile_vals[:, 0:1], tcol[:, 6:7], tcol[:, 4:5], ALU.mult))
            v_.tensor_scalar(tile_vals[:, 1:2], tcol[:, 0:1], float(E - 1), float(WROW), ALU.min, ALU.mult)\
                .then_inc(S["map_vals"], 1)
            dve.wait_ge(S["map_done"], 1)
            v_.tensor_copy(tile_map[:, :, :].rearrange("a c t -> a (c t)"), bank[6][0:1, 0:2 * TILES])\
                .then_inc(S["map_ready"], 1)
            for c in range(E // 4):
                dve.wait_ge(S["we_h"], c + 1)
                cols = slice(4 * c * WROW, 4 * (c + 1) * WROW)
                lo(we_lo[:, cols], we_raw[:, cols], we_hi[:, cols], "we_l")

            chained(v_.tensor_tensor(shift_of[:, :], tile_end[:, :], tiles_of[:, :], ALU.subtract))
            chained(v_.scalar_tensor_tensor(shift_of[:, :], shift_of[:, :], float(P), region_start[:, :],
                                            ALU.mult, ALU.subtract))
            v_.tensor_copy(shift_step[:, 0:1], shift_of[:, 0:1])
            chained(v_.tensor_tensor(shift_step[:, 1:E], shift_of[:, 1:E], shift_of[:, 0:E - 1], ALU.subtract))
            C = B * K * NT
            dve.wait_ge(S["slot_store"], B)
            chained(v_.tensor_tensor(at_least[:, :, :], region_rows[:, :].unsqueeze(2).to_broadcast([P, C, E]),
                                     region_start[:, :].unsqueeze(1).to_broadcast([P, C, E]), ALU.is_ge))
            chained(v_.tensor_tensor(at_least[:, :, :], at_least[:, :, :],
                                     shift_step[:, :].unsqueeze(1).to_broadcast([P, C, E]), ALU.mult))
            chained(v_.tensor_reduce(row_shift[:, :], at_least[:, :, :], AX, ALU.add))
            v_.tensor_tensor(slots[:, :, :].rearrange("p b c -> p (b c)"), region_rows[:, :], row_shift[:, :], ALU.add)\
                .then_inc(S["slots_ready"], 1)

            def c_x(q):
                for h in range(2):
                    dve.wait_ge(S["cxh"], 2 * q + h + 1)
                    lo(cxT_lo[:, 4 * h:4 * h + 4, :].rearrange("p k t -> p (k t)"), bank[h][:, :],
                       cxT_hi[:, 4 * h:4 * h + 4, :].rearrange("p k t -> p (k t)"), "cxl")

            def c_mul(q):
                for h in range(2):
                    dve.wait_ge(S["cs"], 2 * q + h + 1)
                    v_.tensor_tensor(ch[:, 2 * h:2 * h + 2, :], csilu[:, 2 * h:2 * h + 2, :],
                                     bank[2 + h][:, :].rearrange("p (s c f) -> p s c f", s=2, c=2)[:, :, 1, :],
                                     ALU.mult).then_inc(S["chm"], 1)

            def c_h(q):
                dve.wait_ge(S["chh"], q + 1)
                lo(chT_lo[:, :, :].rearrange("p s t -> p (s t)"), bank[4][:, :],
                   chT_hi[:, :, :].rearrange("p s t -> p (s t)"), "chl")

            def c_step(q, par, first=False, last=False):
                c_mul(q)
                if not last:
                    c_x(q + 1)
                c_h(q)

            c_x(0)
            quads(dve, c_step)

            def d_x(b):
                for k in range(DK):
                    dve.wait_ge(S["dxh"], DK * b + k + 1)
                    lo(dxT_lo[:, k, :], bank[k][:, :], dxT_hi[:, k, :], "dxl")

            def d_mul(b):
                for f in range(FK):
                    dve.wait_ge(S["dsi"], FK * b + f + 1)
                    v_.tensor_tensor(dh[:, f, :], dh[:, f, :], bank[3 + 2 * f][:, :], ALU.mult).then_inc(S["dhm"], 1)

            def d_h(b):
                for f in range(FK):
                    dve.wait_ge(S["dhh"], FK * b + f + 1)
                    lo(dh_lo[:, f, :], dh[:, f, :], dh_hi[:, f, :], "dhl")

            def add_shared(b):
                dve.wait_ge(S["res_in"], 16 * B)
                for m in range(2):
                    dve.wait_ge(S["ddn"], 2 * b + m + 1)
                    rows = res[:, bass.ds(b, 1), 2 * m:2 * m + 2, :].rearrange("p b j d -> p (b j d)")
                    last = v_.tensor_tensor(rows, bank[6 + m][:, :], rows, ALU.add)
                last.then_inc(S["dsum"], 1)

            def add_experts(b, buf):
                dve.wait_ge(S[f"got_in{buf}"], 16 * K * NT * (b // 4 + 1) if isinstance(b, int) else
                            (b - buf) * (4 * K * NT) + 16 * K * NT)
                for k in range(K):
                    dve.wait_ge(S["dsum"] if k == 0 else S["dstep"], b + 1)
                    for n in range(NT):
                        row = res[:, bass.ds(b, 1), n, :].rearrange("p b d -> p (b d)")
                        last = v_.scalar_tensor_tensor(
                            row, got[:, buf, k * NT + n, :],
                            gates[:, bass.ds(b, 1), k, n:n + 1].rearrange("p b j -> p (b j)"), row, ALU.mult, ALU.add)
                    last.then_inc(S["dstep" if k == 0 else "got_used"], 1)

            def d_step(b):
                if not (isinstance(b, int) and b >= B):
                    d_mul(b)
                    if not (isinstance(b, int) and b + 1 >= B):
                        d_x(b + 1)
                    d_h(b)
                if not (isinstance(b, int) and b == 0):
                    add_shared(b - 1)

            dve.wait_ge(S["rt_gates"], 2 * B)
            d_x(0)
            d_step(0)
            d_step(1)
            with dve.Fori(0, (B - 4) // 4) as u:
                for j in range(4):
                    d_step(4 * u + (2 + j))
                    add_experts(4 * u + j, j)
            for b in range(B - 4, B):
                if b + 2 <= B:
                    d_step(b + 2)
                add_experts(b, b % 4)

        @block.tensor
        def _(pe):
            t_ = nc.tensor

            def product(dst, terms):
                n = 0
                for a_hi, a_lo, b_hi, b_lo in terms:
                    for l, r in ((a_hi, b_hi), (a_hi, b_lo), (a_lo, b_hi)):
                        last = t_.matmul(dst, l, r, start=(n == 0), stop=(n == 3 * len(terms) - 1))
                        n += 1
                return last

            def transposes(src, banks, done):
                for k in range(DK):
                    for j in range(NT):
                        last = t_.transpose(banks[k][:, j * P:(j + 1) * P], src[:, j, k * P:(k + 1) * P], ident[:, :])
                    last.then_inc(S[done], 1)

            def T1(i):
                pe.wait_ge(S["xn_ready"], i + 1)
                transposes(xn, bank[0:2], "t1")

            def T2(i, par):
                pe.wait_ge(S["xn2_ready"], i + 1)
                transposes(xn2[par], bank[4:6], "t2")

            def Q(i):
                pe.wait_ge(S["xl"], DK * (i + 1))
                for m in range(DK):
                    cols = slice(m * P, (m + 1) * P)
                    product(bank[4 + m][:, :], [(wqk_hi[:, k, cols], wqk_lo[:, k, cols], xT_hi[:, k, :], xT_lo[:, k, :])
                                                for k in range(DK)]).then_inc(S["q_done"], 1)

            def V(i):
                for j in range(NT):
                    cols = slice(j * P, (j + 1) * P)
                    last = product(bank[2 + j // 2][:, j % 2 * D:(j % 2 + 1) * D],
                                   [(xT_hi[:, k, cols], xT_lo[:, k, cols], wvT_hi[:, k, :], wvT_lo[:, k, :])
                                    for k in range(DK)])
                    if j % 2:
                        last.then_inc(S["v_done"], 1)

            def scores(i, rows):
                for n in rows:
                    cols = slice(n * P, (n + 1) * P)
                    product(bank[n][:, :], [(q_hi[:, k, cols], q_lo[:, k, cols], xT_hi[:, k, :], xT_lo[:, k, :])
                                            for k in range(DK)]).then_inc(S["s_done"], 1)

            def logits(i):
                pe.wait_ge(S["x2l"], DK * (i + 1))
                for j in range(NT):
                    cols = slice(j * P, (j + 1) * P)
                    last = product(bank[4][:, j * E:(j + 1) * E],
                                   [(x2T_hi[:, k, cols], x2T_lo[:, k, cols], wr_hi[:, k, :], wr_lo[:, k, :])
                                    for k in range(DK)])
                last.then_inc(S["logits_done"], 1)

            def rank(i):
                pe.wait_ge(S["rt_mask"], i + 1)
                last = t_.matmul(bank[7][:, 0:NT * E], before[:, :], chosen[:, :], start=True, stop=False,
                                 skip_group_check=True)
                for j in range(NT):
                    for c in range(j + 1, NT + 1):
                        last = t_.matmul(bank[7][:, c * E:(c + 1) * E], ones[:, :], chosen[:, j * E:(j + 1) * E],
                                         start=False, stop=(j == NT - 1), skip_group_check=True)
                last.then_inc(S["rank_done"], 1)

            pe.wait_ge(S["consts"], 2)
            T1(0)
            pe.wait_ge(S["wv_in"], 16)
            for k in range(DK):
                for c in range(DK):
                    last = t_.transpose(bank[5][:, k * D + c * P:k * D + (c + 1) * P], wv[:, c, k * P:(k + 1) * P],
                                        ident[:, :])
            last.then_inc(S["wvT_done"], 1)
            pe.wait_ge(S["wqk_raw_lo"], 2)
            for m in range(DK):
                cols = slice(m * P, (m + 1) * P)
                last = product(bank[4][:, m * D:(m + 1) * D],
                               [(wq_hi[:, k, cols], wq_lo[:, k, cols], wk_hi[:, k, :], wk_lo[:, k, :])
                                for k in range(DK)])
            last.then_inc(S["wqk_done"], 1)
            pe.wait_ge(S["wqk_l"], 2)
            pe.wait_ge(S["wr_l"], 1)
            Q(0)
            V(0)

            def step(i, par, first=False, last=False):
                pe.wait_ge(S["ql"], DK * (i + 1))
                for n in range(3):
                    if n < 2 and not first:
                        pe.wait_ge(S["ptL"], NT * i - 1 + n)
                    if n == 2:
                        pe.wait_ge(S["vl"], 2 * i + 1)
                        if first:
                            pe.wait_ge(S["s_l"], 2)
                    scores(i, [n])
                if not first:
                    T2(i - 1, 1 - par)
                pe.wait_ge(S["vl"], 2 * i + 2)
                scores(i, [3])
                if not last:
                    pe.wait_ge(S["e_done"], NT * i + 2)
                    T1(i + 1)
                if not first:
                    logits(i - 1)
                pe.wait_ge(S["e_done"], NT * i + 4)
                for m in range(NT):
                    if m >= 2 and not last:
                        pe.wait_ge(S["xl"], DK * i + DK + m - 1)
                    for n in range(NT):
                        mm = t_.transpose(bank[(2 + m) % NT][:, n * P:(n + 1) * P], prob[:, n, m * P:(m + 1) * P],
                                          ident[:, :])
                    mm.then_inc(S["pt"], 1)
                if not last:
                    if not first:
                        pe.wait_ge(S["logit_read"], i)
                    Q(i + 1)
                if not first:
                    rank(i - 1)
                pe.wait_ge(S["ptL"], NT * (i + 1))
                for n in range(NT):
                    if n == 2 and not first:
                        pe.wait_ge(S["rank_read"], i)
                    cols = slice(n * P, (n + 1) * P)
                    mm = product(bank[6 + n // 2][:, n % 2 * D:(n % 2 + 1) * D],
                                 [(pT_hi[:, m, cols], pT_lo[:, m, cols], v_hi[:, m, :], v_lo[:, m, :])
                                  for m in range(NT)])
                    if n % 2:
                        mm.then_inc(S["o_done"], 1)
                if not last:
                    V(i + 1)

            batches(pe, step)
            T2(B - 1, 1)
            logits(B - 1)
            rank(B - 1)

            pe.wait_ge(S["map_vals"], 1)
            for c in range(2):
                last = t_.matmul(bank[6][0:1, c * TILES:(c + 1) * TILES], tile_vals[0:TILES, c:c + 1],
                                 ident[0:TILES, 0:TILES], start=True, stop=True)
            last.then_inc(S["map_done"], 1)
            pe.wait_ge(S["map_ready"], 1)
            pe.wait_ge(S["we_l"], E // 4)

            def c_t(q, par):
                pe.wait_ge(S[f"cx_in{par}"], 32 * (q - par) + 64)
                for h in range(2):
                    for s in range(2):
                        for k in range(DK):
                            at = (s * DK + k) * P
                            last = t_.transpose(bank[h][:, at:at + P], cx[par][:, 2 * h + s, k * P:(k + 1) * P],
                                                ident[:, :])
                    last.then_inc(S["ct"], 1)

            def c_gu(q):
                at = of_tiles(mybir.EngineType.PE, 1, q)
                for s in range(4):
                    if s % 2 == 0:
                        pe.wait_ge(S["cxl"], 2 * q + s // 2 + 1)
                    last = product(bank[2 + s // 2][:, s % 2 * 2 * F:(s % 2 + 1) * 2 * F],
                                   [(cxT_hi[:, s * DK + k, :], cxT_lo[:, s * DK + k, :],
                                     we_hi[:, bass.ds(at[s] + k * D, D)], we_lo[:, bass.ds(at[s] + k * D, D)])
                                    for k in range(DK)])
                    if s % 2:
                        last.then_inc(S["cgu"], 1)

            def c_ht(q):
                for s in range(4):
                    if s % 2 == 0:
                        pe.wait_ge(S["chm"], 2 * q + s // 2 + 1)
                    last = t_.transpose(bank[4][:, s * P:(s + 1) * P], ch[:, s, :], ident[:, :])
                last.then_inc(S["cth"], 1)

            def c_dn(q):
                at = of_tiles(mybir.EngineType.PE, 1, q)
                pe.wait_ge(S["chl"], q + 1)
                if not isinstance(q, int) or q >= 1:
                    pe.wait_ge(S["cyr"], 2 * q)
                for s in range(4):
                    last = product(bank[6 + s // 2][:, s % 2 * D:(s % 2 + 1) * D],
                                   [(chT_hi[:, s, :], chT_lo[:, s, :],
                                     we_hi[:, bass.ds(at[s] + 2 * D, D)], we_lo[:, bass.ds(at[s] + 2 * D, D)])])
                    if s % 2:
                        last.then_inc(S["cdn"], 1)

            def c_step(q, par, first=False, last=False):
                c_gu(q)
                if not last:
                    c_t(q + 1, 1 - par)
                if not first:
                    c_dn(q - 1)
                c_ht(q)

            c_t(0, 0)
            quads(pe, c_step)
            c_dn(QUADS - 1)

            def d_t(b, par):
                if isinstance(b, int) and b == 0:
                    pe.wait_ge(S["dx_in0"], 16)
                elif isinstance(b, int):
                    pe.wait_ge(S[f"dx_in{par}"], 16 * ((b - par) // 2) + 16)
                else:
                    pe.wait_ge(S[f"dx_in{par}"], (b - par) * 8 + 16)
                if not isinstance(b, int) or b >= 1:
                    pe.wait_ge(S["dxl"], DK * b)
                transposes(xn2[par], bank[0:2], "dt")

            def d_gu(b):
                pe.wait_ge(S["dxl"], DK * (b + 1))
                for f in range(FK):
                    if not isinstance(b, int) or b >= 1:
                        pe.wait_ge(S["dhm"], FK * b - FK + f + 1)
                    for c in range(2):
                        cols = slice(c * FS + f * P, c * FS + (f + 1) * P)
                        last = product(bank[2 + 2 * f + c][:, :],
                                       [(sgu_hi[:, k, cols], sgu_lo[:, k, cols], dxT_hi[:, k, :], dxT_lo[:, k, :])
                                        for k in range(DK)])
                    last.then_inc(S["dgu"], 1)

            def d_dn(b):
                pe.wait_ge(S["dhl"], FK * (b + 1))
                if not isinstance(b, int) or b >= 1:
                    pe.wait_ge(S["dsum"], b)
                for n in range(NT):
                    cols = slice(n * P, (n + 1) * P)
                    last = product(bank[6 + n // 2][:, n % 2 * D:(n % 2 + 1) * D],
                                   [(dh_hi[:, f, cols], dh_lo[:, f, cols], sd_hi[:, f, :], sd_lo[:, f, :])
                                    for f in range(FK)])
                    if n % 2:
                        last.then_inc(S["ddn"], 1)

            def d_step(b, par, first=False, last=False):
                if not last:
                    d_gu(b)
                    if not (isinstance(b, int) and b + 1 >= B):
                        d_t(b + 1, 1 - par)
                if not first:
                    d_dn(b - 1)

            d_t(0, 0)
            d_step(0, 0, first=True)
            pe.wait_ge(S["cyr"], 2 * QUADS)
            with pe.Fori(0, (B - 2) // 2) as u:
                d_step(2 * u + 1, 1)
                d_step(2 * u + 2, 0)
            d_step(B - 1, 1)
            d_step(B, 0, last=True)


_INS = ["L0_attn_x", "L0_attn_Wq", "L0_attn_Wk", "L0_attn_Wv", "L0_ffn_Wr", "L0_ffn_Wg", "L0_ffn_Wu", "L0_ffn_Wd",
        "L0_ffn_Sg", "L0_ffn_Su", "L0_ffn_Sd"]


def kernel(**inputs):
    import numpy as _np
    import concourse.bacc as _bacc
    from concourse import mybir as _mybir
    from concourse.bass_utils import run_bass_kernel_spmd as _run

    nc = _bacc.Bacc("TRN2", target_bir_lowering=False, num_devices=1)
    arrays, args = {}, []
    for name in _INS:
        a = _np.ascontiguousarray(inputs[name])
        arrays[f"in_{name}"] = a
        args.append(nc.dram_tensor(f"in_{name}", a.shape, _mybir.dt.from_np(a.dtype), kind="ExternalInput").ap())
    args.append(nc.dram_tensor("out_0", inputs[_INS[0]].shape, _mybir.dt.float32, kind="ExternalOutput").ap())
    block_kernel(nc, *args)
    r = _run(nc, [arrays], core_ids=[0])
    return r.results[0]["out_0"]
```

```python
from contextlib import ExitStack

import concourse.bass as bass
from concourse import mybir
from concourse.alu_op_type import AluOpType as ALU

F32, F32R, BF16 = mybir.dt.float32, mybir.dt.float32r, mybir.dt.bfloat16
I32, U32 = mybir.dt.int32, mybir.dt.uint32
ACT = mybir.ActivationFunctionType
AX = mybir.AxisListType.X
P = 128
EPS = 1e-5


def block_kernel(nc, x_in, wq_in, wk_in, wv_in, wr_in, wg_in, wu_in, wd_in, sg_in, su_in, sd_in, out):
    B, N, D = x_in.shape
    E, _, F = wg_in.shape
    FS = sg_in.shape[1]
    NT = N // P
    DK = D // P
    FK = FS // P
    K = 2
    T = B * N
    REGION = T + P
    TILES = T * K // P + E
    QUADS = TILES // 4
    WROW = 3 * D
    assert (NT, DK, FK, F, E) == (4, 2, 2, P, 16) and TILES % 8 == 0 and B % 4 == 0 and TILES <= P

    x_v = x_in.rearrange("b (p j) d -> b p (j d)", p=P)
    out_v = out.rearrange("b (p j) d -> b p (j d)", p=P)
    x1_dram = nc.dram_tensor("x1_dram", [B, P, NT * D], F32, kind="Internal").ap()
    xn2_dram = nc.dram_tensor("xn2_dram", [B, P, NT * D], F32, kind="Internal").ap()
    rows_by_expert = nc.dram_tensor("rows_by_expert", [E * REGION, D], F32, kind="Internal").ap()
    outs_by_tile = nc.dram_tensor("outs_by_tile", [TILES * P, D], F32, kind="Internal").ap()

    with ExitStack() as ctx:
        def sb(name, shape, dt=F32):
            return ctx.enter_context(nc.sbuf_tensor(name, shape, dt))

        def sem(name):
            return ctx.enter_context(nc.semaphore(name))

        ATTN_BYTES = 100 * 1024
        LATE_BYTES = 48 * 1024
        attn_start = -(-nc.sbuf_base // 32) * 32
        attn_area = sb("attn_area", [P, ATTN_BYTES // 4])
        late_start = -(-nc.sbuf_base // 32) * 32
        late_area = sb("late_area", [P, LATE_BYTES // 4])
        places = {}

        def place(area, key, name, shape, dt=F32):
            size = 4
            for n in shape[1:]:
                size *= n
            at = places.get(key, 0)
            places[key] = at + size
            assert at + size <= (ATTN_BYTES if area is attn_area else LATE_BYTES), name
            return nc.alloc_sbuf_tensor_at(name, shape, dt, offset=(attn_start if area is attn_area else late_start) + at)

        x = place(attn_area, "A", "x", [P, B, NT, D])
        xn = place(attn_area, "A", "xn", [P, NT, D])
        xT_hi = place(attn_area, "A", "xT_hi", [P, DK, N], F32R)
        xT_lo = place(attn_area, "A", "xT_lo", [P, DK, N], F32R)
        q_hi = place(attn_area, "A", "q_hi", [P, DK, N], F32R)
        q_lo = place(attn_area, "A", "q_lo", [P, DK, N], F32R)
        v_hi = place(attn_area, "A", "v_hi", [P, NT, D], F32R)
        v_lo = place(attn_area, "A", "v_lo", [P, NT, D], F32R)
        wqk_hi = place(attn_area, "A", "wqk_hi", [P, DK, D], F32R)
        wqk_lo = place(attn_area, "A", "wqk_lo", [P, DK, D], F32R)
        wvT_hi = place(attn_area, "A", "wvT_hi", [P, DK, D], F32R)
        wvT_lo = place(attn_area, "A", "wvT_lo", [P, DK, D], F32R)
        x2T_hi = place(attn_area, "A", "x2T_hi", [P, DK, N], F32R)
        x2T_lo = place(attn_area, "A", "x2T_lo", [P, DK, N], F32R)
        places["setup"] = places["A"]
        prob = place(attn_area, "A", "prob", [P, NT, N])
        pT_hi = place(attn_area, "A", "pT_hi", [P, NT, N], F32R)
        pT_lo = place(attn_area, "A", "pT_lo", [P, NT, N], F32R)
        wq = place(attn_area, "setup", "wq", [P, DK, D])
        wk = place(attn_area, "setup", "wk", [P, DK, D])
        wv = place(attn_area, "setup", "wv", [P, DK, D])
        wq_hi = place(attn_area, "setup", "wq_hi", [P, DK, D], F32R)
        wq_lo = place(attn_area, "setup", "wq_lo", [P, DK, D], F32R)
        wk_hi = place(attn_area, "setup", "wk_hi", [P, DK, D], F32R)
        wk_lo = place(attn_area, "setup", "wk_lo", [P, DK, D], F32R)
        sgu = place(attn_area, "setup", "sgu", [P, DK, 2 * FS])
        sd = place(attn_area, "setup", "sd", [P, FK, D])
        we_hi = place(attn_area, "C", "we_hi", [P, E * WROW], F32R)
        we_raw = place(late_area, "raw", "we_raw", [P, E * WROW])
        we_lo = place(late_area, "lo", "we_lo", [P, E * WROW], F32R)
        cx = [place(attn_area, "C", f"cx{i}", [P, 4, D]) for i in range(2)]
        cxT_hi = place(attn_area, "C", "cxT_hi", [P, 4 * DK, P], F32R)
        cxT_lo = place(attn_area, "C", "cxT_lo", [P, 4 * DK, P], F32R)
        csilu = place(attn_area, "C", "csilu", [P, 4, F])
        ch = place(attn_area, "C", "ch", [P, 4, F])
        chT_hi = place(attn_area, "C", "chT_hi", [P, 4, P], F32R)
        chT_lo = place(attn_area, "C", "chT_lo", [P, 4, P], F32R)
        cy = [place(attn_area, "C", f"cy{i}", [P, 4, D]) for i in range(2)]
        got = place(attn_area, "D", "got", [P, 4, K * NT, D])
        res = place(late_area, "D late", "res", [P, B, NT, D])
        dxT_hi = place(attn_area, "C", "dxT_hi", [P, DK, N], F32R)
        dxT_lo = place(attn_area, "C", "dxT_lo", [P, DK, N], F32R)
        dh = place(attn_area, "C", "dh", [P, FK, N])
        dh_hi = place(attn_area, "C", "dh_hi", [P, FK, N], F32R)
        dh_lo = place(attn_area, "C", "dh_lo", [P, FK, N], F32R)

        xn2 = [sb(f"xn2_{i}", [P, NT, D]) for i in range(2)]
        sgu_hi, sgu_lo = sb("sgu_hi", [P, DK, 2 * FS], F32R), sb("sgu_lo", [P, DK, 2 * FS], F32R)
        sd_hi, sd_lo = sb("sd_hi", [P, FK, D], F32R), sb("sd_lo", [P, FK, D], F32R)
        wr = sb("wr", [P, DK, E])
        wr_hi, wr_lo = sb("wr_hi", [P, DK, E], F32R), sb("wr_lo", [P, DK, E], F32R)
        ident = sb("ident", [P, P])
        before = sb("before", [P, P], BF16)
        ones = sb("ones", [P, P], BF16)
        expert_no = sb("expert_no", [P, E])
        region_start = sb("region_start", [P, E])
        tile_no = sb("tile_no", [P, 1])
        ones_e = sb("ones_e", [P, E])
        minus_half = sb("minus_half", [P, NT])
        zeros = sb("zeros", [P, D])
        stat = [sb(f"stat{k}", [P, NT, 6]) for k in range(2)]
        mean_var = [sb(f"mean_var{k}", [P, NT, 2]) for k in range(2)]
        var_eps = [sb(f"var_eps{k}", [P, NT]) for k in range(2)]
        neg_mean = [sb(f"neg_mean{k}", [P, NT]) for k in range(2)]
        rstd = [sb(f"rstd{k}", [P, NT]) for k in range(2)]
        shift = [sb(f"shift{k}", [P, NT]) for k in range(2)]
        neg_max = sb("neg_max", [P, NT])
        prob_sum = sb("prob_sum", [P, NT])
        prob_sum16 = sb("prob_sum16", [P, NT])
        prob_scale = sb("prob_scale", [P, NT])
        logitT = sb("logitT", [E, N])
        logit = sb("logit", [P, NT, E])
        top = sb("top", [P, NT, 8])
        top_no = sb("top_no", [P, NT, 8], U32)
        onehot = sb("onehot", [P, K, NT * E], BF16)
        over = sb("over", [P, NT * E + NT])
        over_exp = sb("over_exp", [P, NT * E + NT])
        gate_sum = sb("gate_sum", [P, NT])
        gates = sb("gates", [P, B, K, NT])
        next_row = sb("next_row", [P, E])
        row_of = sb("row_of", [P, NT * E])
        row_pick = sb("row_pick", [P, K, NT * E])
        slot = [sb(f"slot{i}", [P, K * NT], U32) for i in range(2)]
        region_rows = sb("region_rows", [P, B * K * NT])
        slots = sb("slots", [P, B, K * NT], U32)
        slot_d = [sb(f"slot_d{i}", [P, K * NT], U32) for i in range(4)]
        count = sb("count", [P, E])
        count_i = sb("count_i", [P, E], I32)
        tiles_i = sb("tiles_i", [P, E], I32)
        tiles_of = sb("tiles_of", [P, E])
        tile_end = sb("tile_end", [P, E])
        passed = sb("passed", [P, E])
        passed_tiles = sb("passed_tiles", [P, E])
        tcol = sb("tcol", [P, 12])
        tile_vals = sb("tile_vals", [P, 2])
        tile_map = sb("tile_map", [1, 2, TILES], I32)
        shift_of = sb("shift_of", [P, E])
        shift_step = sb("shift_step", [P, E])
        reached = sb("reached", [P, B * K * NT, E])
        row_shift = sb("row_shift", [P, B * K * NT])
        row_end = sb("row_end", [1, E], I32)

        bank = [ctx.enter_context(nc.psum_tensor(f"bank{i}", [P, 512], F32)) for i in range(8)]

        names = """x0_in x1_in x_in w_in wv_in wr_in s_in raw_in
            consts pool_step
            wqk_raw_hi wqk_raw_lo wqk_done wvT_done wqk_h wqk_l wr_h wr_l s_h s_l
            bn0 bn1 mv0 mv1 pm0 pm1 ln0 ln1 xn_ready xn2_ready t1 t2 xh xl x2h x2l
            q_done qh ql v_done vh vl s_done mx e_done pt ptH ptL ps16 pscale o_done x1_done
            x1_out xn2_out0 xn2_out1
            logitsT_done logitT_read logits_done logit_read rt_top rt_pick rt_hot rt_over rt_exp rt_sum rt_gates
            rank_done rank_read rt_row rt_rowpick rt_slot rt_next slot_store row_end
            scattered0 scattered1 zero_fill
            map_step map_vals map_done map_ready slots_ready
            we_h we_l
            cx_in0 cx_in1 ct cxh cxl cgu cs chm cth chh chl cdn cyr c_out0 c_out1 got_used
            dx_in0 dx_in1 dt dxh dxl dgu dsi dhm dhh dhl ddn slot_cp got_in0 got_in1
            dsum got_in2 got_in3 res_in out_done dstep""".split()
        S = {n: sem(n) for n in names}

        def copies(k):
            return S[f"bn{k}"], S[f"mv{k}"], S[f"pm{k}"], S[f"ln{k}"]

        block = ctx.enter_context(nc.Block())

        def batches(eng, step):
            for i in range(2):
                step(i, i)
            with eng.Fori(0, (B - 4) // 2) as u:
                for par in range(2):
                    step(2 * u + (2 + par), par)
            for i in range(B - 2, B):
                step(i, i % 2)

        def at_least(i, n):
            return not isinstance(i, int) or i >= n

        def below(i, n):
            return not isinstance(i, int) or i < n

        def quads(eng, step):
            for q in range(3):
                step(q, q % 2, first=(q == 0))
            with eng.Fori(0, (QUADS - 4) // 2) as u:
                step(2 * u + 3, 1)
                step(2 * u + 4, 0)
            step(QUADS - 1, 1, last=True)

        def of_tiles(engine, row, q):
            return nc.values_load_multi_w_load_instructions(
                tile_map[0:1, row, bass.ds(4 * q, 4)], engines=[engine], min_val=0,
                max_val=E * REGION - P if row == 0 else (E - 1) * WROW,
                skip_runtime_bounds_check_because="made from counts that are bounded")[1]

        def zero_tails(eng, engine, half):
            eng.wait_ge(S["row_end"], 1)
            with eng.Fori(0, E // 8) as u:
                ends = nc.values_load_multi_w_load_instructions(
                    row_end[0:1, bass.ds(u * 4 + half * (E // 2), 4)], engines=[engine], min_val=0,
                    max_val=E * REGION - P, skip_runtime_bounds_check_because="a count that is bounded")[1]
                for end in ends:
                    eng.dma_start(rows_by_expert[bass.ds(end, P), :], zeros[:, :]).then_inc(S["zero_fill"], 16)

        @block.sync
        def _(sp):
            sp.dma_start(x[:, 0, :, :].rearrange("p j d -> p (j d)"), x_v[0]).then_inc(S["x0_in"], 16)
            sp.dma_start(wq[:, :, :], wq_in.rearrange("(k p) e -> p k e", p=P)).then_inc(S["w_in"], 16)
            sp.dma_start(wk[:, :, :], wk_in.rearrange("(k p) e -> p k e", p=P)).then_inc(S["w_in"], 16)
            sp.dma_start(wv[:, :, :], wv_in.rearrange("(k p) e -> p k e", p=P)).then_inc(S["wv_in"], 16)
            sp.dma_start(wr[:, :, :], wr_in.rearrange("(k p) e -> p k e", p=P)).then_inc(S["wr_in"], 16)
            sp.dma_start(x[:, 1, :, :].rearrange("p j d -> p (j d)"), x_v[1]).then_inc(S["x1_in"], 16)
            sp.dma_start(sgu[:, :, 0:FS], sg_in.rearrange("(k p) f -> p k f", p=P)).then_inc(S["s_in"], 16)
            sp.dma_start(sgu[:, :, FS:2 * FS], su_in.rearrange("(k p) f -> p k f", p=P)).then_inc(S["s_in"], 16)
            sp.dma_start(sd[:, :, :], sd_in.rearrange("(k p) e -> p k e", p=P)).then_inc(S["s_in"], 16)
            for b in range(2, B):
                sp.dma_start(x[:, b, :, :].rearrange("p j d -> p (j d)"), x_v[b]).then_inc(S["x_in"], 16)
            for e in range(E):
                w = we_raw[:, e * WROW:e * WROW + 2 * D].rearrange("p (k c f) -> p k c f", k=DK, c=2)
                sp.dma_start(w[:, :, 0, :], wg_in[e].rearrange("(k p) f -> p k f", p=P)).then_inc(S["raw_in"], 16)
                sp.dma_start(w[:, :, 1, :], wu_in[e].rearrange("(k p) f -> p k f", p=P)).then_inc(S["raw_in"], 16)
                sp.dma_start(we_raw[:, e * WROW + 2 * D:(e + 1) * WROW], wd_in[e]).then_inc(S["raw_in"], 16)

            def store_batch(i, par):
                sp.wait_ge(S["x1_done"], i + 1)
                sp.dma_start(x1_dram[bass.ds(i, 1), :, :].rearrange("b p n -> (b p) n"),
                             x[:, bass.ds(i, 1), :, :].rearrange("p b j d -> p (b j d)")).then_inc(S["x1_out"], 16)
                sp.wait_ge(S["xn2_ready"], i + 1)
                sp.dma_start(xn2_dram[bass.ds(i, 1), :, :].rearrange("b p n -> (b p) n"),
                             xn2[par][:, :, :].rearrange("p j d -> p (j d)")).then_inc(S[f"xn2_out{par}"], 16)

            batches(sp, store_batch)

            zero_tails(sp, mybir.EngineType.SP, 0)

            sp.wait_ge(S["scattered0"], 16 * K * NT * B // 2)
            sp.wait_ge(S["scattered1"], 16 * K * NT * B // 2)
            sp.wait_ge(S["zero_fill"], 16 * E)
            sp.wait_ge(S["map_ready"], 1)
            sp.wait_ge(S["we_h"], 1)

            def load_quad(q, par):
                if not isinstance(q, int) or q >= 2:
                    sp.wait_ge(S["ct"], 2 * q - 2)
                rows = of_tiles(mybir.EngineType.SP, 0, q)
                for s in range(4):
                    sp.dma_start(cx[par][:, s, :], rows_by_expert[bass.ds(rows[s], P), :]).then_inc(S[f"cx_in{par}"], 16)

            def store_quad(q, par):
                sp.wait_ge(S["cyr"], 2 * q + 2)
                sp.dma_start(outs_by_tile[bass.ds(q * (4 * P), 4 * P), :].rearrange("(s p) d -> p s d", p=P),
                             cy[par][:, :, :]).then_inc(S[f"c_out{par}"], 16)

            def load_rows(b, par):
                if not isinstance(b, int) or b >= 2:
                    sp.wait_ge(S["dt"], 2 * b - 2)
                sp.dma_start(xn2[par][:, :, :].rearrange("p j d -> p (j d)"),
                             xn2_dram[bass.ds(b, 1), :, :].rearrange("b p n -> (b p) n")).then_inc(S[f"dx_in{par}"], 16)

            def load_residual(b):
                sp.dma_start(res[:, bass.ds(b, 1), :, :].rearrange("p b j d -> p (b j d)"),
                             x1_dram[bass.ds(b, 1), :, :].rearrange("b p n -> (b p) n")).then_inc(S["res_in"], 16)

            def store_final(b):
                sp.wait_ge(S["got_used"], b + 1)
                sp.dma_start(out_v[bass.ds(b, 1), :, :].rearrange("b p n -> (b p) n"),
                             res[:, bass.ds(b, 1), :, :].rearrange("p b j d -> p (b j d)")).then_inc(S["out_done"], 16)

            sp.wait_ge(S["x1_out"], 16 * B)
            sp.wait_ge(S["xn2_out0"], 8 * B)
            sp.wait_ge(S["xn2_out1"], 8 * B)

            def step(q, par, first=False, last=False):
                if not (isinstance(q, int) and q + 2 >= QUADS):
                    load_quad(q + 2, par)
                if not first:
                    store_quad(q - 1, 1 - par)

            load_quad(0, 0)
            load_quad(1, 1)
            load_rows(0, 0)
            load_rows(1, 1)
            step(0, 0, first=True)
            with sp.Fori(0, (QUADS - 4) // 2) as u:
                step(2 * u + 1, 1)
                step(2 * u + 2, 0)
            for q in range(QUADS - 3, QUADS + 1):
                step(q, q % 2)

            sp.wait_ge(S["cdn"], 2 * QUADS)
            with sp.Fori(0, B) as b:
                load_residual(b)
            with sp.Fori(0, (B - 2) // 2) as u:
                for par in range(2):
                    load_rows(2 * u + (2 + par), par)
            with sp.Fori(0, B) as b:
                store_final(b)
            sp.wait_ge(S["out_done"], 16 * B)

        @block.gpsimd
        def _(pool):
            g = nc.gpsimd

            def hold(name, n):
                pool.wait_ge(S[name], n)
                pool.nop(nofuse=True)

            g.memset(ident[:, :], 0.0).then_inc(S["pool_step"], 1)
            g.memset(before[:, :], 1.0).then_inc(S["pool_step"], 1)
            g.memset(ones[:, :], 1.0).then_inc(S["pool_step"], 1)
            g.memset(ones_e[:, :], 1.0).then_inc(S["pool_step"], 1)
            g.memset(minus_half[:, :], -0.5).then_inc(S["pool_step"], 1)
            g.memset(zeros[:, :], 0.0).then_inc(S["pool_step"], 1)
            g.iota(expert_no[:, :], [[1, E]], base=0, channel_multiplier=0,
                   allow_small_or_imprecise_dtypes=True).then_inc(S["pool_step"], 1)
            g.iota(region_start[:, :], [[REGION, E]], base=0, channel_multiplier=0,
                   allow_small_or_imprecise_dtypes=True).then_inc(S["pool_step"], 1)
            g.iota(next_row[:, :], [[REGION, E]], base=0, channel_multiplier=0,
                   allow_small_or_imprecise_dtypes=True).then_inc(S["pool_step"], 1)
            g.iota(tile_no[:, :], [[0, 1]], base=0, channel_multiplier=1,
                   allow_small_or_imprecise_dtypes=True).then_inc(S["pool_step"], 1)
            pool.wait_ge(S["pool_step"], 10)
            g.affine_select(out=ident[:, :], in_=ident[:, :], compare_op=ALU.not_equal, fill=1.0, base=0,
                            pattern=[[-1, P]], channel_multiplier=1).then_inc(S["consts"], 1)
            g.affine_select(out=before[:, :], in_=before[:, :], compare_op=ALU.is_gt, fill=0.0, base=0,
                            pattern=[[1, P]], channel_multiplier=-1).then_inc(S["consts"], 1)

            def scale_shift(i, k):
                mv, pm, ln = S[f"mv{k}"], f"pm{k}", S[f"ln{k}"]
                hold(f"mv{k}", i + 1)
                g.tensor_scalar(var_eps[k][:, :], mean_var[k][:, :, 1], EPS, None, ALU.add).then_inc(S[pm], 1)
                g.tensor_scalar(neg_mean[k][:, :], mean_var[k][:, :, 0], -1.0, None, ALU.mult).then_inc(S[pm], 1)
                if not isinstance(i, int) or i >= 1:
                    pool.wait_ge(S["xn_ready" if k == 0 else "xn2_ready"], i)
                hold(pm, 3 * i + 2)
                g.tensor_tensor(rstd[k][:, :], var_eps[k][:, :], minus_half[:, :], ALU.pow).then_inc(S[pm], 1)
                hold(pm, 3 * i + 3)
                g.tensor_tensor(shift[k][:, :], neg_mean[k][:, :], rstd[k][:, :], ALU.mult).then_inc(ln, 1)

            def scatter(i, par):
                hold("rt_slot", i + 1)
                for c in range(K * NT):
                    g.indirect_dma_start(rows_by_expert, bass.IndirectOffsetOnAxis(ap=slot[par][:, c:c + 1], axis=0),
                                         xn2[par][:, c % NT, :], None).then_inc(S[f"scattered{par}"], 16)

            def step(i, par):
                if at_least(i, 2):
                    scatter(i - 2, par)
                if below(i, B - 2):
                    scale_shift(i + 2, 0)
                scale_shift(i, 1)

            scale_shift(0, 0)
            scale_shift(1, 0)
            batches(pool, step)
            scatter(B - 2, 0)
            scatter(B - 1, 1)

            def gather(b, buf):
                if not isinstance(b, int) or b >= 4:
                    hold("got_used", b - 3)
                g.tensor_copy(slot_d[buf][:, :], slots[:, bass.ds(b, 1), :].rearrange("p b c -> p (b c)"))\
                    .then_inc(S["slot_cp"], 1)
                hold("slot_cp", b + 1)
                for c in range(K * NT):
                    g.indirect_dma_start(got[:, buf, c, :], None, outs_by_tile,
                                         bass.IndirectOffsetOnAxis(ap=slot_d[buf][:, c:c + 1], axis=0))\
                        .then_inc(S[f"got_in{buf}"], 16)

            pool.wait_ge(S["slots_ready"], 1)
            pool.wait_ge(S["c_out0"], 8 * QUADS)
            pool.wait_ge(S["c_out1"], 8 * QUADS)
            for b in range(4):
                gather(b, b)
            with pool.Fori(0, (B - 4) // 4) as u:
                for b in range(4):
                    gather(4 * u + (4 + b), b)

        @block.scalar
        def _(act):
            a = nc.scalar

            def hi(dst, src, done):
                return a.activation(dst, src, ACT.Copy).then_inc(S[done], 1)

            def normalise(i, k, par=0):
                act.wait_ge(S[f"ln{k}"], i + 1)
                if k == 0:
                    dst, done = xn, "xn_ready"
                    if not isinstance(i, int) or i >= 1:
                        act.wait_ge(S["t1"], DK * i)
                else:
                    dst, done = xn2[par], "xn2_ready"
                    if not isinstance(i, int) or i >= 2:
                        act.wait_ge(S[f"xn2_out{par}"], (i - par) * 8)
                        act.wait_ge(S[f"scattered{par}"], (i - par) * (8 * K * NT))
                for j in range(NT):
                    src = x[:, bass.ds(i, 1), j, :].rearrange("p b d -> p (b d)")
                    last = a.activation(dst[:, j, :], src, ACT.Identity, bias=shift[k][:, j:j + 1],
                                        scale=rstd[k][:, j:j + 1])
                last.then_inc(S[done], 1)

            def xT(i):
                for k in range(DK):
                    act.wait_ge(S["t1"], DK * i + k + 1)
                    hi(xT_hi[:, k, :], bank[k][:, :], "xh")

            def x2T(i):
                for k in range(DK):
                    act.wait_ge(S["t2"], DK * i + k + 1)
                    hi(x2T_hi[:, k, :], bank[6 + k][:, :], "x2h")

            def q(i):
                for m in range(DK):
                    act.wait_ge(S["q_done"], DK * i + m + 1)
                    hi(q_hi[:, m, :], bank[4 + m][:, :], "qh")

            def v(i):
                for m in range(2):
                    act.wait_ge(S["v_done"], 2 * i + m + 1)
                    hi(v_hi[:, 2 * m:2 * m + 2, :].rearrange("p j d -> p (j d)"), bank[2 + m][:, :], "vh")

            def exps(i, rows):
                for n in rows:
                    act.wait_ge(S["mx"], NT * i + n + 1)
                    a.activation(prob[:, n, :], bank[n][:, :], ACT.Exp, bias=neg_max[:, n:n + 1],
                                 accum_out=prob_sum[:, n:n + 1]).then_inc(S["e_done"], 1)

            def pT(i, blocks):
                for m in blocks:
                    act.wait_ge(S["pt"], NT * i + m + 1)
                    hi(pT_hi[:, m, :], bank[(2 + m) % NT][:, :], "ptH")

            def logitsT(i):
                act.wait_ge(S["logitsT_done"], i + 1)
                a.activation(logitT[:, :], bank[2][0:E, :], ACT.Copy).then_inc(S["logitT_read"], 1)

            def gate_exp(i):
                act.wait_ge(S["rt_over"], 2 * i + 2)
                a.activation(over_exp[:, :], over[:, :], ACT.Exp).then_inc(S["rt_exp"], 1)

            act.wait_ge(S["w_in"], 32)
            hi(wq_hi[:, :, :], wq[:, :, :], "wqk_raw_hi")
            hi(wk_hi[:, :, :], wk[:, :, :], "wqk_raw_hi")
            act.wait_ge(S["wr_in"], 16)
            hi(wr_hi[:, :, :], wr[:, :, :], "wr_h")
            normalise(0, 0)
            act.wait_ge(S["wqk_done"], 1)
            hi(wqk_hi[:, :, :].rearrange("p k d -> p (k d)"), bank[4][:, :], "wqk_h")
            act.wait_ge(S["wvT_done"], 1)
            hi(wvT_hi[:, :, :].rearrange("p k d -> p (k d)"), bank[5][:, :], "wqk_h")
            xT(0)
            act.wait_ge(S["s_in"], 48)
            hi(sgu_hi[:, :, :], sgu[:, :, :], "s_h")
            hi(sd_hi[:, :, :], sd[:, :, :], "s_h")
            q(0)
            normalise(1, 0)
            v(0)

            def step(i, par):
                exps(i, range(NT))
                if below(i, B - 1):
                    xT(i + 1)
                pT(i, range(0, 2))
                if at_least(i, 1):
                    x2T(i - 1)
                pT(i, range(2, 4))
                if below(i, B - 1):
                    q(i + 1)
                if at_least(i, 1):
                    logitsT(i - 1)
                    gate_exp(i - 1)
                if below(i, B - 2):
                    normalise(i + 2, 0)
                if below(i, B - 1):
                    v(i + 1)
                normalise(i, 1, par)

            batches(act, step)
            x2T(B - 1)
            logitsT(B - 1)
            gate_exp(B - 1)

            act.wait_ge(S["raw_in"], 16 * 3 * E)
            act.wait_ge(S["logitsT_done"], B)
            act.wait_ge(S["x2l"], DK * B)
            act.wait_ge(S["x1_out"], 16 * B)
            def weights_hi(c):
                cols = slice(4 * c * WROW, 4 * (c + 1) * WROW)
                hi(we_hi[:, cols], we_raw[:, cols], "we_h")

            weights_hi(0)
            weights_hi(1)
            zero_tails(act, mybir.EngineType.Activation, 1)
            weights_hi(2)
            weights_hi(3)

            def c_x(q):
                for h in range(2):
                    act.wait_ge(S["ct"], 2 * q + h + 1)
                    hi(cxT_hi[:, 4 * h:4 * h + 4, :].rearrange("p k t -> p (k t)"), bank[h][:, :], "cxh")

            def c_silu(q):
                for h in range(2):
                    act.wait_ge(S["cgu"], 2 * q + h + 1)
                    a.activation(csilu[:, 2 * h:2 * h + 2, :],
                                 bank[2 + h][:, :].rearrange("p (s c f) -> p s c f", s=2, c=2)[:, :, 0, :],
                                 ACT.Silu).then_inc(S["cs"], 1)

            def c_h(q):
                act.wait_ge(S["cth"], q + 1)
                hi(chT_hi[:, :, :].rearrange("p s t -> p (s t)"), bank[4][:, :], "chh")

            def c_y(q, par):
                if not isinstance(q, int) or q >= 2:
                    act.wait_ge(S[f"c_out{par}"], 8 * (q - par))
                for h in range(2):
                    act.wait_ge(S["cdn"], 2 * q + h + 1)
                    a.activation(cy[par][:, 2 * h:2 * h + 2, :].rearrange("p s d -> p (s d)"), bank[6 + h][:, :],
                                 ACT.Copy).then_inc(S["cyr"], 1)

            def c_step(q, par, first=False, last=False):
                c_silu(q)
                if not last:
                    c_x(q + 1)
                if not first:
                    c_y(q - 1, 1 - par)
                c_h(q)

            c_x(0)
            quads(act, c_step)
            c_y(QUADS - 1, 1)

            def d_x(b):
                for k in range(DK):
                    act.wait_ge(S["dt"], DK * b + k + 1)
                    hi(dxT_hi[:, k, :], bank[k][:, :], "dxh")

            def d_silu(b):
                for f in range(FK):
                    act.wait_ge(S["dgu"], FK * b + f + 1)
                    if not isinstance(b, int) or b >= 1:
                        act.wait_ge(S["dhl"], FK * b)
                    a.activation(dh[:, f, :], bank[2 + 2 * f][:, :], ACT.Silu).then_inc(S["dsi"], 1)

            def d_h(b):
                if not isinstance(b, int) or b >= 1:
                    act.wait_ge(S["ddn"], 2 * b)
                for f in range(FK):
                    act.wait_ge(S["dhm"], FK * b + f + 1)
                    hi(dh_hi[:, f, :], dh[:, f, :], "dhh")

            def d_step(b, par, first=False, last=False):
                if not last:
                    d_silu(b)
                    if not (isinstance(b, int) and b + 1 >= B):
                        d_x(b + 1)
                    d_h(b)

            d_x(0)
            d_step(0, 0, first=True)
            with act.Fori(0, (B - 2) // 2) as u:
                d_step(2 * u + 1, 1)
                d_step(2 * u + 2, 0)
            d_step(B - 1, 1)

        @block.vector
        def _(dve):
            v_ = nc.vector

            def hold(name, n):
                dve.wait_ge(S[name], n)
                dve.nop(nofuse=True)

            def lo(dst, src, hi_half, done):
                return v_.tensor_tensor(dst, src, hi_half.bitcast(F32), ALU.subtract).then_inc(S[done], 1)

            def stats(i, k):
                if k == 0:
                    if isinstance(i, int) and i < 2:
                        dve.wait_ge(S[f"x{i}_in"], 16)
                    else:
                        dve.wait_ge(S["x_in"], 16 * (B - 2))
                else:
                    dve.wait_ge(S["x1_done"], i + 1)
                if not isinstance(i, int) or i >= 1:
                    dve.wait_ge(S[f"pm{k}"], 3 * i)
                    hold(f"ln{k}", i)
                for j in range(NT):
                    last = v_.bn_stats(stat[k][:, j, :], x[:, bass.ds(i, 1), j, :].rearrange("p b d -> p (b d)"))
                last.then_inc(S[f"bn{k}"], 1)
                hold(f"bn{k}", i + 1)
                for j in range(NT):
                    last = v_.bn_aggr(mean_var[k][:, j, :], stat[k][:, j, :])
                last.then_inc(S[f"mv{k}"], 1)

            def maxes(i, rows):
                for n in rows:
                    dve.wait_ge(S["s_done"], NT * i + n + 1)
                    v_.tensor_reduce(neg_max[:, n:n + 1], bank[n][:, :], AX, ALU.max, negate=True)\
                        .then_inc(S["mx"], 1)

            def xT(i):
                for k in range(DK):
                    dve.wait_ge(S["xh"], DK * i + k + 1)
                    lo(xT_lo[:, k, :], bank[k][:, :], xT_hi[:, k, :], "xl")

            def x2T(i):
                for k in range(DK):
                    dve.wait_ge(S["x2h"], DK * i + k + 1)
                    lo(x2T_lo[:, k, :], bank[6 + k][:, :], x2T_hi[:, k, :], "x2l")

            def q(i):
                for m in range(DK):
                    dve.wait_ge(S["qh"], DK * i + m + 1)
                    lo(q_lo[:, m, :], bank[4 + m][:, :], q_hi[:, m, :], "ql")

            def v(i):
                for m in range(2):
                    dve.wait_ge(S["vh"], 2 * i + m + 1)
                    lo(v_lo[:, 2 * m:2 * m + 2, :].rearrange("p j d -> p (j d)"), bank[2 + m][:, :],
                       v_hi[:, 2 * m:2 * m + 2, :].rearrange("p j d -> p (j d)"), "vl")

            def pT(i, blocks):
                for m in blocks:
                    dve.wait_ge(S["ptH"], NT * i + m + 1)
                    lo(pT_lo[:, m, :], bank[(2 + m) % NT][:, :], pT_hi[:, m, :], "ptL")

            def residual(i):
                dve.wait_ge(S["e_done"], NT * (i + 1))
                v_.tensor_scalar(prob_sum16[:, :], prob_sum[:, :], float(D) ** 0.5, None, ALU.mult)\
                    .then_inc(S["ps16"], 1)
                dve.wait_ge(S["ps16"], i + 1)
                v_.reciprocal(prob_scale[:, :], prob_sum16[:, :]).then_inc(S["pscale"], 1)
                dve.wait_ge(S["pscale"], i + 1)
                for n in range(NT):
                    if n % 2 == 0:
                        dve.wait_ge(S["o_done"], 2 * i + n // 2 + 1)
                    row = x[:, bass.ds(i, 1), n, :].rearrange("p b d -> p (b d)")
                    last = v_.scalar_tensor_tensor(row, bank[6 + n // 2][:, n % 2 * D:(n % 2 + 1) * D],
                                                   prob_scale[:, n:n + 1], row, ALU.mult, ALU.add)
                last.then_inc(S["x1_done"], 1)

            per_e = lambda t: t.rearrange("p (j e) -> p j e", e=E)
            wide = lambda col: col.unsqueeze(2).to_broadcast([P, NT, E])

            def route_a(i):
                dve.wait_ge(S["logits_done"], i + 1)
                v_.tensor_copy(logit[:, :, :].rearrange("p j e -> p (j e)"), bank[3][:, 0:NT * E])\
                    .then_inc(S["logit_read"], 1)
                hold("logit_read", i + 1)
                for j in range(NT):
                    last = v_.max(top[:, j, :], logit[:, j, :])
                last.then_inc(S["rt_top"], 1)
                hold("rt_top", i + 1)
                for j in range(NT):
                    last = v_.max_index(top_no[:, j, :], top[:, j, :], logit[:, j, :])
                last.then_inc(S["rt_pick"], 1)
                v_.tensor_tensor(per_e(over[:, 0:NT * E]), logit[:, :, :], wide(top[:, :, 0]), ALU.subtract)\
                    .then_inc(S["rt_over"], 1)
                v_.tensor_tensor(over[:, NT * E:NT * E + NT], top[:, :, 1], top[:, :, 0], ALU.subtract)\
                    .then_inc(S["rt_over"], 1)
                dve.wait_ge(S["rt_pick"], i + 1)
                v_.tensor_tensor(onehot[:, :, :].rearrange("p k (j e) -> p k j e", e=E),
                                 expert_no[:, :].unsqueeze(1).unsqueeze(1).to_broadcast([P, K, NT, E]),
                                 top_no[:, :, 0:K].rearrange("p j k -> p k j").unsqueeze(3).to_broadcast([P, K, NT, E]),
                                 ALU.is_equal).then_inc(S["rt_hot"], 1)

            def route_b(i, par):
                dve.wait_ge(S["rt_exp"], i + 1)
                v_.tensor_reduce(gate_sum[:, :], per_e(over_exp[:, 0:NT * E]), AX, ALU.add).then_inc(S["rt_sum"], 1)
                dve.wait_ge(S["rank_done"], i + 1)
                v_.tensor_tensor(per_e(row_of[:, :]), per_e(bank[5][:, 0:NT * E]),
                                 next_row[:, :].unsqueeze(1).to_broadcast([P, NT, E]), ALU.add).then_inc(S["rt_row"], 1)
                dve.wait_ge(S["rt_sum"], i + 1)
                v_.reciprocal(gates[:, bass.ds(i, 1), 0, :].rearrange("p b j -> p (b j)"), gate_sum[:, :])\
                    .then_inc(S["rt_gates"], 1)
                dve.wait_ge(S["rt_row"], i + 1)
                v_.tensor_tensor(row_pick[:, :, :], row_of[:, :].unsqueeze(1).to_broadcast([P, K, NT * E]),
                                 onehot[:, :, :], ALU.mult).then_inc(S["rt_rowpick"], 1)
                v_.tensor_tensor(next_row[:, :], next_row[:, :], bank[5][:, NT * E:(NT + 1) * E], ALU.add)\
                    .then_inc(S["rank_read"], 1)
                if at_least(i, 2):
                    dve.wait_ge(S[f"scattered{par}"], (i - par) * (8 * K * NT))
                dve.wait_ge(S["rt_rowpick"], i + 1)
                with nc.allow_low_precision(reason="whole numbers below 2**24"):
                    v_.tensor_reduce(slot[par][:, :], row_pick[:, :, :].rearrange("p k (j e) -> p (k j) e", e=E), AX,
                                     ALU.add).then_inc(S["rt_slot"], 1)
                dve.wait_ge(S["rt_gates"], 2 * i + 1)
                v_.tensor_tensor(gates[:, bass.ds(i, 1), 1, :].rearrange("p b j -> p (b j)"),
                                 over_exp[:, NT * E:NT * E + NT],
                                 gates[:, bass.ds(i, 1), 0, :].rearrange("p b j -> p (b j)"), ALU.mult)\
                    .then_inc(S["rt_gates"], 1)
                dve.wait_ge(S["rt_slot"], i + 1)
                v_.tensor_copy(region_rows[:, bass.ds(i * (K * NT), K * NT)], slot[par][:, :])\
                    .then_inc(S["slot_store"], 1)

            stats(0, 0)
            dve.wait_ge(S["wqk_raw_hi"], 1)
            lo(wq_lo[:, :, :], wq[:, :, :], wq_hi[:, :, :], "wqk_raw_lo")
            dve.wait_ge(S["wqk_raw_hi"], 2)
            lo(wk_lo[:, :, :], wk[:, :, :], wk_hi[:, :, :], "wqk_raw_lo")
            dve.wait_ge(S["wr_h"], 1)
            lo(wr_lo[:, :, :], wr[:, :, :], wr_hi[:, :, :], "wr_l")
            stats(1, 0)
            dve.wait_ge(S["wqk_h"], 1)
            lo(wqk_lo[:, :, :].rearrange("p k d -> p (k d)"), bank[4][:, :],
               wqk_hi[:, :, :].rearrange("p k d -> p (k d)"), "wqk_l")
            dve.wait_ge(S["wqk_h"], 2)
            lo(wvT_lo[:, :, :].rearrange("p k d -> p (k d)"), bank[5][:, :],
               wvT_hi[:, :, :].rearrange("p k d -> p (k d)"), "wqk_l")
            xT(0)
            dve.wait_ge(S["s_h"], 1)
            lo(sgu_lo[:, :, :], sgu[:, :, :], sgu_hi[:, :, :], "s_l")
            dve.wait_ge(S["s_h"], 2)
            lo(sd_lo[:, :, :], sd[:, :, :], sd_hi[:, :, :], "s_l")
            q(0)
            v(0)

            def step(i, par):
                maxes(i, range(NT))
                if at_least(i, 2):
                    route_b(i - 2, par)
                if below(i, B - 1):
                    xT(i + 1)
                pT(i, range(0, 2))
                if at_least(i, 1):
                    x2T(i - 1)
                pT(i, range(2, 4))
                if below(i, B - 1):
                    q(i + 1)
                if below(i, B - 2):
                    stats(i + 2, 0)
                if at_least(i, 1):
                    route_a(i - 1)
                residual(i)
                stats(i, 1)
                if below(i, B - 1):
                    v(i + 1)

            batches(dve, step)
            route_b(B - 2, 0)
            x2T(B - 1)
            route_a(B - 1)
            route_b(B - 1, 1)

            made = [0]

            def chained(instruction):
                instruction.then_inc(S["map_step"], 1)
                made[0] += 1
                dve.wait_ge(S["map_step"], made[0])

            dve.wait_ge(S["rank_read"], B)
            v_.tensor_copy(row_end[0:1, :], next_row[0:1, :]).then_inc(S["row_end"], 1)
            chained(v_.tensor_tensor(count[:, :], next_row[:, :], region_start[:, :], ALU.subtract))
            chained(v_.tensor_scalar(count_i[:, :], count[:, :], float(P - 1), None, ALU.add))
            chained(v_.tensor_scalar(tiles_i[:, :], count_i[:, :], P.bit_length() - 1, None, ALU.logical_shift_right))
            chained(v_.tensor_copy(tiles_of[:, :], tiles_i[:, :]))
            chained(v_.tensor_tensor_scan(tile_end[:, :], ones_e[:, :], tiles_of[:, :], 0.0, ALU.mult, ALU.add))
            chained(v_.tensor_scalar(passed[:, :], tile_end[:, :], tile_no[:, 0:1], None, ALU.is_le))
            chained(v_.tensor_reduce(tcol[:, 0:1], passed[:, :], AX, ALU.add))
            chained(v_.tensor_tensor(passed_tiles[:, :], passed[:, :], tiles_of[:, :], ALU.mult))
            chained(v_.tensor_reduce(tcol[:, 1:2], passed_tiles[:, :], AX, ALU.add))
            chained(v_.tensor_tensor(tcol[:, 2:3], tile_no[:, :], tcol[:, 1:2], ALU.subtract))
            chained(v_.tensor_scalar(tcol[:, 3:4], tcol[:, 0:1], float(REGION), None, ALU.mult))
            chained(v_.scalar_tensor_tensor(tcol[:, 6:7], tcol[:, 2:3], float(P), tcol[:, 3:4], ALU.mult, ALU.add))
            chained(v_.tensor_tensor(tcol[:, 4:5], tile_no[:, :], tile_end[:, E - 1:E], ALU.is_lt))
            chained(v_.tensor_tensor(tile_vals[:, 0:1], tcol[:, 6:7], tcol[:, 4:5], ALU.mult))
            v_.tensor_scalar(tile_vals[:, 1:2], tcol[:, 0:1], float(E - 1), float(WROW), ALU.min, ALU.mult)\
                .then_inc(S["map_vals"], 1)
            dve.wait_ge(S["map_done"], 1)
            v_.tensor_copy(tile_map[:, :, :].rearrange("a c t -> a (c t)"), bank[6][0:1, 0:2 * TILES])\
                .then_inc(S["map_ready"], 1)
            for c in range(E // 4):
                dve.wait_ge(S["we_h"], c + 1)
                cols = slice(4 * c * WROW, 4 * (c + 1) * WROW)
                lo(we_lo[:, cols], we_raw[:, cols], we_hi[:, cols], "we_l")

            chained(v_.tensor_tensor(shift_of[:, :], tile_end[:, :], tiles_of[:, :], ALU.subtract))
            chained(v_.scalar_tensor_tensor(shift_of[:, :], shift_of[:, :], float(P), region_start[:, :],
                                            ALU.mult, ALU.subtract))
            v_.tensor_copy(shift_step[:, 0:1], shift_of[:, 0:1])
            chained(v_.tensor_tensor(shift_step[:, 1:E], shift_of[:, 1:E], shift_of[:, 0:E - 1], ALU.subtract))
            C = B * K * NT
            dve.wait_ge(S["slot_store"], B)
            chained(v_.tensor_tensor(reached[:, :, :], region_rows[:, :].unsqueeze(2).to_broadcast([P, C, E]),
                                     region_start[:, :].unsqueeze(1).to_broadcast([P, C, E]), ALU.is_ge))
            chained(v_.tensor_tensor(reached[:, :, :], reached[:, :, :],
                                     shift_step[:, :].unsqueeze(1).to_broadcast([P, C, E]), ALU.mult))
            chained(v_.tensor_reduce(row_shift[:, :], reached[:, :, :], AX, ALU.add))
            v_.tensor_tensor(slots[:, :, :].rearrange("p b c -> p (b c)"), region_rows[:, :], row_shift[:, :], ALU.add)\
                .then_inc(S["slots_ready"], 1)

            def c_x(q):
                for h in range(2):
                    dve.wait_ge(S["cxh"], 2 * q + h + 1)
                    lo(cxT_lo[:, 4 * h:4 * h + 4, :].rearrange("p k t -> p (k t)"), bank[h][:, :],
                       cxT_hi[:, 4 * h:4 * h + 4, :].rearrange("p k t -> p (k t)"), "cxl")

            def c_mul(q):
                for h in range(2):
                    dve.wait_ge(S["cs"], 2 * q + h + 1)
                    v_.tensor_tensor(ch[:, 2 * h:2 * h + 2, :], csilu[:, 2 * h:2 * h + 2, :],
                                     bank[2 + h][:, :].rearrange("p (s c f) -> p s c f", s=2, c=2)[:, :, 1, :],
                                     ALU.mult).then_inc(S["chm"], 1)

            def c_h(q):
                dve.wait_ge(S["chh"], q + 1)
                lo(chT_lo[:, :, :].rearrange("p s t -> p (s t)"), bank[4][:, :],
                   chT_hi[:, :, :].rearrange("p s t -> p (s t)"), "chl")

            def c_step(q, par, first=False, last=False):
                c_mul(q)
                if not last:
                    c_x(q + 1)
                c_h(q)

            c_x(0)
            quads(dve, c_step)

            def d_x(b):
                for k in range(DK):
                    dve.wait_ge(S["dxh"], DK * b + k + 1)
                    lo(dxT_lo[:, k, :], bank[k][:, :], dxT_hi[:, k, :], "dxl")

            def d_mul(b):
                for f in range(FK):
                    dve.wait_ge(S["dsi"], FK * b + f + 1)
                    v_.tensor_tensor(dh[:, f, :], dh[:, f, :], bank[3 + 2 * f][:, :], ALU.mult).then_inc(S["dhm"], 1)

            def d_h(b):
                for f in range(FK):
                    dve.wait_ge(S["dhh"], FK * b + f + 1)
                    lo(dh_lo[:, f, :], dh[:, f, :], dh_hi[:, f, :], "dhl")

            def add_shared(b):
                dve.wait_ge(S["res_in"], 16 * B)
                for m in range(2):
                    dve.wait_ge(S["ddn"], 2 * b + m + 1)
                    rows = res[:, bass.ds(b, 1), 2 * m:2 * m + 2, :].rearrange("p b j d -> p (b j d)")
                    last = v_.tensor_tensor(rows, bank[6 + m][:, :], rows, ALU.add)
                last.then_inc(S["dsum"], 1)

            def add_experts(b, buf):
                dve.wait_ge(S[f"got_in{buf}"], 16 * K * NT * (b // 4 + 1) if isinstance(b, int) else
                            (b - buf) * (4 * K * NT) + 16 * K * NT)
                for k in range(K):
                    dve.wait_ge(S["dsum"] if k == 0 else S["dstep"], b + 1)
                    for n in range(NT):
                        row = res[:, bass.ds(b, 1), n, :].rearrange("p b d -> p (b d)")
                        last = v_.scalar_tensor_tensor(
                            row, got[:, buf, k * NT + n, :],
                            gates[:, bass.ds(b, 1), k, n:n + 1].rearrange("p b j -> p (b j)"), row, ALU.mult, ALU.add)
                    last.then_inc(S["dstep" if k == 0 else "got_used"], 1)

            def d_step(b):
                if not (isinstance(b, int) and b >= B):
                    d_mul(b)
                    if not (isinstance(b, int) and b + 1 >= B):
                        d_x(b + 1)
                    d_h(b)
                if not (isinstance(b, int) and b == 0):
                    add_shared(b - 1)

            dve.wait_ge(S["rt_gates"], 2 * B)
            d_x(0)
            d_step(0)
            d_step(1)
            with dve.Fori(0, (B - 4) // 4) as u:
                for j in range(4):
                    d_step(4 * u + (2 + j))
                    add_experts(4 * u + j, j)
            for b in range(B - 4, B):
                if b + 2 <= B:
                    d_step(b + 2)
                add_experts(b, b % 4)

        @block.tensor
        def _(pe):
            t_ = nc.tensor

            def product(dst, terms):
                n = 0
                for a_hi, a_lo, b_hi, b_lo in terms:
                    for l, r in ((a_hi, b_hi), (a_hi, b_lo), (a_lo, b_hi)):
                        last = t_.matmul(dst, l, r, start=(n == 0), stop=(n == 3 * len(terms) - 1))
                        n += 1
                return last

            def transposes(src, banks, done):
                for k in range(DK):
                    for j in range(NT):
                        last = t_.transpose(banks[k][:, j * P:(j + 1) * P], src[:, j, k * P:(k + 1) * P], ident[:, :])
                    last.then_inc(S[done], 1)

            def T1(i):
                pe.wait_ge(S["xn_ready"], i + 1)
                transposes(xn, bank[0:2], "t1")

            def T2(i, par):
                pe.wait_ge(S["xn2_ready"], i + 1)
                transposes(xn2[par], bank[6:8], "t2")

            def Q(i):
                pe.wait_ge(S["xl"], DK * (i + 1))
                for m in range(DK):
                    cols = slice(m * P, (m + 1) * P)
                    product(bank[4 + m][:, :], [(wqk_hi[:, k, cols], wqk_lo[:, k, cols], xT_hi[:, k, :], xT_lo[:, k, :])
                                                for k in range(DK)]).then_inc(S["q_done"], 1)

            def V(i):
                for j in range(NT):
                    cols = slice(j * P, (j + 1) * P)
                    last = product(bank[2 + j // 2][:, j % 2 * D:(j % 2 + 1) * D],
                                   [(xT_hi[:, k, cols], xT_lo[:, k, cols], wvT_hi[:, k, :], wvT_lo[:, k, :])
                                    for k in range(DK)])
                    if j % 2:
                        last.then_inc(S["v_done"], 1)

            def scores(i, rows):
                for n in rows:
                    cols = slice(n * P, (n + 1) * P)
                    product(bank[n][:, :], [(q_hi[:, k, cols], q_lo[:, k, cols], xT_hi[:, k, :], xT_lo[:, k, :])
                                            for k in range(DK)]).then_inc(S["s_done"], 1)

            def logitsT(i):
                pe.wait_ge(S["x2l"], DK * (i + 1))
                product(bank[2][0:E, :], [(wr_hi[:, k, :], wr_lo[:, k, :], x2T_hi[:, k, :], x2T_lo[:, k, :])
                                          for k in range(DK)]).then_inc(S["logitsT_done"], 1)

            def logits(i):
                pe.wait_ge(S["logitT_read"], i + 1)
                pe.nop(nofuse=True)
                for j in range(NT):
                    last = t_.transpose(bank[3][:, j * E:(j + 1) * E], logitT[:, j * P:(j + 1) * P], ident[0:E, 0:E])
                last.then_inc(S["logits_done"], 1)

            def rank(i):
                pe.wait_ge(S["rt_hot"], i + 1)
                for k in range(K):
                    t_.matmul(bank[5][:, 0:NT * E], before[:, :], onehot[:, k, :], start=(k == 0), stop=False,
                              skip_group_check=True)
                for k in range(K):
                    for j in range(NT):
                        for c in range(j + 1, NT + 1):
                            last = t_.matmul(bank[5][:, c * E:(c + 1) * E], ones[:, :], onehot[:, k, j * E:(j + 1) * E],
                                             start=False, stop=(k == K - 1 and j == NT - 1), skip_group_check=True)
                last.then_inc(S["rank_done"], 1)

            pe.wait_ge(S["consts"], 2)
            T1(0)
            pe.wait_ge(S["wv_in"], 16)
            for k in range(DK):
                for c in range(DK):
                    last = t_.transpose(bank[5][:, k * D + c * P:k * D + (c + 1) * P], wv[:, c, k * P:(k + 1) * P],
                                        ident[:, :])
            last.then_inc(S["wvT_done"], 1)
            pe.wait_ge(S["wqk_raw_lo"], 2)
            for m in range(DK):
                cols = slice(m * P, (m + 1) * P)
                last = product(bank[4][:, m * D:(m + 1) * D],
                               [(wq_hi[:, k, cols], wq_lo[:, k, cols], wk_hi[:, k, :], wk_lo[:, k, :])
                                for k in range(DK)])
            last.then_inc(S["wqk_done"], 1)
            pe.wait_ge(S["wqk_l"], 2)
            pe.wait_ge(S["wr_l"], 1)
            Q(0)
            V(0)

            def step(i, par):
                pe.wait_ge(S["ql"], DK * (i + 1))
                for n in range(NT):
                    if n >= 2:
                        pe.wait_ge(S["vl"], 2 * i + n - 1)
                    if isinstance(i, int) and i == 0 and n == 2:
                        pe.wait_ge(S["s_l"], 2)
                    scores(i, [n])
                if below(i, B - 1):
                    pe.wait_ge(S["e_done"], NT * i + 2)
                    T1(i + 1)
                if at_least(i, 1):
                    T2(i - 1, 1 - par)
                pe.wait_ge(S["e_done"], NT * i + 4)
                for m in range(NT):
                    if m >= 2 and below(i, B - 1):
                        pe.wait_ge(S["xl"], DK * i + DK + m - 1)
                    for n in range(NT):
                        mm = t_.transpose(bank[(2 + m) % NT][:, n * P:(n + 1) * P], prob[:, n, m * P:(m + 1) * P],
                                          ident[:, :])
                    mm.then_inc(S["pt"], 1)
                if below(i, B - 1):
                    if at_least(i, 2):
                        pe.wait_ge(S["rank_read"], i - 1)
                    Q(i + 1)
                if at_least(i, 1):
                    pe.wait_ge(S["ptL"], NT * i + 1)
                    logitsT(i - 1)
                pe.wait_ge(S["ptL"], NT * (i + 1))
                for n in range(NT):
                    if n == 2 and at_least(i, 1):
                        logits(i - 1)
                    cols = slice(n * P, (n + 1) * P)
                    mm = product(bank[6 + n // 2][:, n % 2 * D:(n % 2 + 1) * D],
                                 [(pT_hi[:, m, cols], pT_lo[:, m, cols], v_hi[:, m, :], v_lo[:, m, :])
                                  for m in range(NT)])
                    if n % 2:
                        mm.then_inc(S["o_done"], 1)
                if at_least(i, 1):
                    if below(i, B - 1):
                        pe.wait_ge(S["ql"], DK * (i + 2))
                    else:
                        pe.wait_ge(S["rank_read"], i - 1)
                    rank(i - 1)
                if below(i, B - 1):
                    if at_least(i, 1):
                        pe.wait_ge(S["logit_read"], i)
                    V(i + 1)

            batches(pe, step)
            T2(B - 1, 1)
            logitsT(B - 1)
            logits(B - 1)
            pe.wait_ge(S["rank_read"], B - 1)
            rank(B - 1)

            pe.wait_ge(S["map_vals"], 1)
            for c in range(2):
                last = t_.matmul(bank[6][0:1, c * TILES:(c + 1) * TILES], tile_vals[0:TILES, c:c + 1],
                                 ident[0:TILES, 0:TILES], start=True, stop=True)
            last.then_inc(S["map_done"], 1)
            pe.wait_ge(S["map_ready"], 1)
            pe.wait_ge(S["we_l"], E // 4)

            def c_t(q, par):
                pe.wait_ge(S[f"cx_in{par}"], 32 * (q - par) + 64)
                for h in range(2):
                    for s in range(2):
                        for k in range(DK):
                            at = (s * DK + k) * P
                            last = t_.transpose(bank[h][:, at:at + P], cx[par][:, 2 * h + s, k * P:(k + 1) * P],
                                                ident[:, :])
                    last.then_inc(S["ct"], 1)

            def c_gu(q):
                at = of_tiles(mybir.EngineType.PE, 1, q)
                for s in range(4):
                    if s % 2 == 0:
                        pe.wait_ge(S["cxl"], 2 * q + s // 2 + 1)
                    last = product(bank[2 + s // 2][:, s % 2 * 2 * F:(s % 2 + 1) * 2 * F],
                                   [(cxT_hi[:, s * DK + k, :], cxT_lo[:, s * DK + k, :],
                                     we_hi[:, bass.ds(at[s] + k * D, D)], we_lo[:, bass.ds(at[s] + k * D, D)])
                                    for k in range(DK)])
                    if s % 2:
                        last.then_inc(S["cgu"], 1)

            def c_ht(q):
                for s in range(4):
                    if s % 2 == 0:
                        pe.wait_ge(S["chm"], 2 * q + s // 2 + 1)
                    last = t_.transpose(bank[4][:, s * P:(s + 1) * P], ch[:, s, :], ident[:, :])
                last.then_inc(S["cth"], 1)

            def c_dn(q):
                at = of_tiles(mybir.EngineType.PE, 1, q)
                pe.wait_ge(S["chl"], q + 1)
                if not isinstance(q, int) or q >= 1:
                    pe.wait_ge(S["cyr"], 2 * q)
                for s in range(4):
                    last = product(bank[6 + s // 2][:, s % 2 * D:(s % 2 + 1) * D],
                                   [(chT_hi[:, s, :], chT_lo[:, s, :],
                                     we_hi[:, bass.ds(at[s] + 2 * D, D)], we_lo[:, bass.ds(at[s] + 2 * D, D)])])
                    if s % 2:
                        last.then_inc(S["cdn"], 1)

            def c_step(q, par, first=False, last=False):
                c_gu(q)
                if not last:
                    c_t(q + 1, 1 - par)
                if not first:
                    c_dn(q - 1)
                c_ht(q)

            c_t(0, 0)
            quads(pe, c_step)
            c_dn(QUADS - 1)

            def d_t(b, par):
                if isinstance(b, int) and b == 0:
                    pe.wait_ge(S["dx_in0"], 16)
                elif isinstance(b, int):
                    pe.wait_ge(S[f"dx_in{par}"], 16 * ((b - par) // 2) + 16)
                else:
                    pe.wait_ge(S[f"dx_in{par}"], (b - par) * 8 + 16)
                if not isinstance(b, int) or b >= 1:
                    pe.wait_ge(S["dxl"], DK * b)
                transposes(xn2[par], bank[0:2], "dt")

            def d_gu(b):
                pe.wait_ge(S["dxl"], DK * (b + 1))
                for f in range(FK):
                    if not isinstance(b, int) or b >= 1:
                        pe.wait_ge(S["dhm"], FK * b - FK + f + 1)
                    for c in range(2):
                        cols = slice(c * FS + f * P, c * FS + (f + 1) * P)
                        last = product(bank[2 + 2 * f + c][:, :],
                                       [(sgu_hi[:, k, cols], sgu_lo[:, k, cols], dxT_hi[:, k, :], dxT_lo[:, k, :])
                                        for k in range(DK)])
                    last.then_inc(S["dgu"], 1)

            def d_dn(b):
                pe.wait_ge(S["dhl"], FK * (b + 1))
                if not isinstance(b, int) or b >= 1:
                    pe.wait_ge(S["dsum"], b)
                for n in range(NT):
                    cols = slice(n * P, (n + 1) * P)
                    last = product(bank[6 + n // 2][:, n % 2 * D:(n % 2 + 1) * D],
                                   [(dh_hi[:, f, cols], dh_lo[:, f, cols], sd_hi[:, f, :], sd_lo[:, f, :])
                                    for f in range(FK)])
                    if n % 2:
                        last.then_inc(S["ddn"], 1)

            def d_step(b, par, first=False, last=False):
                if not last:
                    d_gu(b)
                    if not (isinstance(b, int) and b + 1 >= B):
                        d_t(b + 1, 1 - par)
                if not first:
                    d_dn(b - 1)

            d_t(0, 0)
            d_step(0, 0, first=True)
            pe.wait_ge(S["cyr"], 2 * QUADS)
            with pe.Fori(0, (B - 2) // 2) as u:
                d_step(2 * u + 1, 1)
                d_step(2 * u + 2, 0)
            d_step(B - 1, 1)
            d_step(B, 0, last=True)


_INS = ["L0_attn_x", "L0_attn_Wq", "L0_attn_Wk", "L0_attn_Wv", "L0_ffn_Wr", "L0_ffn_Wg", "L0_ffn_Wu", "L0_ffn_Wd",
        "L0_ffn_Sg", "L0_ffn_Su", "L0_ffn_Sd"]


def kernel(**inputs):
    import numpy as _np
    import concourse.bacc as _bacc
    from concourse import mybir as _mybir
    from concourse.bass_utils import run_bass_kernel_spmd as _run

    nc = _bacc.Bacc("TRN2", target_bir_lowering=False, num_devices=1)
    arrays, args = {}, []
    for name in _INS:
        a = _np.ascontiguousarray(inputs[name])
        arrays[f"in_{name}"] = a
        args.append(nc.dram_tensor(f"in_{name}", a.shape, _mybir.dt.from_np(a.dtype), kind="ExternalInput").ap())
    args.append(nc.dram_tensor("out_0", inputs[_INS[0]].shape, _mybir.dt.float32, kind="ExternalOutput").ap())
    block_kernel(nc, *args)
    r = _run(nc, [arrays], core_ids=[0])
    return r.results[0]["out_0"]
```

```python
from contextlib import ExitStack

import concourse.bass as bass
from concourse import mybir
from concourse.alu_op_type import AluOpType as ALU

F32, F32R, BF16 = mybir.dt.float32, mybir.dt.float32r, mybir.dt.bfloat16
I32, U32 = mybir.dt.int32, mybir.dt.uint32
ACT = mybir.ActivationFunctionType
AX = mybir.AxisListType.X
P = 128
EPS = 1e-5


def block_kernel(nc, x_in, wq_in, wk_in, wv_in, wr_in, wg_in, wu_in, wd_in, sg_in, su_in, sd_in, out):
    B, N, D = x_in.shape
    E, _, F = wg_in.shape
    FS = sg_in.shape[1]
    NT = N // P
    DK = D // P
    FK = FS // P
    K = 2
    T = B * N
    REGION = T + P
    TILES = T * K // P + E
    QUADS = TILES // 4
    EARLY = 3
    XW = D + 4
    PAD_ROW = E * REGION
    WROW = 3 * D
    LAST_PAIR = slice((E - 2) * WROW, E * WROW)
    assert (NT, DK, FK, F, E, B) == (4, 2, 2, P, 16, 8) and TILES % 8 == 0 and TILES <= P

    x_v = x_in.rearrange("b (p j) d -> b p (j d)", p=P)
    out_v = out.rearrange("b (p j) d -> b p (j d)", p=P)
    x1_dram = nc.dram_tensor("x1_dram", [B, P, NT * D], F32, kind="Internal").ap()
    xn2_dram = nc.dram_tensor("xn2_dram", [B, P, NT * D], F32, kind="Internal").ap()
    rows_by_expert = nc.dram_tensor("rows_by_expert", [E * REGION + P, XW], F32, kind="Internal").ap()
    y_by_token = nc.dram_tensor("y_by_token", [2 * T, D], F32, kind="Internal").ap()
    y_second = y_by_token[0:T, :].rearrange("(b p j) d -> b p (j d)", b=B, p=P)
    y_best = y_by_token[T:2 * T, :].rearrange("(b p j) d -> b p (j d)", b=B, p=P)
    we_hi_dram = nc.dram_tensor("we_hi_dram", [P, E * WROW], F32, kind="Internal").ap()

    with ExitStack() as ctx:
        def sb(name, shape, dt=F32):
            return ctx.enter_context(nc.sbuf_tensor(name, shape, dt))

        def sem(name):
            return ctx.enter_context(nc.semaphore(name))

        ATTN_BYTES = 100 * 1024 + 256
        LATE_BYTES = 48 * 1024
        attn_start = -(-nc.sbuf_base // 32) * 32
        attn_area = sb("attn_area", [P, ATTN_BYTES // 4])
        late_start = -(-nc.sbuf_base // 32) * 32
        late_area = sb("late_area", [P, LATE_BYTES // 4])
        places = {}

        def place(area, key, name, shape, dt=F32):
            size = 4
            for n in shape[1:]:
                size *= n
            at = places.get(key, 0)
            places[key] = at + size
            assert at + size <= (ATTN_BYTES if area is attn_area else LATE_BYTES), name
            start = attn_start if area is attn_area else late_start
            return nc.alloc_sbuf_tensor_at(name, shape, dt, offset=start + at)

        x = place(attn_area, "A", "x", [P, B, NT, D])
        xn = place(attn_area, "A", "xn", [P, NT, D])
        xT_hi = place(attn_area, "A", "xT_hi", [P, DK, N], F32R)
        xT_lo = place(attn_area, "A", "xT_lo", [P, DK, N], F32R)
        q_hi = place(attn_area, "A", "q_hi", [P, DK, N], F32R)
        v_hi = place(attn_area, "A", "v_hi", [P, NT, D], F32R)
        v_lo = place(attn_area, "A", "v_lo", [P, NT, D], F32R)
        x2T_hi = place(attn_area, "A", "x2T_hi", [P, DK, N], F32R)
        x2T_lo = place(attn_area, "A", "x2T_lo", [P, DK, N], F32R)
        places["late rows"] = places["A"]
        q_lo = place(attn_area, "A", "q_lo", [P, DK, N], F32R)
        wqk_hi = place(attn_area, "A", "wqk_hi", [P, DK, D], F32R)
        wqk_lo = place(attn_area, "A", "wqk_lo", [P, DK, D], F32R)
        places["A"] += 256
        places["setup"] = places["A"]
        prob = place(attn_area, "A", "prob", [P, NT, N])
        pT_hi = place(attn_area, "A", "pT_hi", [P, NT, N], F32R)
        pT_lo = place(attn_area, "A", "pT_lo", [P, NT, N], F32R)
        wvT_hi = place(attn_area, "A", "wvT_hi", [P, DK, D], F32R)
        wvT_lo = place(attn_area, "A", "wvT_lo", [P, DK, D], F32R)
        wq = place(attn_area, "setup", "wq", [P, DK, D])
        wk = place(attn_area, "setup", "wk", [P, DK, D])
        wv = place(attn_area, "setup", "wv", [P, DK, D])
        wq_hi = place(attn_area, "setup", "wq_hi", [P, DK, D], F32R)
        wq_lo = place(attn_area, "setup", "wq_lo", [P, DK, D], F32R)
        wk_hi = place(attn_area, "setup", "wk_hi", [P, DK, D], F32R)
        wk_lo = place(attn_area, "setup", "wk_lo", [P, DK, D], F32R)
        sgu = place(attn_area, "setup", "sgu", [P, DK, 2 * FS])
        sd = place(attn_area, "setup", "sd", [P, FK, D])
        we_hi = place(attn_area, "C", "we_hi", [P, E * WROW], F32R)
        we_raw = place(late_area, "raw", "we_raw", [P, E * WROW])
        we_lo = place(late_area, "lo", "we_lo", [P, E * WROW], F32R)
        def also(tensor_key, name, shape, dt=F32):
            return place(attn_area, tensor_key, name, shape, dt)

        cx = [also("late rows", f"cx{i}", [P, 4, XW]) for i in range(2)]
        places["dxT"] = places["late rows"]
        cxT_hi = also("late rows", "cxT_hi", [P, 4 * DK, P], F32R)
        cxT_lo = also("late rows", "cxT_lo", [P, 4 * DK, P], F32R)
        dxT = [[also("dxT", f"dxT_{half}", [P, DK, N], F32R) for half in ("hi", "lo")]]
        places["hidden"] = places["late rows"]
        csilu = also("hidden", "csilu", [P, 4, F])
        ch = also("hidden", "ch", [P, 4, F])
        chT_hi = also("hidden", "chT_hi", [P, 4, P], F32R)
        chT_lo = also("hidden", "chT_lo", [P, 4, P], F32R)
        dh = also("late rows", "dh", [P, FK, N])
        dh_hi = also("late rows", "dh_hi", [P, FK, N], F32R)
        dh_lo = also("late rows", "dh_lo", [P, FK, N], F32R)
        places["dxT"] = places["late rows"]
        places["D even"] = 32 * 1024
        dxT.append([also("dxT", f"dxT_{half}1", [P, DK, N], F32R) for half in ("hi", "lo")])
        dxT.append([place(attn_area, "D even", f"dxT_{half}_even", [P, DK, N], F32R) for half in ("hi", "lo")])

        places["dxT"] -= 2 * 4 * DK * N
        dh_2 = [also("dxT", f"dh_{half}2", [P, FK, N], F32R) for half in ("hi", "lo")]
        dh_even = [place(attn_area, "D even", f"dh_{half}_even", [P, FK, N], F32R) for half in ("hi", "lo")]

        def dh_of(b):
            return dh_2 if b == 2 else dh_even if b > EARLY and b % 2 == 0 else [dh_hi, dh_lo]

        def dxT_of(b):
            return dxT[0 if b < EARLY and b != 1 or b >= EARLY and b % 2 else 1 if b == 1 else 2]

        cy = [also("late rows", f"cy{i}", [P, 4, D]) for i in range(2)]
        y = [place(attn_area, "D", "y0", [P, B, NT, D]), place(late_area, "D late", "y1", [P, B, NT, D])]
        places["D"] = 48 * 1024
        res_parts = [place(attn_area, "D", "res_early", [P, B // 2, NT, D]),
                     place(late_area, "D late", "res_late", [P, B // 4, NT, D])]

        xn2 = [sb(f"xn2_{i}", [P, NT, XW]) for i in range(2)]
        part_start = -(-nc.sbuf_base // 32) * 32
        sb("part_area", [P, 2 * NT * D])
        we_hi_part = nc.alloc_sbuf_tensor_at("we_hi_part", [P, 2 * WROW], F32R, offset=part_start)
        res_parts.append(nc.alloc_sbuf_tensor_at("res_middle", [P, B // 4, NT, D], F32, offset=part_start))
        res = [res_parts[k][:, j, :, :] for k, n in ((0, B // 2), (2, B // 4), (1, B // 4)) for j in range(n)]
        sgu_hi, sgu_lo = sb("sgu_hi", [P, DK, 2 * FS], F32R), sb("sgu_lo", [P, DK, 2 * FS], F32R)
        sd_hi, sd_lo = sb("sd_hi", [P, FK, D], F32R), sb("sd_lo", [P, FK, D], F32R)
        wr = sb("wr", [P, DK, E])
        wr_hi, wr_lo = sb("wr_hi", [P, DK, E], F32R), sb("wr_lo", [P, DK, E], F32R)
        ident = sb("ident", [P, P])
        before = sb("before", [P, P], BF16)
        ones = sb("ones", [P, P], BF16)
        expert_no = sb("expert_no", [P, E])
        region_start = sb("region_start", [P, E])
        tile_no = sb("tile_no", [P, 1])
        ones_e = sb("ones_e", [P, E])
        minus_half = sb("minus_half", [P, NT])
        pads = sb("pads", [P, XW])
        token_no = sb("token_no", [P, NT])
        stat = [sb(f"stat{k}", [P, NT, 6]) for k in range(2)]
        mean_var = [sb(f"mean_var{k}", [P, NT, 2]) for k in range(2)]
        var_eps = [sb(f"var_eps{k}", [P, NT]) for k in range(2)]
        neg_mean = [sb(f"neg_mean{k}", [P, NT]) for k in range(2)]
        rstd = [sb(f"rstd{k}", [P, NT]) for k in range(2)]
        shift = [sb(f"shift{k}", [P, NT]) for k in range(2)]
        neg_max = sb("neg_max", [P, NT])
        prob_sum = sb("prob_sum", [P, NT])
        prob_sum16 = sb("prob_sum16", [P, NT])
        prob_scale = sb("prob_scale", [P, NT])
        logitT = sb("logitT", [E, N])
        logit = sb("logit", [P, NT, E])
        top = sb("top", [P, NT, 8])
        top_no = sb("top_no", [P, NT, 8], U32)
        onehot = sb("onehot", [P, K, NT * E], BF16)
        over = sb("over", [P, NT * E + NT])
        over_exp = sb("over_exp", [P, NT * E + NT])
        gate_sum = sb("gate_sum", [P, NT])
        next_row = sb("next_row", [P, E])
        row_of = sb("row_of", [P, NT * E])
        row_pick = sb("row_pick", [P, K, NT * E])
        slot = [sb(f"slot{i}", [P, K * NT], U32) for i in range(2)]
        count = sb("count", [P, E])
        count_i = sb("count_i", [P, E], I32)
        tiles_i = sb("tiles_i", [P, E], I32)
        tiles_of = sb("tiles_of", [P, E])
        tile_end = sb("tile_end", [P, E])
        passed = sb("passed", [P, E])
        passed_tiles = sb("passed_tiles", [P, E])
        tcol = sb("tcol", [P, 12])
        tile_vals = sb("tile_vals", [P, 2])
        expert_wide = sb("expert_wide", [P, P])
        tile_expert = sb("tile_expert", [P, TILES])
        tile_map = sb("tile_map", [1, 2, TILES], I32)
        is_best = [sb(f"is_best{i}", [P, 4]) for i in range(4)]
        gate_best = [sb(f"gate_best{i}", [P, 4]) for i in range(4)]
        gate = [sb(f"gate{i}", [P, 4]) for i in range(4)]
        dest = [sb(f"dest{i}", [P, 4], U32) for i in range(4)]
        row_end = sb("row_end", [1, E], I32)

        bank = [ctx.enter_context(nc.psum_tensor(f"bank{i}", [P, 512], F32)) for i in range(8)]

        T1_BANKS = [bank[5], bank[4]]

        names = """x0_in x1_in x_in w_in wv_in wr_in s_in raw_in
            consts pool_step
            wqk_raw_hi wqk_raw_lo wqk_done wvT_done wqk_h wqk_l wr_h wr_l s_h s_l
            bn0 bn1 mv0 mv1 pm0 pm1 ln0 ln1 xn_ready xn2_ready t1 t2 xh xl x2h x2l
            q_done qh ql v_done vh vl s_done mx e_done pt ptH ptL ps16 pscale o_done x1_done
            x1_out xn2_out0 xn2_out1
            logitsT_done logitT_read logits_done logit_read rt_top rt_pick rt_hot rt_over rt_exp rt_sum
            rank_done rank_read rt_row rt_rowpick rt_slot rt_best row_end
            token_cp token_next scattered0 scattered1 zero_fill
            map_step map_vals map_done map_ready
            we_h we_l we_hi_out we_hi_in
            cx_in0 cx_in1 ct cxh cxl cgu cs chm cth chh chl cdn cyr c_out0 c_out1 cbest cdest cgate
            dx_in0 dx_in1 dx_in2 dx_in3 dx_in4 dx_in5 dx_in6 dx_in7 dt dxh dxl dgu dsi dhm dhh dhl ddn dsum
            res_in0 res_in1 res_in2 res_in3 res_in4 res_in5 res_in6 res_in7
            y_in0 y_in1 y_in2 y_in3 y_in4 y_in5 y_in6 y_in7 y_added y_summed res_summed last_added out_done""".split()
        S = {n: sem(n) for n in names}

        block = ctx.enter_context(nc.Block())

        def batches(eng, step):
            for i in range(2):
                step(i, i)
            with eng.Fori(0, (B - 4) // 2) as u:
                for par in range(2):
                    step(2 * u + (2 + par), par)
            for i in range(B - 2, B):
                step(i, i % 2)

        def at_least(i, n):
            return not isinstance(i, int) or i >= n

        def below(i, n):
            return not isinstance(i, int) or i < n

        def quads(eng, step, body=2):
            for q in range(3):
                step(q, q % 4, first=(q == 0))
            with eng.Fori(0, (QUADS - 4) // body) as u:
                for q in range(3, 3 + body):
                    step(body * u + q, q % 4)
            step(QUADS - 1, (QUADS - 1) % 4, last=True)

        def down_banks(b):
            return bank[0:2] if b == B - 1 else bank[2:4] if b == EARLY - 1 else bank[6:8]

        def dxT_banks(b):
            return T1_BANKS if b == 0 else bank[0:2]

        def rows_of(b):
            return [cx[0], cx[1], cx[0], xn2[0], xn2[1], cx[0], cx[1], xn2[0]][b]

        def of_tiles(engine, row, q):
            return nc.values_load_multi_w_load_instructions(
                tile_map[0:1, row, bass.ds(4 * q, 4)], engines=[engine], min_val=0,
                max_val=PAD_ROW if row == 0 else (E - 1) * WROW,
                skip_runtime_bounds_check_because="made from counts that are bounded")[1]

        def pad_tails(eng, engine, e):
            ends = nc.values_load_multi_w_load_instructions(
                row_end[0:1, bass.ds(e, 4)], engines=[engine], min_val=0,
                max_val=PAD_ROW - P, skip_runtime_bounds_check_because="a count that is bounded")[1]
            for end in ends:
                eng.dma_start(rows_by_expert[bass.ds(end, P), :], pads[:, :]).then_inc(S["zero_fill"], 16)

        @block.sync
        def _(sp):
            sp.dma_start(x[:, 0, :, :].rearrange("p j d -> p (j d)"), x_v[0]).then_inc(S["x0_in"], 16)
            sp.dma_start(wq[:, :, :], wq_in.rearrange("(k p) e -> p k e", p=P)).then_inc(S["w_in"], 16)
            sp.dma_start(wk[:, :, :], wk_in.rearrange("(k p) e -> p k e", p=P)).then_inc(S["w_in"], 16)
            sp.dma_start(wv[:, :, :], wv_in.rearrange("(k p) e -> p k e", p=P)).then_inc(S["wv_in"], 16)
            sp.dma_start(wr[:, :, :], wr_in.rearrange("(k p) e -> p k e", p=P)).then_inc(S["wr_in"], 16)
            sp.dma_start(x[:, 1, :, :].rearrange("p j d -> p (j d)"), x_v[1]).then_inc(S["x1_in"], 16)
            sp.dma_start(sgu[:, :, 0:FS], sg_in.rearrange("(k p) f -> p k f", p=P)).then_inc(S["s_in"], 16)
            sp.dma_start(sgu[:, :, FS:2 * FS], su_in.rearrange("(k p) f -> p k f", p=P)).then_inc(S["s_in"], 16)
            sp.dma_start(sd[:, :, :], sd_in.rearrange("(k p) e -> p k e", p=P)).then_inc(S["s_in"], 16)
            for b in range(2, B):
                sp.dma_start(x[:, b, :, :].rearrange("p j d -> p (j d)"), x_v[b]).then_inc(S["x_in"], 16)
            for e in range(E):
                w = we_raw[:, e * WROW:e * WROW + 2 * D].rearrange("p (k c f) -> p k c f", k=DK, c=2)
                sp.dma_start(w[:, :, 0, :], wg_in[e].rearrange("(k p) f -> p k f", p=P)).then_inc(S["raw_in"], 16)
                sp.dma_start(w[:, :, 1, :], wu_in[e].rearrange("(k p) f -> p k f", p=P)).then_inc(S["raw_in"], 16)
                sp.dma_start(we_raw[:, e * WROW + 2 * D:(e + 1) * WROW], wd_in[e]).then_inc(S["raw_in"], 16)

            def load_rows(b):
                sp.dma_start(rows_of(b)[:, :, 0:D], xn2_dram[b].rearrange("p (j d) -> p j d", j=NT))\
                    .then_inc(S[f"dx_in{b}"], 16)

            def load_residual(b):
                sp.dma_start(res[b].rearrange("p j d -> p (j d)"), x1_dram[b]).then_inc(S[f"res_in{b}"], 16)

            def load_weights_hi(first, last):
                cols = slice(first, last)
                sp.dma_start(we_hi[:, cols].bitcast(F32), we_hi_dram[:, cols]).then_inc(S["we_hi_in"], 16)

            def store_batch(i, par):
                if not below(i, B - 2):
                    early_loads(i)
                if below(i, B - 1):
                    sp.wait_ge(S["we_h"], i + 1)
                    sp.nop(nofuse=True)
                    sp.dma_start(we_hi_dram[:, bass.ds(i * (2 * WROW), 2 * WROW)], we_hi_part[:, :].bitcast(F32))\
                        .then_inc(S["we_hi_out"], 16)
                sp.wait_ge(S["x1_done"], i + 1)
                sp.dma_start(x1_dram[bass.ds(i, 1), :, :].rearrange("b p n -> (b p) n"),
                             x[:, bass.ds(i, 1), :, :].rearrange("p b j d -> p (b j d)")).then_inc(S["x1_out"], 16)
                if below(i, B - 2):
                    store_rows(i, par)
                elif i == B - 1:
                    store_rows(B - 2, 0)
                    store_rows(B - 1, 1)

            def store_rows(i, par):
                sp.wait_ge(S["xn2_ready"], i + 1)
                sp.dma_start(xn2_dram[bass.ds(i, 1), :, :].rearrange("b p (j d) -> (b p) j d", j=NT),
                             xn2[par][:, :, 0:D]).then_inc(S[f"xn2_out{par}"], 16)

            def early_loads(i):
                if i == B - 2:
                    sp.wait_ge(S["we_hi_out"], 16 * i)
                    sp.wait_ge(S["x1_out"], 16 * i)
                    sp.wait_ge(S["xn2_ready"], i)
                    load_weights_hi(0, i * NT * D)
                else:
                    sp.wait_ge(S["xn2_out0"], 8 * B - 16)
                    sp.wait_ge(S["xn2_out1"], 8 * B - 16)
                    sp.wait_ge(S["s_done"], NT * B)
                    load_rows(0)
                    load_rows(1)
                    sp.wait_ge(S["we_hi_out"], 16 * i)
                    load_weights_hi(B * NT * D, (E - 2) * WROW)
                    sp.wait_ge(S["x1_out"], 16 * i)
                    sp.wait_ge(S["xn2_ready"], i)
                    load_weights_hi((B - 2) * NT * D, (B - 1) * NT * D)
                    last_loads()

            def last_loads():
                sp.wait_ge(S["o_done"], 2 * B)
                load_residual(0)
                load_residual(1)
                sp.wait_ge(S["dt"], DK)
                load_rows(2)

            batches(sp, store_batch)
            sp.wait_ge(S["x1_out"], 16 * B)
            load_weights_hi((B - 1) * NT * D, B * NT * D)
            sp.wait_ge(S["logitsT_done"], B)
            load_residual(2)

            sp.dma_start(rows_by_expert[PAD_ROW:PAD_ROW + P, :], pads[:, :]).then_inc(S["zero_fill"], 16)
            sp.wait_ge(S["row_end"], 1)
            with sp.Fori(0, E // 4 - 1) as u:
                pad_tails(sp, mybir.EngineType.SP, 4 * u)

            sp.wait_ge(S["map_ready"], 2)
            sp.wait_ge(S["zero_fill"], 16 * (E + 1))
            sp.wait_ge(S["scattered0"], 16 * K * NT * B // 2)
            sp.wait_ge(S["scattered1"], 16 * K * NT * B // 2)
            sp.wait_ge(S["dt"], DK * EARLY)

            def load_quad(q, par):
                if at_least(q, 2):
                    sp.wait_ge(S["cgate"], q - 1)
                rows = of_tiles(mybir.EngineType.SP, 0, q)
                for s in range(4):
                    sp.dma_start(cx[par][:, s, :], rows_by_expert[bass.ds(rows[s], P), :]).then_inc(S[f"cx_in{par}"], 16)

            load_quad(0, 0)
            load_quad(1, 1)
            between = [lambda: load_residual(EARLY), lambda: load_residual(EARLY + 1), lambda: load_residual(EARLY + 2),
                       lambda: load_rows(EARLY), lambda: load_rows(EARLY + 1)]
            for q in range(2, 7):
                load_quad(q, q % 2)
                between[q - 2]()
            with sp.Fori(0, (QUADS - 8) // 2) as u:
                load_quad(2 * u + 7, 1)
                load_quad(2 * u + 8, 0)
            load_quad(QUADS - 1, 1)

            sp.wait_ge(S["ct"], 2 * QUADS)
            sp.wait_ge(S["cgate"], QUADS)
            load_rows(EARLY + 2)
            load_rows(EARLY + 3)
            sp.wait_ge(S["cdn"], 2 * QUADS)
            for b in range(EARLY + 3, B):
                load_residual(b)

            def load_y(b):
                for k, rows in enumerate([y_second, y_best]):
                    sp.dma_start(y[k][:, b, :, :].rearrange("p j d -> p (j d)"), rows[b]).then_inc(S[f"y_in{b}"], 16)

            def store_final(b):
                sp.wait_ge(S["y_added"], b + 1)
                if b >= EARLY:
                    sp.wait_ge(S["dsum"], b + 1)
                sp.dma_start(out_v[b], res[b].rearrange("p j d -> p (j d)")).then_inc(S["out_done"], 16)

            def store_last_half(m):
                sp.wait_ge(S["last_added"], m + 1)
                cols = slice(m * NT * D // 2, (m + 1) * NT * D // 2)
                sp.dma_start(out_v[B - 1][:, cols], res[B - 1].rearrange("p j d -> p (j d)")[:, cols])\
                    .then_inc(S["out_done"], 16)

            sp.wait_ge(S["c_out0"], 32 * QUADS)
            sp.wait_ge(S["c_out1"], 32 * QUADS)
            for b in range(B):
                load_y(b)
                if b == 1:
                    sp.wait_ge(S["dt"], DK * (EARLY + 1))
                    load_rows(EARLY + 4)
            for b in range(B - 1):
                store_final(b)
            store_last_half(0)
            store_last_half(1)
            sp.wait_ge(S["out_done"], 16 * (B + 1))

        @block.gpsimd
        def _(pool):
            g = nc.gpsimd

            def hold(name, n):
                pool.wait_ge(S[name], n)
                pool.nop(nofuse=True)

            g.memset(ident[:, :], 0.0).then_inc(S["pool_step"], 1)
            g.memset(before[:, :], 1.0).then_inc(S["pool_step"], 1)
            g.memset(ones[:, :], 1.0).then_inc(S["pool_step"], 1)
            g.memset(ones_e[:, :], 1.0).then_inc(S["pool_step"], 1)
            g.memset(minus_half[:, :], -0.5).then_inc(S["pool_step"], 1)
            g.memset(pads[:, :], 0.0).then_inc(S["pool_step"], 1)
            g.iota(expert_no[:, :], [[1, E]], base=0, channel_multiplier=0,
                   allow_small_or_imprecise_dtypes=True).then_inc(S["pool_step"], 1)
            g.iota(region_start[:, :], [[REGION, E]], base=0, channel_multiplier=0,
                   allow_small_or_imprecise_dtypes=True).then_inc(S["pool_step"], 1)
            g.iota(next_row[:, :], [[REGION, E]], base=0, channel_multiplier=0,
                   allow_small_or_imprecise_dtypes=True).then_inc(S["pool_step"], 1)
            g.iota(tile_no[:, :], [[0, 1]], base=0, channel_multiplier=1,
                   allow_small_or_imprecise_dtypes=True).then_inc(S["pool_step"], 1)
            g.iota(token_no[:, :], [[1, NT]], base=0, channel_multiplier=NT,
                   allow_small_or_imprecise_dtypes=True).then_inc(S["pool_step"], 1)
            pool.wait_ge(S["pool_step"], 11)
            g.memset(pads[:, D:D + 1], float(2 * T)).then_inc(S["consts"], 1)
            g.memset(pads[:, D + 1:D + 2], -1.0).then_inc(S["consts"], 1)
            g.affine_select(out=ident[:, :], in_=ident[:, :], compare_op=ALU.not_equal, fill=1.0, base=0,
                            pattern=[[-1, P]], channel_multiplier=1).then_inc(S["consts"], 1)
            g.affine_select(out=before[:, :], in_=before[:, :], compare_op=ALU.is_gt, fill=0.0, base=0,
                            pattern=[[1, P]], channel_multiplier=-1).then_inc(S["consts"], 1)

            def scale_shift(i, k):
                mv, pm, ln = S[f"mv{k}"], f"pm{k}", S[f"ln{k}"]
                hold(f"mv{k}", i + 1)
                g.tensor_scalar(var_eps[k][:, :], mean_var[k][:, :, 1], EPS, None, ALU.add).then_inc(S[pm], 1)
                g.tensor_scalar(neg_mean[k][:, :], mean_var[k][:, :, 0], -1.0, None, ALU.mult).then_inc(S[pm], 1)
                if not isinstance(i, int) or i >= 1:
                    pool.wait_ge(S["xn_ready" if k == 0 else "xn2_ready"], i)
                hold(pm, 3 * i + 2)
                g.tensor_tensor(rstd[k][:, :], var_eps[k][:, :], minus_half[:, :], ALU.pow).then_inc(S[pm], 1)
                hold(pm, 3 * i + 3)
                g.tensor_tensor(shift[k][:, :], neg_mean[k][:, :], rstd[k][:, :], ALU.mult).then_inc(ln, 1)

            def scatter(i, par):
                hold("rt_slot", i + 1)
                if at_least(i, 1):
                    hold("token_next", i)
                g.tensor_copy(xn2[par][:, :, D], token_no[:, :]).then_inc(S["token_cp"], 1)
                hold("token_cp", i + 1)
                g.tensor_scalar(token_no[:, :], token_no[:, :], float(N), None, ALU.add).then_inc(S["token_next"], 1)
                hold("rt_best", 3 * i + 3)
                for c in range(K * NT):
                    g.indirect_dma_start(rows_by_expert, bass.IndirectOffsetOnAxis(ap=slot[par][:, c:c + 1], axis=0),
                                         xn2[par][:, c % NT, :], None).then_inc(S[f"scattered{par}"], 16)

            def step(i, par):
                if at_least(i, 2):
                    scatter(i - 2, par)
                if below(i, B - 2):
                    scale_shift(i + 2, 0)
                if isinstance(i, int) and i == 0:
                    scale_shift(0, 1)
                if isinstance(i, int) and i == 0:
                    pool.wait_ge(S["raw_in"], 16 * 3 * E)
                hold("we_h", i + 1)
                cols = bass.ds(i * (2 * WROW), 2 * WROW)
                part = we_hi_part[:, :] if below(i, B - 1) else we_hi[:, LAST_PAIR]
                g.tensor_tensor(we_lo[:, cols], we_raw[:, cols], part.bitcast(F32), ALU.subtract)\
                    .then_inc(S["we_l"], 1)
                if at_least(i, 1):
                    scale_shift(i, 1)

            scale_shift(0, 0)
            scale_shift(1, 0)
            batches(pool, step)
            scatter(B - 2, 0)
            scatter(B - 1, 1)

            def scatter_outputs(q, m, first=False, last=False):
                hold("cyr", 4 * q + 4)
                for s in range(4):
                    g.indirect_dma_start(y_by_token, bass.IndirectOffsetOnAxis(ap=dest[m][:, s:s + 1], axis=0),
                                         cy[m % 2][:, s, :], None, bounds_check=2 * T - 1,
                                         oob_is_err=False).then_inc(S[f"c_out{m % 2}"], 16)

            quads(pool, scatter_outputs, 4)
            for b in range(B):
                pool.wait_ge(S[f"y_in{b}"], 32)
                rows = [y[k][:, b, :, :].rearrange("p j d -> p (j d)") for k in range(K)]
                g.tensor_tensor(rows[0], rows[0], rows[1], ALU.add).then_inc(S["y_summed"], 1)
            pool.wait_ge(S["y_summed"], B)
            pool.wait_ge(S[f"res_in{B - 1}"], 16)
            last_res = res[B - 1].rearrange("p j d -> p (j d)")
            g.tensor_tensor(last_res, last_res, rows[0], ALU.add).then_inc(S["res_summed"], 1)

        @block.scalar
        def _(act):
            a = nc.scalar

            def hi(dst, src, done):
                return a.activation(dst, src, ACT.Copy).then_inc(S[done], 1)

            def normalise(i, k, par=0):
                act.wait_ge(S[f"ln{k}"], i + 1)
                if k == 0:
                    dst, done = xn, "xn_ready"
                    if not isinstance(i, int) or i >= 1:
                        act.wait_ge(S["t1"], DK * i)
                else:
                    dst, done = xn2[par], "xn2_ready"
                    if not isinstance(i, int) or i >= 2:
                        act.wait_ge(S[f"xn2_out{par}"], (i - par) * 8)
                        act.wait_ge(S[f"scattered{par}"], (i - par) * (8 * K * NT))
                for j in range(NT):
                    src = x[:, bass.ds(i, 1), j, :].rearrange("p b d -> p (b d)")
                    last = a.activation(dst[:, j, 0:D], src, ACT.Identity, bias=shift[k][:, j:j + 1],
                                        scale=rstd[k][:, j:j + 1])
                last.then_inc(S[done], 1)

            def xT(i):
                for k in range(DK):
                    act.wait_ge(S["t1"], DK * i + k + 1)
                    hi(xT_hi[:, k, :], T1_BANKS[k][:, :], "xh")

            def x2T(i):
                for k in range(DK):
                    act.wait_ge(S["t2"], DK * i + k + 1)
                    hi(x2T_hi[:, k, :], bank[6 + k][:, :], "x2h")

            def q(i):
                for m in range(DK):
                    act.wait_ge(S["q_done"], DK * i + m + 1)
                    hi(q_hi[:, m, :], T1_BANKS[m][:, :], "qh")

            def v(i):
                for m in range(2):
                    act.wait_ge(S["v_done"], 2 * i + m + 1)
                    hi(v_hi[:, 2 * m:2 * m + 2, :].rearrange("p j d -> p (j d)"), bank[2 + m][:, :], "vh")

            def exps(i, rows):
                for n in rows:
                    act.wait_ge(S["mx"], NT * i + n + 1)
                    a.activation(prob[:, n, :], bank[n][:, :], ACT.Exp, bias=neg_max[:, n:n + 1],
                                 accum_out=prob_sum[:, n:n + 1]).then_inc(S["e_done"], 1)

            def pT(i, blocks):
                for m in blocks:
                    act.wait_ge(S["pt"], NT * i + m + 1)
                    hi(pT_hi[:, m, :], bank[(2 + m) % NT][:, :], "ptH")

            def logitsT(i):
                act.wait_ge(S["logitsT_done"], i + 1)
                a.activation(logitT[:, :], bank[2][0:E, :], ACT.Copy).then_inc(S["logitT_read"], 1)

            def hi_of_experts(i):
                if isinstance(i, int) and i == 0:
                    act.wait_ge(S["raw_in"], 16 * 3 * E)
                if at_least(i, 1) and below(i, B - 1):
                    act.wait_ge(S["we_hi_out"], 16 * i)
                    act.wait_ge(S["we_l"], i)
                hi(we_hi_part[:, :] if below(i, B - 1) else we_hi[:, LAST_PAIR],
                   we_raw[:, bass.ds(i * (2 * WROW), 2 * WROW)], "we_h")

            def gate_exp(i):
                act.wait_ge(S["rt_over"], 2 * i + 2)
                a.activation(over_exp[:, :], over[:, :], ACT.Exp).then_inc(S["rt_exp"], 1)

            act.wait_ge(S["w_in"], 32)
            hi(wq_hi[:, :, :], wq[:, :, :], "wqk_raw_hi")
            hi(wk_hi[:, :, :], wk[:, :, :], "wqk_raw_hi")
            act.wait_ge(S["wr_in"], 16)
            hi(wr_hi[:, :, :], wr[:, :, :], "wr_h")
            act.wait_ge(S["wvT_done"], 1)
            hi(wvT_hi[:, :, :].rearrange("p k d -> p (k d)"), bank[5][:, :], "wqk_h")
            normalise(0, 0)
            act.wait_ge(S["wqk_done"], 1)
            hi(wqk_hi[:, :, :].rearrange("p k d -> p (k d)"), bank[0][:, :], "wqk_h")
            xT(0)
            act.wait_ge(S["s_in"], 48)
            hi(sgu_hi[:, :, :], sgu[:, :, :], "s_h")
            hi(sd_hi[:, :, :], sd[:, :, :], "s_h")
            q(0)
            normalise(1, 0)
            v(0)

            def step(i, par):
                exps(i, range(NT))
                if below(i, B - 1):
                    xT(i + 1)
                pT(i, range(0, 2))
                if at_least(i, 1):
                    x2T(i - 1)
                pT(i, range(2, 4))
                if below(i, B - 1):
                    q(i + 1)
                if at_least(i, 1):
                    logitsT(i - 1)
                if not below(i, B - 1):
                    d_x(0)
                if isinstance(i, int) and i == 0:
                    normalise(2, 0)
                    v(1)
                    hi_of_experts(0)
                    normalise(0, 1, 0)
                else:
                    hi_of_experts(i)
                    gate_exp(i - 1)
                    if below(i, B - 2):
                        normalise(i + 2, 0)
                    if below(i, B - 1):
                        v(i + 1)
                    else:
                        d_silu(0, 0)
                    normalise(i, 1, par)

            def d_x(b):
                for k in range(DK):
                    act.wait_ge(S["dt"], DK * b + k + 1)
                    hi(dxT_of(b)[0][:, k, :], dxT_banks(b)[k][:, :], "dxh")

            def d_silu(b, f):
                act.wait_ge(S["dgu"], FK * b + f + 1)
                if b >= 1:
                    act.wait_ge(S["dhl"], FK * b)
                a.activation(dh[:, f, :], bank[2 + 2 * f][:, :], ACT.Silu).then_inc(S["dsi"], 1)

            def d_h(b):
                if b >= 1:
                    act.wait_ge(S["ddn"], 2 if b == 1 else 2 * b - 2)
                for f in range(FK):
                    act.wait_ge(S["dhm"], FK * b + f + 1)
                    hi(dh_of(b)[0][:, f, :], dh[:, f, :], "dhh")

            batches(act, step)
            d_silu(0, 1)
            x2T(B - 1)
            d_h(0)
            d_x(1)
            logitsT(B - 1)
            gate_exp(B - 1)
            d_silu(1, 0)
            d_x(2)
            act.wait_ge(S["row_end"], 1)
            pad_tails(act, mybir.EngineType.Activation, E - 4)
            d_silu(1, 1)
            d_h(1)
            d_silu(2, 0)
            d_silu(2, 1)
            d_h(2)

            def c_x(q):
                for h in range(2):
                    act.wait_ge(S["ct"], 2 * q + h + 1)
                    hi(cxT_hi[:, 4 * h:4 * h + 4, :].rearrange("p k t -> p (k t)"), bank[h][:, :], "cxh")

            def c_silu(q):
                for h in range(2):
                    act.wait_ge(S["cgu"], 2 * q + h + 1)
                    a.activation(csilu[:, 2 * h:2 * h + 2, :],
                                 bank[2 + h][:, :].rearrange("p (s c f) -> p s c f", s=2, c=2)[:, :, 0, :],
                                 ACT.Silu).then_inc(S["cs"], 1)

            def c_h(q):
                act.wait_ge(S["cth"], q + 1)
                hi(chT_hi[:, :, :].rearrange("p s t -> p (s t)"), bank[4][:, :], "chh")

            def c_y(q, m):
                if at_least(q, 2):
                    act.wait_ge(S[f"c_out{m % 2}"], 32 * (q - m % 2))
                act.wait_ge(S["cgate"], q + 1)
                for s in range(4):
                    if s % 2 == 0:
                        act.wait_ge(S["cdn"], 2 * q + s // 2 + 1)
                    a.activation(cy[m % 2][:, s, :], bank[6 + s // 2][:, s % 2 * D:(s % 2 + 1) * D], ACT.Copy,
                                 scale=gate[m][:, s:s + 1]).then_inc(S["cyr"], 1)

            def c_step(q, m, first=False, last=False):
                c_silu(q)
                if not last:
                    c_x(q + 1)
                else:
                    d_x(EARLY)
                if not first:
                    c_y(q - 1, (m - 1) % 4)
                c_h(q)

            c_x(0)
            quads(act, c_step, 4)
            c_y(QUADS - 1, (QUADS - 1) % 4)
            act.wait_ge(S["cdn"], 2 * QUADS)
            d_x(EARLY + 1)
            for b in range(EARLY, B):
                d_silu(b, 0)
                d_silu(b, 1)
                if b + 2 < B:
                    d_x(b + 2)
                d_h(b)

        @block.vector
        def _(dve):
            v_ = nc.vector

            def hold(name, n):
                dve.wait_ge(S[name], n)
                dve.nop(nofuse=True)

            def lo(dst, src, hi_half, done):
                return v_.tensor_tensor(dst, src, hi_half.bitcast(F32), ALU.subtract).then_inc(S[done], 1)

            def stats(i, k):
                if k == 0:
                    if isinstance(i, int) and i < 2:
                        dve.wait_ge(S[f"x{i}_in"], 16)
                    else:
                        dve.wait_ge(S["x_in"], 16 * (B - 2))
                else:
                    dve.wait_ge(S["x1_done"], i + 1)
                if not isinstance(i, int) or i >= 1:
                    dve.wait_ge(S[f"pm{k}"], 3 * i)
                    hold(f"ln{k}", i)
                for j in range(NT):
                    last = v_.bn_stats(stat[k][:, j, :], x[:, bass.ds(i, 1), j, :].rearrange("p b d -> p (b d)"))
                last.then_inc(S[f"bn{k}"], 1)
                hold(f"bn{k}", i + 1)
                for j in range(NT):
                    last = v_.bn_aggr(mean_var[k][:, j, :], stat[k][:, j, :])
                last.then_inc(S[f"mv{k}"], 1)

            def maxes(i, rows):
                for n in rows:
                    dve.wait_ge(S["s_done"], NT * i + n + 1)
                    v_.tensor_reduce(neg_max[:, n:n + 1], bank[n][:, :], AX, ALU.max, negate=True)\
                        .then_inc(S["mx"], 1)

            def xT(i):
                for k in range(DK):
                    dve.wait_ge(S["xh"], DK * i + k + 1)
                    lo(xT_lo[:, k, :], T1_BANKS[k][:, :], xT_hi[:, k, :], "xl")

            def x2T(i):
                for k in range(DK):
                    dve.wait_ge(S["x2h"], DK * i + k + 1)
                    lo(x2T_lo[:, k, :], bank[6 + k][:, :], x2T_hi[:, k, :], "x2l")

            def q(i):
                for m in range(DK):
                    dve.wait_ge(S["qh"], DK * i + m + 1)
                    lo(q_lo[:, m, :], T1_BANKS[m][:, :], q_hi[:, m, :], "ql")

            def v(i):
                for m in range(2):
                    dve.wait_ge(S["vh"], 2 * i + m + 1)
                    lo(v_lo[:, 2 * m:2 * m + 2, :].rearrange("p j d -> p (j d)"), bank[2 + m][:, :],
                       v_hi[:, 2 * m:2 * m + 2, :].rearrange("p j d -> p (j d)"), "vl")

            def pT(i, blocks):
                for m in blocks:
                    dve.wait_ge(S["ptH"], NT * i + m + 1)
                    lo(pT_lo[:, m, :], bank[(2 + m) % NT][:, :], pT_hi[:, m, :], "ptL")

            def residual(i):
                dve.wait_ge(S["e_done"], NT * (i + 1))
                v_.tensor_scalar(prob_sum16[:, :], prob_sum[:, :], float(D) ** 0.5, None, ALU.mult)\
                    .then_inc(S["ps16"], 1)
                dve.wait_ge(S["ps16"], i + 1)
                v_.reciprocal(prob_scale[:, :], prob_sum16[:, :]).then_inc(S["pscale"], 1)
                dve.wait_ge(S["pscale"], i + 1)
                for n in range(NT):
                    if n % 2 == 0:
                        dve.wait_ge(S["o_done"], 2 * i + n // 2 + 1)
                    row = x[:, bass.ds(i, 1), n, :].rearrange("p b d -> p (b d)")
                    last = v_.scalar_tensor_tensor(row, bank[6 + n // 2][:, n % 2 * D:(n % 2 + 1) * D],
                                                   prob_scale[:, n:n + 1], row, ALU.mult, ALU.add)
                last.then_inc(S["x1_done"], 1)

            per_e = lambda t: t.rearrange("p (j e) -> p j e", e=E)
            wide = lambda col: col.unsqueeze(2).to_broadcast([P, NT, E])

            def route_a(i, at=3):
                dve.wait_ge(S["logits_done"], i + 1)
                v_.tensor_copy(logit[:, :, :].rearrange("p j e -> p (j e)"), bank[at][:, 0:NT * E])\
                    .then_inc(S["logit_read"], 1)
                hold("logit_read", i + 1)
                for j in range(NT):
                    last = v_.max(top[:, j, :], logit[:, j, :])
                last.then_inc(S["rt_top"], 1)
                hold("rt_top", i + 1)
                for j in range(NT):
                    last = v_.max_index(top_no[:, j, :], top[:, j, :], logit[:, j, :])
                last.then_inc(S["rt_pick"], 1)
                v_.tensor_tensor(per_e(over[:, 0:NT * E]), logit[:, :, :], wide(top[:, :, 0]), ALU.subtract)\
                    .then_inc(S["rt_over"], 1)
                v_.tensor_tensor(over[:, NT * E:NT * E + NT], top[:, :, 1], top[:, :, 0], ALU.subtract)\
                    .then_inc(S["rt_over"], 1)
                dve.wait_ge(S["rt_pick"], i + 1)
                v_.tensor_tensor(onehot[:, :, :].rearrange("p k (j e) -> p k j e", e=E),
                                 expert_no[:, :].unsqueeze(1).unsqueeze(1).to_broadcast([P, K, NT, E]),
                                 top_no[:, :, 0:K].rearrange("p j k -> p k j").unsqueeze(3).to_broadcast([P, K, NT, E]),
                                 ALU.is_equal).then_inc(S["rt_hot"], 1)

            def route_rows(i, at=5):
                dve.wait_ge(S["rank_done"], i + 1)
                v_.tensor_tensor(per_e(row_of[:, :]), per_e(bank[at][:, 0:NT * E]),
                                 next_row[:, :].unsqueeze(1).to_broadcast([P, NT, E]), ALU.add).then_inc(S["rt_row"], 1)
                dve.wait_ge(S["rt_row"], i + 1)
                v_.tensor_tensor(next_row[:, :], next_row[:, :], bank[at][:, NT * E:(NT + 1) * E], ALU.add)\
                    .then_inc(S["rank_read"], 1)

            def route_b(i, par):
                dve.wait_ge(S["rt_exp"], i + 1)
                v_.tensor_reduce(gate_sum[:, :], per_e(over_exp[:, 0:NT * E]), AX, ALU.add).then_inc(S["rt_sum"], 1)
                v_.tensor_tensor(row_pick[:, :, :], row_of[:, :].unsqueeze(1).to_broadcast([P, K, NT * E]),
                                 onehot[:, :, :], ALU.mult).then_inc(S["rt_rowpick"], 1)
                if at_least(i, 2):
                    dve.wait_ge(S[f"scattered{par}"], (i - par) * (8 * K * NT))
                dve.wait_ge(S["rt_sum"], i + 1)
                v_.reciprocal(xn2[par][:, :, D + 2], gate_sum[:, :]).then_inc(S["rt_best"], 1)
                v_.tensor_copy(xn2[par][:, :, D + 1], top_no[:, :, 0]).then_inc(S["rt_best"], 1)
                dve.wait_ge(S["rt_rowpick"], i + 1)
                with nc.allow_low_precision(reason="whole numbers below 2**24"):
                    v_.tensor_reduce(slot[par][:, :], row_pick[:, :, :].rearrange("p k (j e) -> p (k j) e", e=E), AX,
                                     ALU.add).then_inc(S["rt_slot"], 1)
                dve.wait_ge(S["rt_best"], 3 * i + 2)
                v_.tensor_tensor(xn2[par][:, :, D + 3], over_exp[:, NT * E:NT * E + NT], xn2[par][:, :, D + 2], ALU.mult)\
                    .then_inc(S["rt_best"], 1)

            stats(0, 0)
            dve.wait_ge(S["wqk_raw_hi"], 1)
            lo(wq_lo[:, :, :], wq[:, :, :], wq_hi[:, :, :], "wqk_raw_lo")
            dve.wait_ge(S["wqk_raw_hi"], 2)
            lo(wk_lo[:, :, :], wk[:, :, :], wk_hi[:, :, :], "wqk_raw_lo")
            dve.wait_ge(S["wr_h"], 1)
            lo(wr_lo[:, :, :], wr[:, :, :], wr_hi[:, :, :], "wr_l")
            dve.wait_ge(S["wqk_h"], 1)
            lo(wvT_lo[:, :, :].rearrange("p k d -> p (k d)"), bank[5][:, :],
               wvT_hi[:, :, :].rearrange("p k d -> p (k d)"), "wqk_l")
            stats(1, 0)
            dve.wait_ge(S["wqk_h"], 2)
            lo(wqk_lo[:, :, :].rearrange("p k d -> p (k d)"), bank[0][:, :],
               wqk_hi[:, :, :].rearrange("p k d -> p (k d)"), "wqk_l")
            xT(0)
            dve.wait_ge(S["s_h"], 1)
            lo(sgu_lo[:, :, :], sgu[:, :, :], sgu_hi[:, :, :], "s_l")
            dve.wait_ge(S["s_h"], 2)
            lo(sd_lo[:, :, :], sd[:, :, :], sd_hi[:, :, :], "s_l")
            q(0)
            v(0)

            def step(i, par):
                maxes(i, range(NT - 1))
                if at_least(i, 2):
                    route_rows(i - 2)
                maxes(i, [NT - 1])
                if at_least(i, 2):
                    route_b(i - 2, par)
                if below(i, B - 1):
                    xT(i + 1)
                pT(i, range(0, 2))
                if at_least(i, 1):
                    x2T(i - 1)
                pT(i, range(2, 4))
                if below(i, B - 1):
                    q(i + 1)
                else:
                    d_x(0)
                if below(i, B - 2):
                    stats(i + 2, 0)
                if at_least(i, 1):
                    route_a(i - 1)
                residual(i)
                stats(i, 1)
                if below(i, B - 1):
                    v(i + 1)

            def d_x(b):
                for k in range(DK):
                    dve.wait_ge(S["dxh"], DK * b + k + 1)
                    lo(dxT_of(b)[1][:, k, :], dxT_banks(b)[k][:, :], dxT_of(b)[0][:, k, :], "dxl")

            def d_mul(b, f):
                dve.wait_ge(S["dsi"], FK * b + f + 1)
                v_.tensor_tensor(dh[:, f, :], dh[:, f, :], bank[3 + 2 * f][:, :], ALU.mult).then_inc(S["dhm"], 1)

            def d_h(b):
                for f in range(FK):
                    dve.wait_ge(S["dhh"], FK * b + f + 1)
                    lo(dh_of(b)[1][:, f, :], dh[:, f, :], dh_of(b)[0][:, f, :], "dhl")

            def add_shared(b, to):
                for m in range(2):
                    dve.wait_ge(S["ddn"], 2 * b + m + 1)
                    rows = to[:, 2 * m:2 * m + 2, :].rearrange("p j d -> p (j d)")
                    last = v_.tensor_tensor(rows, down_banks(b)[m][:, :], rows, ALU.add)
                last.then_inc(S["dsum"], 1)

            def add_early(b):
                dve.wait_ge(S[f"res_in{b}"], 16)
                add_shared(b, res[b])

            batches(dve, step)
            d_mul(0, 0)
            route_rows(B - 2, at=1)
            route_b(B - 2, 0)
            d_mul(0, 1)
            x2T(B - 1)
            d_h(0)
            d_x(1)
            route_a(B - 1, at=1)
            route_rows(B - 1, at=0)
            route_b(B - 1, 1)
            dve.wait_ge(S["rank_read"], B)
            v_.tensor_copy(row_end[0:1, :], next_row[0:1, :]).then_inc(S["row_end"], 1)
            add_early(0)
            d_mul(1, 0)
            d_x(2)

            made = [0]

            def chained(instruction):
                instruction.then_inc(S["map_step"], 1)
                made[0] += 1
                dve.wait_ge(S["map_step"], made[0])

            chained(v_.tensor_tensor(count[:, :], next_row[:, :], region_start[:, :], ALU.subtract))
            chained(v_.tensor_scalar(count_i[:, :], count[:, :], float(P - 1), None, ALU.add))
            chained(v_.tensor_scalar(tiles_i[:, :], count_i[:, :], P.bit_length() - 1, None, ALU.logical_shift_right))
            chained(v_.tensor_copy(tiles_of[:, :], tiles_i[:, :]))
            chained(v_.tensor_tensor_scan(tile_end[:, :], ones_e[:, :], tiles_of[:, :], 0.0, ALU.mult, ALU.add))
            chained(v_.tensor_scalar(passed[:, :], tile_end[:, :], tile_no[:, 0:1], None, ALU.is_le))
            chained(v_.tensor_reduce(tcol[:, 0:1], passed[:, :], AX, ALU.add))
            chained(v_.tensor_tensor(passed_tiles[:, :], passed[:, :], tiles_of[:, :], ALU.mult))
            chained(v_.tensor_reduce(tcol[:, 1:2], passed_tiles[:, :], AX, ALU.add))
            chained(v_.tensor_tensor(tcol[:, 2:3], tile_no[:, :], tcol[:, 1:2], ALU.subtract))
            chained(v_.tensor_scalar(tcol[:, 3:4], tcol[:, 0:1], float(REGION), float(-PAD_ROW), ALU.mult, ALU.add))
            chained(v_.scalar_tensor_tensor(tcol[:, 6:7], tcol[:, 2:3], float(P), tcol[:, 3:4], ALU.mult, ALU.add))
            chained(v_.tensor_tensor(tcol[:, 4:5], tile_no[:, :], tile_end[:, E - 1:E], ALU.is_lt))
            v_.tensor_scalar(tile_vals[:, 0:1], tcol[:, 6:7], tcol[:, 4:5], float(PAD_ROW), ALU.mult, ALU.add)\
                .then_inc(S["map_vals"], 1)
            v_.tensor_scalar(tile_vals[:, 1:2], tcol[:, 0:1], float(E - 1), float(WROW), ALU.min, ALU.mult)\
                .then_inc(S["map_vals"], 1)
            v_.tensor_scalar(expert_wide[:, :], pads[:, 0:P], tcol[:, 0:1], None, ALU.add).then_inc(S["map_vals"], 1)
            d_mul(1, 1)
            dve.wait_ge(S["map_done"], 1)
            v_.tensor_copy(tile_map[:, :, :].rearrange("a c t -> a (c t)"), bank[0][0:1, 0:2 * TILES])\
                .then_inc(S["map_ready"], 1)
            v_.tensor_copy(tile_expert[:, :], bank[0][:, 2 * TILES:3 * TILES]).then_inc(S["map_ready"], 1)
            d_h(1)
            d_mul(2, 0)
            d_mul(2, 1)
            d_h(2)
            add_early(1)
            add_early(2)

            def c_x(q):
                for h in range(2):
                    dve.wait_ge(S["cxh"], 2 * q + h + 1)
                    lo(cxT_lo[:, 4 * h:4 * h + 4, :].rearrange("p k t -> p (k t)"), bank[h][:, :],
                       cxT_hi[:, 4 * h:4 * h + 4, :].rearrange("p k t -> p (k t)"), "cxl")

            def c_mul(q):
                for h in range(2):
                    dve.wait_ge(S["cs"], 2 * q + h + 1)
                    v_.tensor_tensor(ch[:, 2 * h:2 * h + 2, :], csilu[:, 2 * h:2 * h + 2, :],
                                     bank[2 + h][:, :].rearrange("p (s c f) -> p s c f", s=2, c=2)[:, :, 1, :],
                                     ALU.mult).then_inc(S["chm"], 1)

            def c_h(q):
                dve.wait_ge(S["chh"], q + 1)
                lo(chT_lo[:, :, :].rearrange("p s t -> p (s t)"), bank[4][:, :],
                   chT_hi[:, :, :].rearrange("p s t -> p (s t)"), "chl")

            def c_gate(q, m):
                rows = cx[m % 2]
                if isinstance(q, int) and q == 0:
                    dve.wait_ge(S["cx_in0"], 64)
                v_.tensor_tensor(is_best[m][:, :], rows[:, :, D + 1], tile_expert[:, bass.ds(4 * q, 4)], ALU.is_equal)\
                    .then_inc(S["cbest"], 1)
                dve.wait_ge(S["cbest"], q + 1)
                v_.scalar_tensor_tensor(dest[m][:, :], is_best[m][:, :], float(T), rows[:, :, D], ALU.mult, ALU.add)\
                    .then_inc(S["cdest"], 1)
                v_.tensor_tensor(gate_best[m][:, :], is_best[m][:, :], rows[:, :, D + 2], ALU.mult)\
                    .then_inc(S["cdest"], 1)
                dve.wait_ge(S["cdest"], 2 * q + 2)
                v_.tensor_tensor(gate[m][:, :], gate_best[m][:, :], rows[:, :, D + 3], ALU.max)\
                    .then_inc(S["cgate"], 1)

            def c_step(q, m, first=False, last=False):
                c_mul(q)
                if not last:
                    c_x(q + 1)
                else:
                    d_x(EARLY)
                c_h(q)
                if not last:
                    c_gate(q + 1, (m + 1) % 4)

            dve.wait_ge(S["map_ready"], 2)
            c_x(0)
            c_gate(0, 0)
            quads(dve, c_step, 4)

            def add_experts(b):
                dve.wait_ge(S["y_summed"], b + 1)
                dve.wait_ge(S[f"res_in{b}"], 16)
                dve.wait_ge(S["dsum"], b + 1)
                rows = res[b].rearrange("p j d -> p (j d)")
                v_.tensor_tensor(rows, rows, y[0][:, b, :, :].rearrange("p j d -> p (j d)"), ALU.add)\
                    .then_inc(S["y_added"], 1)

            d_x(EARLY + 1)
            between = {EARLY + 2: [0], EARLY + 3: [2], EARLY + 4: [5]}
            behind = {EARLY + 2: [1], EARLY + 3: [3, 4], EARLY + 4: [6]}
            for b in range(EARLY, B):
                d_mul(b, 0)
                for other in between.get(b, ()):
                    add_experts(other)
                d_mul(b, 1)
                if b + 2 < B:
                    d_x(b + 2)
                d_h(b)
                if b > EARLY:
                    dve.wait_ge(S[f"res_in{b - 1}"], 16)
                    add_shared(b - 1, res[b - 1])
                for other in behind.get(b, ()):
                    add_experts(other)
            dve.wait_ge(S["res_summed"], 1)
            for m in range(2):
                dve.wait_ge(S["ddn"], 2 * B - 1 + m)
                rows = res[B - 1][:, 2 * m:2 * m + 2, :].rearrange("p j d -> p (j d)")
                v_.tensor_tensor(rows, down_banks(B - 1)[m][:, :], rows, ALU.add).then_inc(S["last_added"], 1)

        @block.tensor
        def _(pe):
            t_ = nc.tensor

            def product(dst, terms, split="", first=0):
                n = 0
                for k, (a_hi, a_lo, b_hi, b_lo) in enumerate(terms):
                    if split:
                        pe.wait_ge(S[split], first + k + 1)
                    for l, r in ((a_hi, b_hi), (a_hi, b_lo), (a_lo, b_hi)):
                        last = t_.matmul(dst, l, r, start=(n == 0), stop=(n == 3 * len(terms) - 1))
                        n += 1
                return last

            def transposes(src, banks, done):
                for k in range(DK):
                    for j in range(NT):
                        last = t_.transpose(banks[k][:, j * P:(j + 1) * P], src[:, j, k * P:(k + 1) * P], ident[:, :])
                    last.then_inc(S[done], 1)

            def T1(i):
                pe.wait_ge(S["xn_ready"], i + 1)
                transposes(xn, T1_BANKS, "t1")

            def T2(i, par):
                pe.wait_ge(S["xn2_ready"], i + 1)
                transposes(xn2[par], bank[6:8], "t2")

            def Q(i):
                for m in range(DK):
                    cols = slice(m * P, (m + 1) * P)
                    product(T1_BANKS[m][:, :], [(wqk_hi[:, k, cols], wqk_lo[:, k, cols], xT_hi[:, k, :], xT_lo[:, k, :])
                                                for k in range(DK)], split="xl", first=DK * i)\
                        .then_inc(S["q_done"], 1)

            def V(i):
                for j in range(NT):
                    cols = slice(j * P, (j + 1) * P)
                    last = product(bank[2 + j // 2][:, j % 2 * D:(j % 2 + 1) * D],
                                   [(xT_hi[:, k, cols], xT_lo[:, k, cols], wvT_hi[:, k, :], wvT_lo[:, k, :])
                                    for k in range(DK)])
                    if j % 2:
                        last.then_inc(S["v_done"], 1)

            def scores(i, rows):
                for n in rows:
                    cols = slice(n * P, (n + 1) * P)
                    product(bank[n][:, :], [(q_hi[:, k, cols], q_lo[:, k, cols], xT_hi[:, k, :], xT_lo[:, k, :])
                                            for k in range(DK)]).then_inc(S["s_done"], 1)

            def logitsT(i):
                product(bank[2][0:E, :], [(wr_hi[:, k, :], wr_lo[:, k, :], x2T_hi[:, k, :], x2T_lo[:, k, :])
                                          for k in range(DK)], split="x2l", first=DK * i).then_inc(S["logitsT_done"], 1)

            def logits(i, at=3):
                pe.wait_ge(S["logitT_read"], i + 1)
                pe.nop(nofuse=True)
                for j in range(NT):
                    last = t_.transpose(bank[at][:, j * E:(j + 1) * E], logitT[:, j * P:(j + 1) * P], ident[0:E, 0:E])
                last.then_inc(S["logits_done"], 1)

            def rank(i, at=5):
                pe.wait_ge(S["rt_hot"], i + 1)
                for k in range(K):
                    t_.matmul(bank[at][:, 0:NT * E], before[:, :], onehot[:, k, :], start=(k == 0), stop=False,
                              skip_group_check=True)
                for k in range(K):
                    for j in range(NT):
                        last = t_.matmul(bank[at][:, (j + 1) * E:(NT + 1) * E].rearrange("p (c e) -> p c e", e=E),
                                         ones[:, :],
                                         onehot[:, k, j * E:(j + 1) * E].unsqueeze(1).to_broadcast([P, NT - j, E]),
                                         start=False, stop=(k == K - 1 and j == NT - 1), skip_group_check=True)
                last.then_inc(S["rank_done"], 1)

            pe.wait_ge(S["consts"], 4)
            pe.wait_ge(S["wv_in"], 16)
            for k in range(DK):
                for c in range(DK):
                    last = t_.transpose(bank[5][:, k * D + c * P:k * D + (c + 1) * P], wv[:, c, k * P:(k + 1) * P],
                                        ident[:, :])
            last.then_inc(S["wvT_done"], 1)
            pe.wait_ge(S["wqk_raw_lo"], 2)
            for m in range(DK):
                cols = slice(m * P, (m + 1) * P)
                last = product(bank[0][:, m * D:(m + 1) * D],
                               [(wq_hi[:, k, cols], wq_lo[:, k, cols], wk_hi[:, k, :], wk_lo[:, k, :])
                                for k in range(DK)])
            last.then_inc(S["wqk_done"], 1)
            pe.wait_ge(S["wqk_l"], 1)
            T1(0)
            pe.wait_ge(S["wqk_l"], 2)
            pe.wait_ge(S["wr_l"], 1)
            Q(0)
            V(0)

            def step(i, par):
                pe.wait_ge(S["ql"], DK * (i + 1))
                for n in range(NT):
                    if n >= 2:
                        pe.wait_ge(S["vl"], 2 * i + n - 1)
                    if isinstance(i, int) and i == 0 and n == 2:
                        pe.wait_ge(S["s_l"], 2)
                    scores(i, [n])
                if at_least(i, 1):
                    T2(i - 1, 1 - par)
                if below(i, B - 1):
                    if at_least(i, 2):
                        pe.wait_ge(S["rank_read"], i - 1)
                    T1(i + 1)
                def PT(m, rows):
                    for n in rows:
                        mm = t_.transpose(bank[(2 + m) % NT][:, n * P:(n + 1) * P], prob[:, n, m * P:(m + 1) * P],
                                          ident[:, :])
                    return mm

                pe.wait_ge(S["e_done"], NT * i + 3)
                PT(0, range(0, 3))
                PT(2, range(0, 3))
                pe.wait_ge(S["e_done"], NT * i + 4)
                PT(0, [3]).then_inc(S["pt"], 1)
                PT(1, range(NT)).then_inc(S["pt"], 1)
                PT(2, [3]).then_inc(S["pt"], 1)
                PT(3, range(NT)).then_inc(S["pt"], 1)
                if below(i, B - 1):
                    Q(i + 1)
                if not below(i, B - 1):
                    pe.wait_ge(S["rank_read"], i - 1)
                    d_t(0)
                if at_least(i, 1):
                    pe.wait_ge(S["ptL"], NT * i + 1)
                    logitsT(i - 1)
                for n in range(NT):
                    if n == 2 and at_least(i, 1):
                        logits(i - 1)
                    cols = slice(n * P, (n + 1) * P)
                    mm = product(bank[6 + n // 2][:, n % 2 * D:(n % 2 + 1) * D],
                                 [(pT_hi[:, m, cols], pT_lo[:, m, cols], v_hi[:, m, :], v_lo[:, m, :])
                                  for m in range(NT)], split="ptL" if n == 0 else "", first=NT * i)
                    if n % 2:
                        mm.then_inc(S["o_done"], 1)
                if not below(i, B - 1):
                    rank(i - 1, at=1)
                elif at_least(i, 1):
                    pe.wait_ge(S["ql"], DK * (i + 2))
                    rank(i - 1)
                if below(i, B - 1):
                    if at_least(i, 1):
                        pe.wait_ge(S["logit_read"], i)
                    V(i + 1)

            def d_t(b):
                pe.wait_ge(S[f"dx_in{b}"], 16)
                if b >= 2:
                    pe.wait_ge(S["dxl"], DK * b)
                transposes(rows_of(b), dxT_banks(b), "dt")

            def d_gu(b, f, parts=(0, 1)):
                if 0 in parts:
                    pe.wait_ge(S["dxl"], DK * (b + 1))
                    if b >= 1:
                        pe.wait_ge(S["dhm"], FK * b - FK + f + 1)
                for c in parts:
                    cols = slice(c * FS + f * P, c * FS + (f + 1) * P)
                    last = product(bank[2 + 2 * f + c][:, :],
                                   [(sgu_hi[:, k, cols], sgu_lo[:, k, cols], dxT_of(b)[0][:, k, :], dxT_of(b)[1][:, k, :])
                                    for k in range(DK)])
                if 1 in parts:
                    last.then_inc(S["dgu"], 1)

            def d_dn(b, between={}):
                pe.wait_ge(S["dhl"], FK * (b + 1))
                if b == B - 1:
                    pe.wait_ge(S["dxl"], DK * B)
                elif b == EARLY - 1:
                    pe.wait_ge(S["dhm"], FK * b + 1)
                elif b >= 1:
                    pe.wait_ge(S["dsum"], b)
                for n in range(NT):
                    if n in between:
                        between[n]()
                    cols = slice(n * P, (n + 1) * P)
                    last = product(down_banks(b)[n // 2][:, n % 2 * D:(n % 2 + 1) * D],
                                   [(dh_of(b)[0][:, f, cols], dh_of(b)[1][:, f, cols], sd_hi[:, f, :], sd_lo[:, f, :])
                                    for f in range(FK)])
                    if n % 2:
                        last.then_inc(S["ddn"], 1)

            batches(pe, step)

            def last_logits():
                pe.wait_ge(S["dxl"], 2 * DK)
                logits(B - 1, at=1)
                d_gu(1, 0, parts=[0])

            pe.wait_ge(S["logit_read"], B - 1)
            d_gu(0, 0)
            pe.wait_ge(S["rank_read"], B - 2)
            d_gu(0, 1)
            T2(B - 1, 1)
            pe.wait_ge(S["rank_read"], B - 1)
            d_t(1)
            pe.wait_ge(S["dhm"], 1)
            logitsT(B - 1)
            d_dn(0, between={2: last_logits, 3: lambda: rank(B - 1, at=0)})
            d_gu(1, 0, parts=[1])
            pe.wait_ge(S["logit_read"], B)
            pe.wait_ge(S["rank_read"], B)
            d_t(2)
            d_gu(1, 1)
            d_gu(2, 0)
            pe.wait_ge(S["map_vals"], 3)
            for c in range(2):
                t_.matmul(bank[0][0:1, c * TILES:(c + 1) * TILES], tile_vals[0:TILES, c:c + 1],
                          ident[0:TILES, 0:TILES], start=True, stop=True)
            t_.matmul(bank[0][:, 2 * TILES:3 * TILES], expert_wide[0:TILES, :], ident[0:TILES, 0:TILES],
                      start=True, stop=True).then_inc(S["map_done"], 1)
            d_gu(2, 1)
            d_dn(1)
            d_dn(2)
            pe.wait_ge(S["map_ready"], 2)
            pe.wait_ge(S["we_hi_in"], 64)
            pe.wait_ge(S["we_l"], B)

            def c_t(q, par):
                pe.wait_ge(S[f"cx_in{par}"], 32 * (q - par) + 64)
                for h in range(2):
                    for s in range(2):
                        for k in range(DK):
                            at = (s * DK + k) * P
                            last = t_.transpose(bank[h][:, at:at + P], cx[par][:, 2 * h + s, k * P:(k + 1) * P],
                                                ident[:, :])
                    last.then_inc(S["ct"], 1)

            def c_gu(q):
                at = of_tiles(mybir.EngineType.PE, 1, q)
                if isinstance(q, int) and q == 0:
                    pe.wait_ge(S["dsum"], EARLY)
                for s in range(4):
                    if s % 2 == 0:
                        pe.wait_ge(S["cxl"], 2 * q + s // 2 + 1)
                    last = product(bank[2 + s // 2][:, s % 2 * 2 * F:(s % 2 + 1) * 2 * F],
                                   [(cxT_hi[:, s * DK + k, :], cxT_lo[:, s * DK + k, :],
                                     we_hi[:, bass.ds(at[s] + k * D, D)], we_lo[:, bass.ds(at[s] + k * D, D)])
                                    for k in range(DK)])
                    if s % 2:
                        last.then_inc(S["cgu"], 1)

            def c_ht(q):
                for s in range(4):
                    if s % 2 == 0:
                        pe.wait_ge(S["chm"], 2 * q + s // 2 + 1)
                    last = t_.transpose(bank[4][:, s * P:(s + 1) * P], ch[:, s, :], ident[:, :])
                last.then_inc(S["cth"], 1)

            def c_dn(q):
                at = of_tiles(mybir.EngineType.PE, 1, q)
                pe.wait_ge(S["chl"], q + 1)
                if at_least(q, 1):
                    pe.wait_ge(S["cyr"], 4 * q)
                for s in range(4):
                    last = product(bank[6 + s // 2][:, s % 2 * D:(s % 2 + 1) * D],
                                   [(chT_hi[:, s, :], chT_lo[:, s, :],
                                     we_hi[:, bass.ds(at[s] + 2 * D, D)], we_lo[:, bass.ds(at[s] + 2 * D, D)])])
                    if s % 2:
                        last.then_inc(S["cdn"], 1)

            def c_step(q, m, first=False, last=False):
                c_gu(q)
                if not last:
                    c_t(q + 1, (m + 1) % 2)
                else:
                    d_t(EARLY)
                if not first:
                    c_dn(q - 1)
                c_ht(q)

            c_t(0, 0)
            quads(pe, c_step)
            d_t(EARLY + 1)
            d_gu(EARLY, 0, parts=[0])
            c_dn(QUADS - 1)

            for b in range(EARLY, B):
                d_gu(b, 0, parts=[1] if b == EARLY else [0, 1])
                d_gu(b, 1)
                if b + 2 < B:
                    d_t(b + 2)
                if b > EARLY:
                    d_dn(b - 1)
                else:
                    pe.wait_ge(S["cyr"], 4 * QUADS)
            d_dn(B - 1)


_INS = ["L0_attn_x", "L0_attn_Wq", "L0_attn_Wk", "L0_attn_Wv", "L0_ffn_Wr", "L0_ffn_Wg", "L0_ffn_Wu", "L0_ffn_Wd",
        "L0_ffn_Sg", "L0_ffn_Su", "L0_ffn_Sd"]


def kernel(**inputs):
    import numpy as _np
    import concourse.bacc as _bacc
    from concourse import mybir as _mybir
    from concourse.bass_utils import run_bass_kernel_spmd as _run

    nc = _bacc.Bacc("TRN2", target_bir_lowering=False, num_devices=1)
    arrays, args = {}, []
    for name in _INS:
        a = _np.ascontiguousarray(inputs[name])
        arrays[f"in_{name}"] = a
        args.append(nc.dram_tensor(f"in_{name}", a.shape, _mybir.dt.from_np(a.dtype), kind="ExternalInput").ap())
    args.append(nc.dram_tensor("out_0", inputs[_INS[0]].shape, _mybir.dt.float32, kind="ExternalOutput").ap())
    block_kernel(nc, *args)
    r = _run(nc, [arrays], core_ids=[0])
    return r.results[0]["out_0"]
```
